# Optimizing a Trainium2 kernel written in Bass

```python
import numpy as np
import jax
import jax.numpy as jnp

def _softmax(x, axis=-1):
    return jax.nn.softmax(x, axis=axis)

def _gelu(x):
    return jax.nn.gelu(x, approximate=True)

def _silu(x):
    return jax.nn.silu(x)

def _sigmoid(x):
    return jax.nn.sigmoid(x)

def _layernorm(x, axis=-1, eps=1e-05):
    m = jnp.mean(x, axis=axis, keepdims=True)
    v = jnp.var(x, axis=axis, keepdims=True)
    return (x - m) / jnp.sqrt(v + eps)

def _scatter_add(tgt, idx, src, axis=0):
    return tgt.at[idx].add(src)

def _segment_sum(src, seg, n):
    return jax.ops.segment_sum(src, seg, n)
kernel_name = 'mk_decoder_preln_d1_seqx_r8_5bf762'

def setup_inputs(seed: int=0):
    np.random.seed(seed)
    _w = jnp.asarray

    def _rec_inputs():
        import jax
        import jax.numpy as jnp
        _rk = jax.random.key(seed)
        x = -0.0002928 + 1 * jax.random.normal(jax.random.fold_in(_rk, 1), (32, 128, 128), jnp.float32)
        _lenS = 128 - jax.random.randint(jax.random.fold_in(_rk, 7), (32,), 0, max(1, 128 // 4) + 1, jnp.int32)
        _lenS2 = 128 - jax.random.randint(jax.random.fold_in(_rk, 8), (32,), 0, max(1, 128 // 4) + 1, jnp.int32)
        _ctx_1024P = jax.random.normal(jax.random.fold_in(_rk, 11), (32, 16, 128), jnp.float32)
        _ctx_1024c = jax.random.dirichlet(jax.random.fold_in(_rk, 511), 0.3 * jnp.ones((16,), jnp.float32), (32, 128))
        _ctx_1024t = jnp.einsum('bsk,bkd->bsd', _ctx_1024c, _ctx_1024P)
        _ctx_1024t = _ctx_1024t * jax.lax.rsqrt(jnp.mean(jnp.square(_ctx_1024t)) + 1e-12) * 0.953939
        ctx_1024 = -1.39393e-06 + 0.999914 * (_ctx_1024t + 0.3 * jax.random.normal(jax.random.fold_in(_rk, 611), (32, 128, 128), jnp.float32))
        fside_Bx16xSxS2_0 = 9.80324e-06 + 0.100009 * jax.random.normal(jax.random.fold_in(_rk, 12), (32, 16, 128, 128), jnp.float32)
        fside_SxS2_0 = -2.64403e-05 + 0.100002 * jax.random.normal(jax.random.fold_in(_rk, 14), (128, 128), jnp.float32)
        _validS = jnp.arange(128)[None, :] < _lenS[:, None]
        _validS2 = jnp.arange(128)[None, :] < _lenS2[:, None]
        _causal = jnp.tril(jnp.ones((128, 128), dtype=bool))
        mask_BxS2_bf0 = jnp.logical_not(jnp.ones((32, 128), dtype=bool))
        return (x, ctx_1024, fside_Bx16xSxS2_0, fside_SxS2_0, mask_BxS2_bf0)
    x, ctx_1024, fside_Bx16xSxS2_0, fside_SxS2_0, mask_BxS2_bf0 = _rec_inputs()

    def _L0_attn_setup():
        import jax, jax.numpy as jnp
        import numpy as np
        B, T, D = (4, 256, 128)
        H = 4
        K = D // H
        V = D // H
        M = 64
        GATE_LOGIT_NORMALIZER = 8.0
        NORM_EPS = 1e-05

        def _swish(x):
            return x * jax.nn.sigmoid(x)

        def _gsa_recurrence(q, k, v, s, g, scale):
            b, t, h, dk = q.shape
            dv = v.shape[-1]
            m = s.shape[-1]

            def step(carry, inp):
                hk, hv = carry
                q_t, k_t, v_t, s_t, g_t = inp
                ge = jnp.exp(g_t)
                hk = hk * ge[:, :, None, :] + k_t[..., :, None] * s_t[..., None, :]
                logits = jnp.einsum('bhk,bhkm->bhm', q_t * scale, hk)
                p = jax.nn.softmax(logits, axis=-1)
                hv = hv * ge[..., :, None] + s_t[..., :, None] * v_t[..., None, :]
                o_t = jnp.einsum('bhm,bhmv->bhv', p, hv)
                return ((hk, hv), o_t)
            init = (jnp.zeros((b, h, dk, m), q.dtype), jnp.zeros((b, h, m, dv), q.dtype))
            xs = tuple((jnp.moveaxis(a, 1, 0) for a in (q, k, v, s, g)))
            _, o = jax.lax.scan(step, init, xs)
            return jnp.moveaxis(o, 0, 1)
        key = jax.random.key(seed)
        ks = jax.random.split(key, 6)
        sc = lambda n: 1.0 / np.sqrt(n)
        return {'x': jax.random.normal(ks[0], (B, T, D), jnp.float32), 'Wq': jax.random.normal(ks[1], (D, H * K), jnp.float32) * sc(D), 'Wk': jax.random.normal(ks[2], (D, H * K), jnp.float32) * sc(D), 'Wv': jax.random.normal(ks[3], (D, H * V), jnp.float32) * sc(D), 'Wf': jax.random.normal(ks[4], (D, H * M), jnp.float32) * sc(D), 'g_norm_w': jnp.ones((V,), jnp.float32), 'Wo': jax.random.normal(ks[5], (H * V, D), jnp.float32) * sc(H * V)}
    _L0_attn_all = _L0_attn_setup()
    _L0_attn_in = {k: v for k, v in _L0_attn_all.items() if k in ('Wq', 'Wk', 'Wv', 'Wf', 'g_norm_w', 'Wo')}
    del _L0_attn_all

    def _L0_xattn_setup():
        import jax, jax.numpy as jnp
        import numpy as np
        E = 128
        H = 16
        D = E // H
        key = jax.random.key(seed)
        ks = jax.random.split(key, 12)
        B, T, S = (2, 256, 256)
        inp = {'query': jax.random.normal(ks[0], (B, T, E), jnp.float32), 'key': jax.random.normal(ks[1], (B, S, E), jnp.float32), 'value': jax.random.normal(ks[2], (B, S, E), jnp.float32), 'spatial_bias': jax.random.normal(ks[3], (B, H, T, S), jnp.float32) * 0.1, 'directional_bias': jax.random.normal(ks[4], (B, H, T, S), jnp.float32) * 0.1, 'key_padding_mask': jnp.zeros((B, S), dtype=bool), 'attn_mask': jax.random.normal(ks[5], (T, S), jnp.float32) * 0.1, 'Wq': jax.random.normal(ks[6], (E, E), jnp.float32) / np.sqrt(E), 'bq': jnp.zeros((E,), jnp.float32), 'Wk': jax.random.normal(ks[7], (E, E), jnp.float32) / np.sqrt(E), 'bk': jnp.zeros((E,), jnp.float32), 'Wv': jax.random.normal(ks[8], (E, E), jnp.float32) / np.sqrt(E), 'bv': jnp.zeros((E,), jnp.float32), 'Wo': jax.random.normal(ks[9], (E, E), jnp.float32) / np.sqrt(E), 'bo': jnp.zeros((E,), jnp.float32)}
        return inp
    _L0_xattn_all = _L0_xattn_setup()
    _L0_xattn_in = {k: v for k, v in _L0_xattn_all.items() if k in ('Wq', 'bq', 'Wk', 'bk', 'Wv', 'bv', 'Wo', 'bo')}
    del _L0_xattn_all

    def _L0_ffn_setup():
        import jax, jax.numpy as jnp
        import numpy as np
        B, S, D_MODEL, D_FF, E, R, TOP_K = (4, 256, 128, 512, 8, 16, 2)
        key = jax.random.key(seed)
        ks = jax.random.split(key, 9)
        sd = 1.0 / np.sqrt(D_MODEL)
        return {'hidden_states': jax.random.normal(ks[0], (B, S, D_MODEL), jnp.float32), 'wi': jax.random.normal(ks[1], (D_FF, D_MODEL), jnp.float32) * sd, 'bi': jax.random.normal(ks[2], (D_FF,), jnp.float32) * 0.01, 'wo': jax.random.normal(ks[3], (D_MODEL, D_FF), jnp.float32) * (1.0 / np.sqrt(D_FF)), 'bo': jax.random.normal(ks[4], (D_MODEL,), jnp.float32) * 0.01, 'lora_A': jax.random.normal(ks[5], (E, R, D_MODEL), jnp.float32) * sd, 'lora_B': jax.random.normal(ks[6], (E, D_FF, R), jnp.float32) * 0.02, 'gate_w': jax.random.normal(ks[7], (E, D_MODEL), jnp.float32) * sd, 'gate_b': jax.random.normal(ks[8], (E,), jnp.float32) * 0.01}
    _L0_ffn_all = _L0_ffn_setup()
    _L0_ffn_in = {k: v for k, v in _L0_ffn_all.items() if k in ('wi', 'bi', 'wo', 'bo', 'lora_A', 'lora_B', 'gate_w', 'gate_b')}
    del _L0_ffn_all
    return {'x': x, 'ctx_1024': ctx_1024, 'fside_Bx16xSxS2_0': fside_Bx16xSxS2_0, 'fside_SxS2_0': fside_SxS2_0, 'mask_BxS2_bf0': mask_BxS2_bf0, 'L0_attn_Wq': _L0_attn_in['Wq'], 'L0_attn_Wk': _L0_attn_in['Wk'], 'L0_attn_Wv': _L0_attn_in['Wv'], 'L0_attn_Wf': _L0_attn_in['Wf'], 'L0_attn_g_norm_w': _L0_attn_in['g_norm_w'], 'L0_attn_Wo': _L0_attn_in['Wo'], 'L0_xattn_Wq': _L0_xattn_in['Wq'], 'L0_xattn_bq': _L0_xattn_in['bq'], 'L0_xattn_Wk': _L0_xattn_in['Wk'], 'L0_xattn_bk': _L0_xattn_in['bk'], 'L0_xattn_Wv': _L0_xattn_in['Wv'], 'L0_xattn_bv': _L0_xattn_in['bv'], 'L0_xattn_Wo': _L0_xattn_in['Wo'], 'L0_xattn_bo': _L0_xattn_in['bo'], 'L0_ffn_wi': _L0_ffn_in['wi'], 'L0_ffn_bi': _L0_ffn_in['bi'], 'L0_ffn_wo': _L0_ffn_in['wo'], 'L0_ffn_bo': _L0_ffn_in['bo'], 'L0_ffn_lora_A': _L0_ffn_in['lora_A'], 'L0_ffn_lora_B': _L0_ffn_in['lora_B'], 'L0_ffn_gate_w': _L0_ffn_in['gate_w'], 'L0_ffn_gate_b': _L0_ffn_in['gate_b']}

def reference(x, ctx_1024, fside_Bx16xSxS2_0, fside_SxS2_0, mask_BxS2_bf0, L0_attn_Wq, L0_attn_Wk, L0_attn_Wv, L0_attn_Wf, L0_attn_g_norm_w, L0_attn_Wo, L0_xattn_Wq, L0_xattn_bq, L0_xattn_Wk, L0_xattn_bk, L0_xattn_Wv, L0_xattn_bv, L0_xattn_Wo, L0_xattn_bo, L0_ffn_wi, L0_ffn_bi, L0_ffn_wo, L0_ffn_bo, L0_ffn_lora_A, L0_ffn_lora_B, L0_ffn_gate_w, L0_ffn_gate_b):
    import jax
    import jax.numpy as jnp

    def _L0_attn_ref(x, Wq, Wk, Wv, Wf, g_norm_w, Wo):
        import jax, jax.numpy as jnp
        import numpy as np
        B, T, D = (4, 256, 128)
        H = 4
        K = D // H
        V = D // H
        M = 64
        GATE_LOGIT_NORMALIZER = 8.0
        NORM_EPS = 1e-05

        def _swish(x):
            return x * jax.nn.sigmoid(x)

        def _gsa_recurrence(q, k, v, s, g, scale):
            b, t, h, dk = q.shape
            dv = v.shape[-1]
            m = s.shape[-1]

            def step(carry, inp):
                hk, hv = carry
                q_t, k_t, v_t, s_t, g_t = inp
                ge = jnp.exp(g_t)
                hk = hk * ge[:, :, None, :] + k_t[..., :, None] * s_t[..., None, :]
                logits = jnp.einsum('bhk,bhkm->bhm', q_t * scale, hk)
                p = jax.nn.softmax(logits, axis=-1)
                hv = hv * ge[..., :, None] + s_t[..., :, None] * v_t[..., None, :]
                o_t = jnp.einsum('bhm,bhmv->bhv', p, hv)
                return ((hk, hv), o_t)
            init = (jnp.zeros((b, h, dk, m), q.dtype), jnp.zeros((b, h, m, dv), q.dtype))
            xs = tuple((jnp.moveaxis(a, 1, 0) for a in (q, k, v, s, g)))
            _, o = jax.lax.scan(step, init, xs)
            return jnp.moveaxis(o, 0, 1)
        b, t, d = x.shape
        q = _swish((x @ Wq).reshape(b, t, H, K))
        k = _swish((x @ Wk).reshape(b, t, H, K))
        v = (x @ Wv).reshape(b, t, H, V)
        f = jax.nn.log_sigmoid((x @ Wf).reshape(b, t, H, M)) / GATE_LOGIT_NORMALIZER
        s = 1.0 - jnp.exp(f)
        o = _gsa_recurrence(q, k, v, s, f, scale=K ** (-0.5))
        o = o * jax.lax.rsqrt(jnp.mean(o * o, axis=-1, keepdims=True) + NORM_EPS) * g_norm_w
        return o.reshape(b, t, H * V) @ Wo

    def _L0_xattn_ref(query, key, value, spatial_bias, directional_bias, key_padding_mask, attn_mask, Wq, bq, Wk, bk, Wv, bv, Wo, bo):
        import jax, jax.numpy as jnp
        import numpy as np
        E = 128
        H = 16
        D = E // H
        B, T, _ = query.shape
        S = key.shape[1]
        scale = D ** (-0.5)
        q = (query @ Wq.T + bq).reshape(B, T, H, D).transpose(0, 2, 1, 3)
        k = (key @ Wk.T + bk).reshape(B, S, H, D).transpose(0, 2, 1, 3)
        v = (value @ Wv.T + bv).reshape(B, S, H, D).transpose(0, 2, 1, 3)
        scores = jnp.einsum('bhtd,bhsd->bhts', q, k) * scale
        scores = scores + attn_mask[None, None, :, :]
        pad = key_padding_mask[:, None, None, :]
        scores = jnp.where(pad, -jnp.inf, scores)
        if T == S:
            scores = scores + spatial_bias + directional_bias
        probs = jax.nn.softmax(scores, axis=-1)
        out = jnp.einsum('bhts,bhsd->bhtd', probs, v)
        out = out.transpose(0, 2, 1, 3).reshape(B, T, E)
        return out @ Wo.T + bo

    def _L0_ffn_ref(hidden_states, wi, bi, wo, bo, lora_A, lora_B, gate_w, gate_b):
        import jax, jax.numpy as jnp
        import numpy as np
        B, S, D_MODEL, D_FF, E, R, TOP_K = (4, 256, 128, 512, 8, 16, 2)
        logits = jnp.einsum('bsd,ed->bse', hidden_states, gate_w) + gate_b
        scores = jax.nn.softmax(logits, axis=-1)
        top_v, top_i = jax.lax.top_k(scores, TOP_K)
        val_sum = top_v.sum(axis=-1)
        out = jnp.zeros_like(hidden_states)
        for e in range(E):
            count = (top_i == e).sum(axis=-1).astype(hidden_states.dtype)
            gate = count * val_sum
            inter = jnp.einsum('bsd,fd->bsf', hidden_states, wi) + bi + jnp.einsum('bsr,fr->bsf', jnp.einsum('bsd,rd->bsr', hidden_states, lora_A[e]), lora_B[e])
            h = jax.nn.relu(inter)
            expert_out = jnp.einsum('bsf,df->bsd', h, wo) + bo
            out = out + gate[..., None] * expert_out
        return out
    x = x + _L0_attn_ref(_layernorm(x, axis=-1), L0_attn_Wq, L0_attn_Wk, L0_attn_Wv, L0_attn_Wf, L0_attn_g_norm_w, L0_attn_Wo)
    x = x + _L0_xattn_ref(_layernorm(x, axis=-1), ctx_1024, ctx_1024, fside_Bx16xSxS2_0, fside_Bx16xSxS2_0, mask_BxS2_bf0, fside_SxS2_0, L0_xattn_Wq, L0_xattn_bq, L0_xattn_Wk, L0_xattn_bk, L0_xattn_Wv, L0_xattn_bv, L0_xattn_Wo, L0_xattn_bo)
    x = x + _L0_ffn_ref(_layernorm(x, axis=-1), L0_ffn_wi, L0_ffn_bi, L0_ffn_wo, L0_ffn_bo, L0_ffn_lora_A, L0_ffn_lora_B, L0_ffn_gate_w, L0_ffn_gate_b)
    return x

_drawn_inputs = setup_inputs


def setup_inputs(seed=0):
    import zlib

    import numpy as np

    out = dict(_drawn_inputs(seed))
    spreads = {'L0_attn_g_norm_w': (1.0, 0.2),
     'L0_xattn_bq': (0.0, 0.459),
     'L0_xattn_bk': (0.0, 2.0),
     'L0_xattn_bv': (0.0, 0.1),
     'L0_xattn_bo': (0.0, 0.1)}
    factors = {'fside_Bx16xSxS2_0': 3.675,
     'fside_SxS2_0': 7.206,
     'L0_attn_Wq': 7.119,
     'L0_attn_Wk': 6.586,
     'L0_ffn_bi': 8.0,
     'L0_ffn_bo': 8.0,
     'L0_ffn_gate_b': 22.782}
    for name, (base, spread) in spreads.items():
        noise = np.random.default_rng([zlib.crc32(name.encode()), seed]).standard_normal(out[name].shape)
        drawn = base * np.exp(spread * noise) if base else spread * noise
        out[name] = jnp.asarray(drawn.astype(out[name].dtype))
    for name, factor in factors.items():
        out[name] = (out[name] * factor).astype(out[name].dtype)
    return out
```

```python
import concourse.bass as bass
from concourse import mybir
from contextlib import ExitStack

B, T, D = 32, 128, 128
GH, GK, GM = 4, 32, 64
XH, XD = 16, 8
XG = 4
NI = XH // XG
F, E, R = 512, 8, 16
FC = F // 128
PAIRS = B // 2
GROUP = 4
GROUPS = B // GROUP
EPS = 1e-5
EXP_FLOOR = -87.33654
GATE_DIV = 8.0


def need(engine, semaphore, count):
    if isinstance(count, int) and count <= 0:
        return
    engine.wait_ge(semaphore, count)


def hold(engine, semaphore, count, passed):
    if isinstance(count, int) and count <= 0:
        return
    engine.wait_ge(semaphore, count)
    engine.sem_inc(passed, 1)


def decoder(nc, x, ctx_in, fside, amask, kmask, g_wq, g_wk, g_wv, g_wf, g_norm, g_wo,
            x_wq, x_bq, x_wk, x_bk, x_wv, x_bv, x_wo, x_bo,
            wi, bi, wo, bo, lora_a, lora_b, gate_w, gate_b, out, phases=3):
    fp32, u8 = mybir.dt.float32, mybir.dt.uint8
    ALU, ACT, AX = mybir.AluOpType, mybir.ActivationFunctionType, mybir.AxisListType

    stack = ExitStack()
    with stack:
        def sb(name, shape, dt=fp32):
            return stack.enter_context(nc.sbuf_tensor(name, shape, dt))

        def sem(name):
            return stack.enter_context(nc.semaphore(name))

        X = sb("X", [128, B, D])
        ident = sb("ident", [128, 128])
        ones = sb("ones", [128, 128])
        minus_half = sb("minus_half", [128, 16])
        eps_tile = sb("eps_tile", [128, 16])
        stats = sb("stats", [128, GROUP, 6])
        meanvar = sb("meanvar", [128, GROUP, 2])
        vareps = sb("vareps", [128, GROUP])
        rstd = sb("rstd", [128, GROUP])

        g_wqkf = sb("g_wqkf", [128, 512])
        g_wv_sb = sb("g_wv_sb", [128, 128])
        g_wo_raw = sb("g_wo_raw", [128, 128])
        g_wo_sb = sb("g_wo_sb", [128, 128])
        g_norm_col = sb("g_norm_col", [128, 1])
        mask_a = sb("mask_a", [128, 128])
        mask_b = sb("mask_b", [128, 128])
        tri_centred = sb("tri_centred", [128, 128])
        head_mask = sb("head_mask", [128, GH])
        x_w_raw = sb("x_w_raw", [128, 4, 128])
        x_wT = sb("x_wT", [128, 4, 128])
        bq_raw = sb("bq_raw", [128, 1])
        bq_col = sb("bq_col", [128, 1])
        bk_col = sb("bk_col", [128, 1])
        bv_col = sb("bv_col", [128, 1])
        bv_wide = sb("bv_wide", [128, 128])
        bo_row = sb("bo_row", [1, 128])
        x_bias = sb("x_bias", [128, 128])
        in_head = sb("in_head", [128, XH])
        k_mask = sb("k_mask", [128, XG])
        half_mask = sb("half_mask", [128, 128])
        amask_sb = sb("amask_sb", [128, 128])
        kmask_sb = sb("kmask_sb", [128, B * 128], u8)
        wi_raw = sb("wi_raw", [128, FC, 128])
        wo_raw = sb("wo_raw", [128, F])
        lb_raw = sb("lb_raw", [128, FC, E * R])
        la_raw = sb("la_raw", [128, 128])
        gw_raw = sb("gw_raw", [E, 128])
        wiT = sb("wiT", [128, F])
        woT = sb("woT", [128, FC, 128])
        lbT = sb("lbT", [128, F])
        laT = sb("laT", [128, 128])
        gwT = sb("gwT", [128, E])
        bi_col = sb("bi_col", [128, FC])
        neg_bi = sb("neg_bi", [128, FC])
        bi_wide = sb("bi_wide", [128, FC, 128])
        fbo_row = sb("fbo_row", [1, 128])
        twos = sb("twos", [1, 128])
        f_bias = sb("f_bias", [128, 128])
        gb_sb = sb("gb_sb", [128, E])
        before = sb("before", [128, E, E])

        SHARED = 20736
        shared = sb("shared", [128, SHARED])
        at = [0]

        def carve(shape):
            n = 1
            for k in shape[1:]:
                n *= k
            part = shared[:, at[0]:at[0] + n]
            at[0] += n
            assert at[0] <= SHARED
            names = "abcde"[:len(shape) - 1]
            if len(names) == 1:
                return part
            return part.rearrange(f"p ({' '.join(names)}) -> p {' '.join(names)}", **dict(zip(names, shape[1:])))

        banks = stack.enter_context(nc.psum_tensor("banks", [128, 8, 512], fp32))

        s_x = [sem(f"x_loaded{i}") for i in range(4)]
        s_gw = sem("slot_weights_loaded")
        s_xw = sem("cross_weights_loaded")
        s_fw = sem("expert_weights_loaded")
        s_km = sem("key_mask_loaded")
        s_const = sem("constants_made")
        s_passed = sem("waits_passed")
        s_cstep = sem("constant_step")
        s_wT = sem("weights_transposed")
        s_wcopy = sem("transposed_weights_copied")
        s_wide = sem("wide_biases_made")
        s_dconst = sem("vector_constants_made")

        x_d = x.rearrange("b t d -> t b d")
        out_d = out.rearrange("b t d -> t b d")
        XC = B // 4

        def bank(i):
            return banks[:, i, :]

        def setup_sync(sp):
            sp.dma_start(X[:, 0:XC, :], x_d[:, 0:XC, :]).then_inc(s_x[0], 16)
            for src, lo in ((g_wq, 0), (g_wk, 128), (g_wf, 256)):
                sp.dma_start(g_wqkf[:, lo:lo + src.shape[1]], src).then_inc(s_gw, 16)
            sp.dma_start(g_wv_sb[:], g_wv).then_inc(s_gw, 16)
            sp.dma_start(g_wo_raw[:], g_wo).then_inc(s_gw, 16)
            for h in range(GH):
                sp.dma_start(g_norm_col[GK * h:GK * h + GK, :], g_norm[:, None]).then_inc(s_gw, 16)
            for c in range(1, 4):
                sp.dma_start(X[:, c * XC:(c + 1) * XC, :], x_d[:, c * XC:(c + 1) * XC, :]).then_inc(s_x[c], 16)
            for i, w in enumerate((x_wq, x_wk, x_wv, x_wo)):
                sp.dma_start(x_w_raw[:, i, :], w).then_inc(s_xw, 16)
            for dst, src in ((bq_raw, x_bq), (bk_col, x_bk), (bv_col, x_bv)):
                sp.dma_start(dst[:], src[:, None]).then_inc(s_xw, 16)
            sp.dma_start(bo_row[:], x_bo[None, :]).then_inc(s_xw, 16)
            sp.dma_start(amask_sb[:], amask).then_inc(s_xw, 16)
            sp.dma_start(kmask_sb[:], kmask.rearrange("b s -> (b s)")[None, :].broadcast_to([128, B * 128])).then_inc(s_km, 16)
            sp.dma_start(wi_raw[:], wi.rearrange("(c p) d -> p c d", p=128)).then_inc(s_fw, 16)
            sp.dma_start(wo_raw[:], wo).then_inc(s_fw, 16)
            for c in range(FC):
                sp.dma_start(lb_raw[:, c, :].rearrange("p (e r) -> p e r", r=R),
                             lora_b[:, c * 128:(c + 1) * 128, :].rearrange("e p r -> p e r")).then_inc(s_fw, 16)
            sp.dma_start(la_raw[:], lora_a.rearrange("e r d -> (e r) d")).then_inc(s_fw, 16)
            sp.dma_start(gw_raw[:], gate_w).then_inc(s_fw, 16)
            for c in range(FC):
                sp.dma_start(bi_col[:, c:c + 1], bi[c * 128:(c + 1) * 128, None]).then_inc(s_fw, 16)
            sp.dma_start(fbo_row[:], bo[None, :]).then_inc(s_fw, 16)
            sp.dma_start(gb_sb[:], gate_b[None, :].broadcast_to([128, E])).then_inc(s_fw, 16)
        GW, XW, FW = 16 * 9, 16 * 9, 16 * (2 + FC + 2 + FC + 2)

        def setup_pool(pool):
            steps = [0]

            def step(ins):
                steps[0] += 1
                ins.then_inc(s_cstep, 1)
                pool.wait_ge(s_cstep, steps[0])

            for tile, value in ((ones, 1.0), (twos, 2.0), (minus_half, -0.5), (eps_tile, EPS), (head_mask, 1.0), (before, 1.0),
                                (in_head, 1.0), (mask_a, -float(GK) ** -0.5), (mask_b, -1.0),
                                (tri_centred, 1.0 / GATE_DIV), (ident, 0.0), (vp, 0.0)):
                step(nc.gpsimd.memset(tile[:], value))
            step(nc.gpsimd.affine_select(out=ident[:], in_=ident[:], compare_op=ALU.not_equal, fill=1.0, base=0,
                                         pattern=[[-1, 128]], channel_multiplier=1))
            for m in (mask_a, mask_b, tri_centred):
                step(nc.gpsimd.affine_select(out=m[:], in_=m[:], compare_op=ALU.is_ge, fill=0.0, base=0,
                                             pattern=[[1, 128]], channel_multiplier=-1))
            step(nc.gpsimd.tensor_scalar(tri_centred[0:T // 2, :], tri_centred[0:T // 2, :], -1.0 / GATE_DIV, None, ALU.add))
            step(nc.gpsimd.affine_select(out=before[:], in_=before[:], compare_op=ALU.is_gt, fill=0.0, base=0,
                                         pattern=[[1, E], [-1, E]], channel_multiplier=0))
            for m, heads, width in ((in_head, XH, XD), (head_mask, GH, GK)):
                step(nc.gpsimd.affine_select(out=m[:], in_=m[:], compare_op=ALU.is_ge, fill=0.0, base=0,
                                             pattern=[[-width, heads]], channel_multiplier=1))
                step(nc.gpsimd.affine_select(out=m[:], in_=m[:], compare_op=ALU.is_ge, fill=0.0, base=width - 1,
                                             pattern=[[width, heads]], channel_multiplier=-1))
            nc.gpsimd.memset(ppbd[:], 0.0).then_inc(s_const, 1)

        CONST = 1

        def setup_tensor(pe):
            pe.wait_ge(s_const, CONST)
            pe.wait_ge(s_xw, XW)
            for i in range(4):
                last = nc.tensor.transpose(bank(0)[:, 128 * i:128 * i + 128], x_w_raw[:, i, :], ident[:])
            last.then_inc(s_wT, 1)
            pe.wait_ge(s_fw, FW)
            for c in range(FC):
                last = nc.tensor.transpose(bank(1)[:, 128 * c:128 * c + 128], wi_raw[:, c, :], ident[:])
            last.then_inc(s_wT, 1)
            for c in range(FC):
                last = nc.tensor.transpose(bank(2)[:, 128 * c:128 * c + 128], wo_raw[:, 128 * c:128 * c + 128], ident[:])
            last.then_inc(s_wT, 1)
            for c in range(FC):
                last = nc.tensor.transpose(bank(3)[:, 128 * c:128 * c + 128], lb_raw[:, c, :], ident[:])
            last.then_inc(s_wT, 1)
            nc.tensor.transpose(bank(4)[:, 0:128], la_raw[:], ident[:])
            nc.tensor.transpose(bank(4)[:, 128:128 + E], gw_raw[:], ident[0:E, 0:E]).then_inc(s_wT, 1)
            pe.wait_ge(s_wcopy, 5)
            pe.wait_ge(s_dconst, 3)
            nc.tensor.matmul(bank(5)[:, 0:128], bv_wide[:], x_wT[:, 3, :], start=True, stop=False)
            nc.tensor.matmul(bank(5)[:, 0:128], ones[0:1, :], bo_row[:], start=False, stop=True).then_inc(s_wT, 1)
            for c in range(FC):
                nc.tensor.matmul(bank(6)[:, 0:128], bi_wide[:, c, :], woT[:, c, :], start=(c == 0), stop=False)
            nc.tensor.matmul(bank(6)[:, 0:128], twos[:], fbo_row[:], start=False, stop=True).then_inc(s_wT, 1)

        def setup_scalar(act):
            nc.scalar.preload_act_table_set("natural_log_exp_and_others")
            for n, (dst, src) in enumerate(((x_wT[:].rearrange("p i d -> p (i d)"), bank(0)), (wiT[:], bank(1)),
                                            (woT[:].rearrange("p i d -> p (i d)"), bank(2)), (lbT[:], bank(3)))):
                act.wait_ge(s_wT, n + 1)
                nc.scalar.copy(dst, src).then_inc(s_wcopy, 1)
            act.wait_ge(s_wT, 5)
            nc.scalar.copy(laT[:], bank(4)[:, 0:128])
            nc.scalar.copy(gwT[:], bank(4)[:, 128:128 + E]).then_inc(s_wcopy, 1)
            act.wait_ge(s_wT, 6)
            nc.scalar.copy(x_bias[:], bank(5)[:, 0:128]).then_inc(s_wcopy, 1)
            act.wait_ge(s_wT, 7)
            nc.scalar.copy(f_bias[:], bank(6)[:, 0:128]).then_inc(s_wcopy, 1)

        def setup_vector(dve):
            dve.wait_ge(s_const, CONST)
            dve.wait_ge(s_gw, GW)
            nc.vector.tensor_scalar(g_wo_sb[:], g_wo_raw[:], g_norm_col[:], float(GK) ** 0.5, ALU.mult,
                                    ALU.mult).then_inc(s_dconst, 1)
            dve.wait_ge(s_xw, XW)
            nc.vector.tensor_reduce(k_mask[:], in_head[:].rearrange("p (i j) -> p j i", j=XG), AX.X, ALU.add)
            nc.vector.tensor_scalar(half_mask[:], amask_sb[:], 0.5, None, ALU.mult)
            nc.vector.tensor_scalar(bq_col[:], bq_raw[:], 0.5 * float(XD) ** -0.5, None, ALU.mult)
            nc.vector.tensor_scalar(bv_wide[:], ones[:], bv_col[:], None, ALU.mult).then_inc(s_dconst, 1)
            dve.wait_ge(s_fw, FW)
            nc.vector.tensor_scalar(neg_bi[:], bi_col[:], -1.0, None, ALU.mult)
            for c in range(FC):
                last = nc.vector.tensor_scalar(bi_wide[:, c, :], ones[:], bi_col[:, c:c + 1], None, ALU.mult)
            last.then_inc(s_dconst, 1)

        xn = carve([128, 2, 128])
        xT = carve([128, 2, 2, 128])
        wk = carve([128, 2, 512])
        LS = carve([128, 2, 512])
        sg = carve([128, 2, 256])
        dec = carve([128, 2, 256])
        qk = carve([128, 2, 256])
        qkT = carve([128, 2, 2, 2, 128])
        qbd = carve([128, 2, 2, GH, 128])
        Ep = carve([128, 2, 2, 256])
        Em = carve([128, 2, 256])
        sp_ = carve([128, 2, 2, 256])
        spT = carve([128, 2, 2, 2, 128])
        vS = carve([128, 2, 2, 128])
        Am = carve([128, 2 * GH, 128])
        lg = carve([128, 2 * GH, GM])
        mx = carve([128, 2 * GH])
        rs = carve([128, 2, 2 * GH])
        pp = carve([128, 2, 256])
        ppbd = carve([128, 2, 2, 2, 2, 128])
        Bm = carve([128, 2 * GH, 128])
        sq = carve([128, 2 * GH, GK])
        ss = carve([128, 2 * GH])
        rt = carve([128, 2 * GH])
        rr = carve([128, 2 * GH])
        on = carve([128, 2 * GH, GK])
        onT = carve([128, 2, 128])

        G = {n: sem("g_" + n) for n in (
            "stats", "aggr", "vareps", "rstd", "xn", "xTp", "xT", "z", "abs", "exp1", "ln", "ls", "sig", "dec",
            "silu", "qkTp", "qkT", "qbd", "csum", "eplus", "eminus", "s", "sTp", "sT", "a", "am", "l", "vp", "v",
            "lgts", "mx", "shift", "p", "sum", "pp", "ppTp", "ppT", "b", "bm", "o", "sq", "ss", "rt", "rt2", "r",
            "on", "onTp", "onT", "y", "x1")}

        def bc(ap, n):
            return ap[:, None, :].broadcast_to([128, n, ap.shape[1]])

        def inner(ap, n):
            return ap[:, :, None].broadcast_to([128, ap.shape[1], n])

        def gsa_tensor(pe, t, par, gate, intra, mix):
            if mix:
                p, q = t - 2, par
                need(pe, G["ppT"], 2 * (p + 1))
                need(pe, G["onT"], p)
                need(pe, G["x1"], p)
                for b in range(2):
                    for c in range(2):
                        last = nc.tensor.matmul(bank(6 + b)[:, 256 * c:256 * c + 256], spT[:, q, b, c, :],
                                                ppbd[:, q, b, c, :, :].rearrange("p h t -> p (h t)"), start=True, stop=True)
                last.then_inc(G["b"], 1)
            if gate:
                p, q = t, par
                need(pe, G["xn"], p + 1)
                need(pe, G["sT"], p)
                for b in range(2):
                    last = nc.tensor.transpose(bank(2)[:, 128 * b:128 * b + 128], xn[:, b, :], ident[:])
                last.then_inc(G["xTp"], 1)
            if intra:
                p, q = t - 1, 1 - par
                need(pe, G["qbd"], p + 1)
                need(pe, G["ppT"], 2 * p)
                need(pe, G["lgts"], p)
                for b in range(2):
                    last = nc.tensor.matmul(bank(4 + b), qkT[:, q, 1, b, :], qbd[:, q, b, :, :].rearrange("p h t -> p (h t)"),
                                            start=True, stop=True)
                last.then_inc(G["a"], 1)
            if gate:
                p, q = t, par
                need(pe, G["xT"], p + 1)
                need(pe, G["silu"], p)
                for b in range(2):
                    last = nc.tensor.matmul(bank(b), xT[:, q, b, :], g_wqkf[:], start=True, stop=True)
                last.then_inc(G["z"], 1)
            if mix:
                p, q = t - 2, par
                need(pe, G["bm"], p + 1)
                for b in range(2):
                    for h in range(GH):
                        last = nc.tensor.matmul(bank(6)[:, 128 * b + GK * h:128 * b + GK * h + GK], Bm[:, GH * b + h, :],
                                                vS[:, q, b, GK * h:GK * h + GK], start=True, stop=True)
                last.then_inc(G["o"], 1)
            if intra:
                p, q = t - 1, 1 - par
                need(pe, G["am"], p + 1)
                for b in range(2):
                    for h in range(GH):
                        last = nc.tensor.matmul(bank(4)[:, 256 * b + GM * h:256 * b + GM * h + GM], Am[:, GH * b + h, :],
                                                sp_[:, q, b, GM * h:GM * h + GM], start=True, stop=True)
                last.then_inc(G["l"], 1)
                for b in range(2):
                    last = nc.tensor.matmul(bank(5)[:, 128 * b:128 * b + 128], xT[:, q, b, :], g_wv_sb[:], start=True, stop=True)
                last.then_inc(G["vp"], 1)
            if gate:
                p, q = t, par
                need(pe, G["ls"], p + 1)
                need(pe, G["eminus"], p)
                nc.tensor.matmul(bank(3), tri_centred[:], LS[:, :, 256:512], start=True, stop=True).then_inc(G["csum"], 1)
                need(pe, G["silu"], p + 1)
                for w in range(2):
                    for b in range(2):
                        i = 2 * w + b
                        last = nc.tensor.transpose(bank(2)[:, 128 * i:128 * i + 128], qk[:, b, 128 * w:128 * w + 128], ident[:])
                last.then_inc(G["qkTp"], 1)
            if mix:
                p = t - 2
                need(pe, G["on"], p + 1)
                for b in range(2):
                    last = nc.tensor.transpose(bank(7)[:, 128 * b:128 * b + 128],
                                               on[:, GH * b:GH * b + GH, :].rearrange("p h v -> p (h v)"), ident[:])
                last.then_inc(G["onTp"], 1)
            if intra:
                p = t - 1
                need(pe, G["v"], p + 1)
                need(pe, G["pp"], p + 1)
                for b in range(2):
                    for c in range(2):
                        i = 2 * b + c
                        last = nc.tensor.transpose(bank(5)[:, 128 * i:128 * i + 128], pp[:, b, 128 * c:128 * c + 128], ident[:])
                last.then_inc(G["ppTp"], 1)
            if mix:
                p = t - 2
                need(pe, G["onT"], p + 1)
                for b in range(2):
                    last = nc.tensor.matmul(bank(6)[:, 128 * b:128 * b + 128], onT[:, b, :], g_wo_sb[:], start=True, stop=True)
                last.then_inc(G["y"], 1)
            if gate:
                p, q = t, par
                need(pe, G["s"], p + 1)
                need(pe, G["qkT"], p + 1)
                for b in range(2):
                    for c in range(2):
                        i = 2 * b + c
                        last = nc.tensor.transpose(bank(2)[:, 128 * i:128 * i + 128], sp_[:, q, b, 128 * c:128 * c + 128], ident[:])
                last.then_inc(G["sTp"], 1)

        def gsa_scalar(act, t, par, gate, intra, mix):
            if gate:
                p, q = t, par
                need(act, G["xTp"], p + 1)
                nc.scalar.copy(xT[:, q, :, :], bank(2)[:, 0:256].rearrange("p (b t) -> p b t", b=2)).then_inc(G["xT"], 1)
            if mix:
                p = t - 2
                need(act, G["o"], p + 1)
                nc.scalar.activation(sq[:].rearrange("p h v -> p (h v)"), bank(6)[:, 0:256], ACT.Square).then_inc(G["sq"], 1)
            if gate:
                p = t
                need(act, G["z"], p + 1)
                need(act, G["ls"], p)
                nc.scalar.activation(wk[:], banks[:, 0:2, :], ACT.Abs).then_inc(G["abs"], 1)
                need(act, G["abs"], p + 1)
                nc.scalar.activation(wk[:], wk[:], ACT.Exp, scale=-1.0).then_inc(G["exp1"], 1)
                need(act, G["exp1"], p + 1)
                nc.scalar.activation(wk[:], wk[:], ACT.Ln, bias=1.0).then_inc(G["ln"], 1)
            if intra:
                p, q = t - 1, 1 - par
                need(act, G["vp"], p + 1)
                nc.scalar.copy(vS[:, q, :, :], bank(5)[:, 0:256].rearrange("p (b v) -> p b v", b=2)).then_inc(G["v"], 1)
                need(act, G["shift"], p + 1)
                nc.scalar.activation(lg[:], lg[:], ACT.Exp).then_inc(G["p"], 1)
            if gate:
                p, q = t, par
                need(act, G["ls"], p + 1)
                nc.scalar.activation(sg[:], LS[:, :, 0:256], ACT.Exp).then_inc(G["sig"], 1)
                need(act, G["s"], p)
                nc.scalar.activation(dec[:], LS[:, :, 256:512], ACT.Exp, scale=1.0 / GATE_DIV).then_inc(G["dec"], 1)
                need(act, G["csum"], p + 1)
                csum = bank(3).rearrange("p (b m) -> p b m", b=2)
                nc.scalar.activation(Em[:], csum, ACT.Exp, scale=-1.0)
                nc.scalar.activation(Ep[:, q, :, :], csum, ACT.Exp).then_inc(G["eminus"], 1)
                need(act, G["qkTp"], p + 1)
                nc.scalar.copy(qkT[:, q, :, :, :].rearrange("p w b t -> p (w b t)"), bank(2)).then_inc(G["qkT"], 1)
            if mix:
                p = t - 2
                need(act, G["onTp"], p + 1)
                nc.scalar.copy(onT[:].rearrange("p b t -> p (b t)"), bank(7)[:, 0:256]).then_inc(G["onT"], 1)
            if intra:
                p, q = t - 1, 1 - par
                need(act, s_const, CONST)
                need(act, G["ppTp"], p + 1)
                src = bank(5).rearrange("p (b c t) -> p b c t", b=2, c=2)
                for half in range(2):
                    rows = slice(64 * half, 64 * half + 64)
                    nc.scalar.copy(ppbd[rows, q, :, :, half, :], src[rows, :, :, :]).then_inc(G["ppT"], 1)
            if gate:
                p, q = t, par
                need(act, G["sTp"], p + 1)
                nc.scalar.copy(spT[:, q, :, :, :].rearrange("p b c t -> p (b c t)"), bank(2)).then_inc(G["sT"], 1)

        def gsa_stats(dve, p, q):
            need(dve, G["xn"], p)
            need(dve, G["aggr"], 2 * p)
            for b in range(2):
                nc.vector.bn_stats(stats[:, b, :], X[:, 2 * p + b, :]).then_inc(G["stats"], 1)
            need(dve, G["vareps"], p)
            hold(dve, G["stats"], 2 * p + 2, s_passed)
            for b in range(2):
                nc.vector.bn_aggr(meanvar[:, b, :], stats[:, b, :]).then_inc(G["aggr"], 1)

        def gsa_normalise(dve, p, q):
            need(dve, G["rstd"], p + 1)
            need(dve, G["xTp"], p)
            for b in range(2):
                last = nc.vector.tensor_scalar(xn[:, b, :], X[:, 2 * p + b, :], meanvar[:, b, 0:1], rstd[:, b:b + 1],
                                               ALU.subtract, ALU.mult)
            last.then_inc(G["xn"], 1)

        def gsa_vector(dve, t, par, gate, intra, mix, ahead):
            if mix:
                p = t - 2
                need(dve, G["b"], p + 1)
                need(dve, G["o"], p)
                nc.vector.tensor_tensor(Bm[:], banks[:, 6:8, :].rearrange("p a (h t) -> p (a h) t", t=128),
                                        bc(mask_b[:], 2 * GH), ALU.mult).then_inc(G["bm"], 1)
            if intra:
                p = t - 1
                need(dve, G["a"], p + 1)
                need(dve, G["l"], p)
                nc.vector.tensor_tensor(Am[:], banks[:, 4:6, :].rearrange("p a (h t) -> p (a h) t", t=128),
                                        bc(mask_a[:], 2 * GH), ALU.mult).then_inc(G["am"], 1)
            if ahead:
                gsa_stats(dve, t + 1, 1 - par)
            if mix:
                p, q = t - 2, par
                need(dve, G["r"], p)
                nc.vector.scalar_tensor_tensor(rt[:], rs[:, q, :], GK * EPS, rs[:, q, :], ALU.mult, ALU.mult).then_inc(G["rt"], 1)
                need(dve, G["sq"], p + 1)
                nc.vector.tensor_reduce(ss[:], sq[:], AX.X, ALU.add).then_inc(G["ss"], 1)
                need(dve, G["ss"], p + 1)
                need(dve, G["rt"], p + 1)
                nc.vector.tensor_tensor(rt[:], rt[:], ss[:], ALU.add).then_inc(G["rt2"], 1)
            if gate:
                p = t
                need(dve, G["ln"], p + 1)
                need(dve, G["csum"], p)
                need(dve, G["dec"], p)
                nc.vector.scalar_tensor_tensor(LS[:].rearrange("p b n -> p (b n)"),
                                               banks[:, 0:2, :].rearrange("p b n -> p (b n)"), 0.0,
                                               wk[:].rearrange("p b n -> p (b n)"), ALU.min, ALU.subtract).then_inc(G["ls"], 1)
            if intra:
                p, q = t - 1, 1 - par
                need(dve, G["l"], p + 1)
                need(dve, G["pp"], p)
                nc.vector.tensor_tensor(lg[:], bank(4).rearrange("p (h m) -> p h m", m=GM),
                                        Ep[:, q, :, :].rearrange("p b (h m) -> p (b h) m", m=GM), ALU.mult).then_inc(G["lgts"], 1)
                need(dve, G["lgts"], p + 1)
                nc.vector.tensor_reduce(mx[:], lg[:], AX.X, ALU.max).then_inc(G["mx"], 1)
                need(dve, G["mx"], p + 1)
                nc.vector.tensor_tensor(lg[:], lg[:], inner(mx[:], GM), ALU.subtract).then_inc(G["shift"], 1)
            if gate:
                p = t
                need(dve, G["sig"], p + 1)
                need(dve, G["qkTp"], p)
                nc.vector.tensor_tensor(qk[:], banks[:, 0:2, 0:256], sg[:], ALU.mult).then_inc(G["silu"], 1)
            if intra:
                p, q = t - 1, 1 - par
                need(dve, G["p"], p + 1)
                nc.vector.tensor_reduce(rs[:, q, :], lg[:], AX.X, ALU.add).then_inc(G["sum"], 1)
            if mix:
                p = t - 2
                need(dve, G["r"], p + 1)
                need(dve, G["onTp"], p)
                nc.vector.tensor_tensor(on[:], bank(6)[:, 0:256].rearrange("p (h v) -> p h v", v=GK), inner(rr[:], GK),
                                        ALU.mult).then_inc(G["on"], 1)
            if gate:
                p, q = t, par
                need(dve, G["eminus"], p + 1)
                need(dve, G["dec"], p + 1)
                nc.vector.scalar_tensor_tensor(sp_[:, q, :, :].rearrange("p b m -> p (b m)"),
                                               dec[:].rearrange("p b m -> p (b m)"), 1.0, Em[:].rearrange("p b m -> p (b m)"),
                                               ALU.subtract, ALU.mult).then_inc(G["s"], 1)
                need(dve, G["qkT"], p + 1)
                for b in range(2):
                    last = nc.vector.tensor_tensor(qbd[:, q, b, :, :], bc(qkT[:, q, 0, b, :], GH), inner(head_mask[:], 128), ALU.mult)
                last.then_inc(G["qbd"], 1)
            if ahead:
                gsa_normalise(dve, t + 1, 1 - par)
            if mix:
                p = t - 2
                need(dve, G["y"], p + 1)
                x1 = X[:, 2 * p:2 * p + 2, :] if isinstance(p, int) else X[:, bass.ds(2 * p, 2), :]
                nc.vector.tensor_tensor(x1, bank(6)[:, 0:256].rearrange("p (b d) -> p b d", b=2), x1, ALU.add).then_inc(G["x1"], 1)

        def gsa_rstd(pool, p):
            need(pool, G["aggr"], 2 * (p + 1))
            need(pool, G["rstd"], p)
            nc.gpsimd.tensor_tensor(vareps[:, 0:2], meanvar[:, 0:2, 1], eps_tile[:, 0:2], ALU.add).then_inc(G["vareps"], 1)
            need(pool, G["vareps"], p + 1)
            need(pool, G["xn"], p)
            nc.gpsimd.tensor_tensor(rstd[:, 0:2], vareps[:, 0:2], minus_half[:, 0:2], ALU.pow).then_inc(G["rstd"], 1)

        def gsa_pool(pool, t, par, gate, intra, mix, ahead):
            if ahead:
                gsa_rstd(pool, t + 1)
            if mix:
                p = t - 2
                need(pool, G["rt2"], p + 1)
                need(pool, G["on"], p)
                nc.gpsimd.tensor_tensor(rr[:], rt[:], minus_half[:, 0:2 * GH], ALU.pow).then_inc(G["r"], 1)
            if intra:
                p, q = t - 1, 1 - par
                need(pool, G["p"], p + 1)
                need(pool, G["ppTp"], p)
                nc.gpsimd.tensor_tensor(pp[:].rearrange("p b m -> p (b m)"), lg[:].rearrange("p h m -> p (h m)"),
                                        Ep[:, q, :, :].rearrange("p b m -> p (b m)"), ALU.mult).then_inc(G["pp"], 1)

        def gsa_ticks(engine, tick):
            tick(0, 0, True, False, False, True)
            tick(1, 1, True, True, False, True)
            tick(2, 0, True, True, True, True)
            tick(3, 1, True, True, True, True)
            with engine.Fori(4, PAIRS - 2, 2) as t:
                tick(t, 0, True, True, True, True)
                tick(t + 1, 1, True, True, True, True)
            tick(PAIRS - 2, 0, True, True, True, True)
            tick(PAIRS - 1, 1, True, True, True, False)
            tick(PAIRS, 0, False, True, True, False)
            tick(PAIRS + 1, 1, False, False, True, False)

        ctxb = sb("c_ctx", [128, 2, 128])
        fs = sb("c_fside", [128, 2, XH, 128])
        fm = sb("c_bias", [128, 2, XH, 128])
        cm = sb("c_cm", [128, 128])
        xn2 = sb("c_xn", [128, 128])
        xT2 = sb("c_xT", [128, 128])
        cT = sb("c_cT", [128, 2, 128])
        qx = sb("c_q", [128, 2, 128])
        kx = sb("c_k", [128, 128])
        kbd = sb("c_kbd", [128, 2, XG, 128])
        VPAD = XG * (32 + XD)
        vp = sb("c_vpad", [128, 2, NI * VPAD])
        P = sb("c_P", [128, 2, XH, 128])
        mn = sb("c_min", [128, 2, XH])
        rsx = sb("c_sum", [128, 2, XH])
        rc = sb("c_recip", [128, XH])
        rx = sb("c_recipx", [128, XH, XD])
        RT = sb("c_recipT", [128, 128])
        PTs = sb("c_PT", [128, NI, 512])
        oTs = sb("c_oT", [128, 128])

        C = {n: sem("c_" + n) for n in (
            "stats", "aggr", "vareps", "rstd", "xn", "xbias", "Tp", "T", "qkp", "q", "k", "kbd", "cm", "fm", "vpz",
            "sc", "tt", "ex", "rc", "rx", "Rp", "RT", "pt", "ptD", "ptA", "pv", "oT", "yv", "v", "x2")}
        s_ctx = [sem(f"c_ctx_loaded{i}") for i in range(2)]
        s_fs = [sem(f"c_fside_loaded{i}") for i in range(2)]

        def x_tensor(pe, m, q, norm, project, scores, attend, finish):
            n = 2 * m + q
            o = 1 - q
            for i in range(NI):
                if scores:
                    if i == 0:
                        need(pe, C["q"], n + 2)
                        need(pe, C["kbd"], n + 2)
                    need(pe, C["tt"], 4 * n + i + 1)
                    rows = slice(32 * i, 32 * i + 32)
                    nc.tensor.matmul(bank(i), qx[rows, o, :], kbd[rows, o, :, :].rearrange("p j s -> p (j s)"),
                                     start=True, stop=True).then_inc(C["sc"], 1)
                if i == 0 and project:
                    need(pe, C["xn"], n + 3)
                    need(pe, s_ctx[q], 16 * (m + 2))
                    need(pe, C["RT"], n)
                    need(pe, C["k"], n + 2)
                    nc.tensor.transpose(bank(7)[:, 0:128], xn2[:], ident[:])
                    nc.tensor.transpose(bank(7)[:, 128:256], ctxb[:, q, :], ident[:]).then_inc(C["Tp"], 1)
                if i == 1 and project:
                    need(pe, C["T"], n + 3)
                    nc.tensor.matmul(bank(7)[:, 0:128], x_wT[:, 0, :], xT2[:], start=True, stop=True)
                    nc.tensor.matmul(bank(7)[:, 128:256], x_wT[:, 1, :], cT[:, q, :], start=True, stop=True).then_inc(C["qkp"], 1)
                if i == 2 and (scores or finish):
                    if project:
                        need(pe, C["k"], n + 3)
                    elif not project:
                        need(pe, C["RT"], n)
                    if finish:
                        need(pe, C["oT"], n)
                        last = nc.tensor.matmul(bank(7)[:, 0:128], oTs[:], x_wT[:, 3, :], start=True, stop=True)
                    if scores:
                        last = nc.tensor.matmul(bank(7)[:, 128:256], cT[:, o, :], x_wT[:, 2, :], start=True, stop=True)
                    last.then_inc(C["yv"], 1)
                if i == 3 and attend:
                    need(pe, C["rx"], n + 1)
                    need(pe, C["x2"], n)
                    if scores:
                        need(pe, C["v"], n + 2)
                    nc.tensor.transpose(bank(7)[:, 0:128], rx[:].rearrange("p h d -> p (h d)"), ident[:]).then_inc(C["Rp"], 1)
                if attend:
                    need(pe, C["ex"], 4 * n + i + 1)
                    if i == 1:
                        need(pe, C["ptA"], n)
                    else:
                        need(pe, C["ptD"], 3 * n + max(0, i - 1))
                    for j in range(XG):
                        last = nc.tensor.transpose(bank(4 + i % 2)[:, 128 * j:128 * j + 128], P[:, q, XG * i + j, :], ident[:])
                    last.then_inc(C["pt"], 1)
                if (attend and i > 0) or (finish and i == 0):
                    r, rq = (i - 1, q) if i else (NI - 1, o)
                    if i == 0:
                        need(pe, C["ptA"], n)
                    else:
                        need(pe, C["ptD"], 3 * n + i)
                    if i == 1:
                        need(pe, C["oT"], n)
                        need(pe, C["v"], n + 1)
                    for j in range(XG):
                        last = nc.tensor.matmul(bank(6)[32 * r:32 * r + 32, 0:128],
                                                vp[:, rq, VPAD * r + 32 * j:VPAD * r + 32 * j + 32],
                                                PTs[:, r, 128 * j:128 * j + 128], start=(j == 0), stop=(j == XG - 1))
                    last.then_inc(C["pv"], 1)

        def x_exps(act, batch, q, i):
            need(act, C["tt"], 4 * batch + i + 1)
            for h in range(XG * i, XG * i + XG):
                last = nc.scalar.activation(P[:, q, h, :], P[:, q, h, :], ACT.Exp, bias=mn[:, q, h:h + 1], scale=-1.0,
                                            accum_out=rsx[:, q, h:h + 1])
            last.then_inc(C["ex"], 1)

        def x_scalar(act, m, q, norm, project, scores, attend, finish):
            n = 2 * m + q
            o = 1 - q
            if attend:
                x_exps(act, n, q, 3)
            if project:
                need(act, C["Tp"], n + 3)
                need(act, C["yv"], n + 1)
                nc.scalar.copy(xT2[:], bank(7)[:, 0:128])
                nc.scalar.copy(cT[:, q, :], bank(7)[:, 128:256]).then_inc(C["T"], 1)
            if scores:
                x_exps(act, n + 1, o, 0)
            if project:
                need(act, C["qkp"], n + 3)
                need(act, C["sc"], 4 * n + 4)
                nc.scalar.activation(qx[:, q, :], bank(7)[:, 0:128], ACT.Identity, bias=bq_col[:],
                                     scale=0.5 * float(XD) ** -0.5).then_inc(C["q"], 1)
                need(act, C["kbd"], n + 2)
                nc.scalar.activation(kx[:], bank(7)[:, 128:256], ACT.Identity, bias=bk_col[:]).then_inc(C["k"], 1)
            if scores:
                x_exps(act, n + 1, o, 1)
                x_exps(act, n + 1, o, 2)
            if attend:
                need(act, C["Rp"], n + 1)
                need(act, C["oT"], n)
                nc.scalar.copy(RT[:], bank(7)[:, 0:128]).then_inc(C["RT"], 1)
                need(act, C["pt"], 4 * n + 4)
                need(act, C["pv"], 4 * n)
                nc.scalar.copy(PTs[:, 3, :], bank(5)).then_inc(C["ptA"], 1)

        def x_score(dve, batch, q, i, psum):
            need(dve, C["fm"], batch + 1)
            need(dve, C["pt"], 4 * batch - 7 + i)
            hold(dve, C["sc"], 4 * batch + i + 1, s_passed)
            for j in range(XG):
                h = XG * i + j
                last = nc.vector.tensor_tensor_reduce(out=P[:, q, h, :], in0=psum[:, 128 * j:128 * j + 128], in1=fm[:, q, h, :],
                                                      scale=-2.0, scalar=3.0e38, op0=ALU.add, op1=ALU.min,
                                                      accum_out=mn[:, q, h:h + 1])
            last.then_inc(C["tt"], 1)

        def x_turned(dve, n, i):
            need(dve, C["pt"], 4 * n + i + 1)
            need(dve, C["pv"], 4 * n - 3 + i)
            nc.vector.tensor_copy(PTs[:, i, :], bank(4 + i % 2)).then_inc(C["ptD"], 1)

        def x_row(m, q, k):
            n = 2 * m + q + k
            return X[:, n, :] if isinstance(n, int) else X[:, bass.ds(n, 1), :].rearrange("p a d -> p (a d)")

        def x_vector(dve, m, q, norm, project, scores, attend, finish):
            n = 2 * m + q
            o = 1 - q
            if scores:
                x_score(dve, n + 1, o, 0, bank(0))
            if norm:
                need(dve, C["xn"], n + 3)
                need(dve, C["aggr"], n + 3)
                nc.vector.bn_stats(stats[:, 0, :], x_row(m, q, 3)).then_inc(C["stats"], 1)
            if project:
                need(dve, C["fm"], n + 2)
                km = kmask_sb[:, bass.ds((n + 2) * T, T)]
                nc.vector.scalar_tensor_tensor(cm[:], km, -3.0e38, half_mask[:], ALU.mult, ALU.add).then_inc(C["cm"], 1)
            if finish:
                need(dve, C["pv"], 4 * n)
                need(dve, C["RT"], n)
                need(dve, C["yv"], n + 1)
                nc.vector.tensor_tensor(oTs[:], bank(6)[:, 0:128], RT[:], ALU.mult).then_inc(C["oT"], 1)
            if norm:
                need(dve, C["vareps"], n + 3)
                hold(dve, C["stats"], n + 4, s_passed)
                nc.vector.bn_aggr(meanvar[:, 0, :], stats[:, 0, :]).then_inc(C["aggr"], 1)
            if attend:
                x_turned(dve, n, 0)
            if scores:
                x_score(dve, n + 1, o, 1, bank(1))
            if attend:
                need(dve, C["ex"], 4 * n + 4)
                nc.vector.reciprocal(rc[:], rsx[:, q, :]).then_inc(C["rc"], 1)
                x_turned(dve, n, 1)
                need(dve, C["rc"], n + 1)
                need(dve, C["Rp"], n)
                nc.vector.tensor_copy(rx[:], inner(rc[:], XD)).then_inc(C["rx"], 1)
            if scores:
                x_score(dve, n + 1, o, 2, bank(2))
            if finish:
                need(dve, C["yv"], n + 2)
                need(dve, C["xbias"], n)
                nc.vector.tensor_tensor(x_row(m, q, -1), bank(7)[:, 0:128], x_row(m, q, -1), ALU.add).then_inc(C["x2"], 1)
            if scores:
                need(dve, C["yv"], n + 2)
                need(dve, C["pv"], 4 * n)
                dst = vp[:, o, :].rearrange("p (i j w) -> p i j w", i=NI, j=XG)[:, :, :, 0:XD]
                nc.vector.tensor_copy(dst, bank(7)[:, 128:256].rearrange("p (i j d) -> p i j d", i=NI, j=XG)).then_inc(C["v"], 1)
            if attend:
                x_turned(dve, n, 2)
            if scores:
                x_score(dve, n + 1, o, 3, bank(3))
            if norm:
                need(dve, C["rstd"], n + 4)
                need(dve, C["Tp"], n + 3)
                nc.vector.tensor_scalar(xn2[:], x_row(m, q, 3), meanvar[:, 0, 0:1], rstd[:, 0:1],
                                        ALU.subtract, ALU.mult).then_inc(C["xn"], 1)

        def x_pool(pool, m, q, norm, project, scores, attend, finish):
            n = 2 * m + q
            o = 1 - q
            if project:
                need(pool, C["xn"], n + 3)
                nc.gpsimd.tensor_tensor(x_row(m, q, 2), x_row(m, q, 2), x_bias[:], ALU.add).then_inc(C["xbias"], 1)
            if norm:
                need(pool, C["aggr"], n + 4)
                need(pool, C["rstd"], n + 3)
                nc.gpsimd.tensor_tensor(vareps[:, 0:1], meanvar[:, 0, 1:2], eps_tile[:, 0:1], ALU.add).then_inc(C["vareps"], 1)
                need(pool, C["vareps"], n + 4)
                need(pool, C["xn"], n + 3)
                nc.gpsimd.tensor_tensor(rstd[:, 0:1], vareps[:, 0:1], minus_half[:, 0:1], ALU.pow).then_inc(C["rstd"], 1)
            if project:
                need(pool, C["cm"], n + 3)
                need(pool, s_fs[q], 32 * (m + 2))
                need(pool, C["tt"], 4 * n + 4)
                nc.gpsimd.tensor_tensor(fm[:, q, :, :], fs[:, q, :, :], bc(cm[:], XH), ALU.add).then_inc(C["fm"], 1)
                need(pool, C["k"], n + 3)
                need(pool, C["sc"], 4 * n + 4)
                nc.gpsimd.tensor_tensor(kbd[:, q, :, :], bc(kx[:], XG), inner(k_mask[:], 128), ALU.mult).then_inc(C["kbd"], 1)

        def x_flags(n):
            return tuple(0 <= n + k < B for k in (3, 2, 1, 0, -1))

        def x_steps(engine, step):
            for n in range(-3, 2):
                step(n // 2, n % 2, *x_flags(n))
            with engine.Fori(1, B // 2 - 2, 1) as m:
                step(m, 0, True, True, True, True, True)
                step(m, 1, True, True, True, True, True)
            for n in range(B - 4, B + 1):
                step(n // 2, n % 2, *x_flags(n))

        def x_loads(sp):
            def load(m, q):
                n = 2 * m + q
                need(sp, C["Tp"], n - 1)
                sp.dma_start(ctxb[:, q, :], ctx_in[bass.ds(n, 1)].rearrange("o s d -> (o s) d")).then_inc(s_ctx[q], 16)
                need(sp, C["fm"], n - 1)
                bias = fside[bass.ds(n, 1)].rearrange("o h t s -> (o t) h s")
                for half in range(2):
                    rows = slice(64 * half, 64 * half + 64)
                    sp.dma_start(fs[rows, q, :, :], bias[rows, :, :]).then_inc(s_fs[q], 16)
            load(0, 0)
            load(0, 1)
            with sp.Fori(1, B // 2, 1) as m:
                load(m, 0)
                load(m, 1)

        NT = GROUP * 128
        at[0] = 0
        xn3 = carve([128, GROUP, 128])
        xT3 = carve([128, 2, NT])
        uT = carve([128, NT])
        um = carve([128, 2, 2, NT])
        lgt = carve([128, GROUP, E])
        rmx = carve([128, GROUP])
        ex = carve([128, GROUP, E])
        beats = carve([128, GROUP, E, E])
        ties = carve([128, GROUP, E, E])
        rank = carve([128, GROUP * E])
        top = carve([128, GROUP * E])
        den = carve([128, GROUP])
        rden = carve([128, GROUP])
        num = carve([128, GROUP])
        vs = carve([128, 2, GROUP])
        hot = carve([128, 2, GROUP, E * R])
        r1 = carve([128, FC, NT])
        hT = carve([128, FC, NT])
        y3 = carve([128, 2, GROUP, 128])

        M = {n: sem("f_" + n) for n in (
            "stats", "aggr", "vareps", "rstd", "xn", "Tp", "xT", "lg", "up", "uT", "l0", "mx", "sh", "ex", "fl", "gt", "eq",
            "eq2", "sum", "rank", "top", "et", "num", "den", "rden", "vs", "hot1", "hot", "hp", "um", "i1", "r1", "i2", "h",
            "y", "out")}
        s_out = [sem(f"stored{i}") for i in range(2)]

        def f_tensor(pe, m, q, norm, route, expert):
            t = 2 * m + q
            def route_turn():
                need(pe, M["xn"], t + 1)
                need(pe, M["xT"], t)
                for b in range(GROUP):
                    last = nc.tensor.transpose(bank(0)[:, 128 * b:128 * b + 128], xn3[:, b, :], ident[:])
                last.then_inc(M["Tp"], 1)

            def route_logits():
                need(pe, M["xT"], t + 1)
                need(pe, M["l0"], t)
                for b in range(GROUP):
                    last = nc.tensor.matmul(bank(1)[:, E * b:E * b + E], xT3[:, q, 128 * b:128 * b + 128], gwT[:],
                                            start=True, stop=True)
                last.then_inc(M["lg"], 1)
                need(pe, M["uT"], t)
                nc.tensor.matmul(bank(2), laT[:], xT3[:, q, :], start=True, stop=True).then_inc(M["up"], 1)

            def route_hot():
                need(pe, M["hot"], t + 1)
                need(pe, M["um"], t)
                for w in range(2):
                    for b in range(GROUP):
                        last = nc.tensor.transpose(bank(3 + w)[:, 128 * b:128 * b + 128], hot[:, w, b, :], ident[:])
                last.then_inc(M["hp"], 1)

            p, o = t - 1, 1 - q

            def first(c):
                need(pe, M["h"], FC * p + c - 1)
                nc.tensor.matmul(bank(5 + c % 2), wiT[:, 128 * c:128 * c + 128], xT3[:, o, :], start=True, stop=False)
                nc.tensor.matmul(bank(5 + c % 2), lbT[:, 128 * c:128 * c + 128], um[:, o, 0, :], start=False,
                                 stop=True).then_inc(M["i1"], 1)

            def second(c):
                need(pe, M["r1"], FC * p + c + 1)
                nc.tensor.matmul(bank(5 + c % 2), lbT[:, 128 * c:128 * c + 128], um[:, o, 1, :], start=False, stop=True,
                                 skip_group_check=True).then_inc(M["i2"], 1)

            def down():
                need(pe, M["h"], FC * p + FC)
                need(pe, M["out"], p)
                for b in range(GROUP):
                    for c in range(FC):
                        nc.tensor.matmul(bank(7)[:, 128 * b:128 * b + 128], hT[:, c, 128 * b:128 * b + 128], woT[:, c, :],
                                         start=(c == 0), stop=False)
                    last = nc.tensor.matmul(bank(7)[:, 128 * b:128 * b + 128], ones[0:1, :], f_bias[0:1, :],
                                            start=False, stop=True)
                last.then_inc(M["y"], 1)

            if expert:
                need(pe, M["um"], p + 1)
            for stage in ((route, route_turn), (expert, lambda: first(0)), (route, route_logits), (expert, lambda: first(1)),
                          (expert, lambda: second(0)), (expert, lambda: first(2)), (expert, lambda: second(1)),
                          (expert, lambda: first(3)), (expert, lambda: second(2)), (expert, lambda: second(3)),
                          (route, route_hot), (expert, down)):
                if stage[0]:
                    stage[1]()

        def f_scalar(act, m, q, norm, route, expert):
            t = 2 * m + q
            p = t - 1

            def relu(c):
                need(act, M["i1"], FC * p + c + 1)
                need(act, M["h"], FC * (p - 1) + c + 1)
                nc.scalar.activation(r1[:, c, :], bank(5 + c % 2), ACT.Relu, bias=bi_col[:, c:c + 1]).then_inc(M["r1"], 1)

            if route:
                need(act, M["Tp"], t + 1)
                need(act, M["i2"], FC * (t - 1))
                nc.scalar.copy(xT3[:, q, :], bank(0)).then_inc(M["xT"], 1)
            if expert:
                relu(0)
            if route:
                need(act, M["up"], t + 1)
                need(act, M["um"], t)
                nc.scalar.copy(uT[:], bank(2)).then_inc(M["uT"], 1)
            if expert:
                relu(1)
            if route:
                need(act, M["sh"], t + 1)
                need(act, M["den"], t)
                nc.scalar.activation(ex[:], lgt[:], ACT.Exp).then_inc(M["ex"], 1)
            if expert:
                relu(2)
                relu(3)

        def f_vector(dve, m, q, norm, route, expert):
            t = 2 * m + q
            p = t - 1

            def x3(k):
                g = t + k
                return X[:, GROUP * g:GROUP * g + GROUP, :] if isinstance(g, int) else X[:, bass.ds(GROUP * g, GROUP), :]

            def hidden(c):
                need(dve, M["i2"], FC * p + c + 1)
                need(dve, M["y"], p)
                nc.vector.scalar_tensor_tensor(hT[:, c, :], bank(5 + c % 2), neg_bi[:, c:c + 1], r1[:, c, :],
                                               ALU.max, ALU.add).then_inc(M["h"], 1)

            def merge(ap):
                return ap.rearrange("p b e -> p (b e)")

            def step(ins, name):
                ins.then_inc(M[name], 1)
                need(dve, M[name], t + 1)

            if norm:
                need(dve, M["aggr"], GROUP * (t + 1))
                src = x3(1)
                for b in range(GROUP):
                    nc.vector.bn_stats(stats[:, b, :], src[:, b, :]).then_inc(M["stats"], 1)
                need(dve, M["vareps"], t + 1)
                hold(dve, M["stats"], GROUP * (t + 2), s_passed)
                for b in range(GROUP):
                    nc.vector.bn_aggr(meanvar[:, b, :], stats[:, b, :]).then_inc(M["aggr"], 1)
            if route:
                need(dve, M["lg"], t + 1)
                step(nc.vector.tensor_tensor(lgt[:], bank(1)[:, 0:GROUP * E].rearrange("p (b e) -> p b e", e=E),
                                             bc(gb_sb[:], GROUP), ALU.add), "l0")
                step(nc.vector.tensor_reduce(rmx[:], lgt[:], AX.X, ALU.max), "mx")
                step(nc.vector.tensor_tensor(lgt[:], lgt[:], inner(rmx[:], E), ALU.subtract), "sh")
                need(dve, M["ex"], t + 1)
                step(nc.vector.tensor_scalar(lgt[:], lgt[:], EXP_FLOOR, None, ALU.max), "fl")
                other = lgt[:, :, None, :].broadcast_to([128, GROUP, E, E])
                own = lgt[:, :, :, None].broadcast_to([128, GROUP, E, E])
            if expert:
                hidden(0)
            if route:
                nc.vector.tensor_tensor(beats[:], other, own, ALU.is_gt).then_inc(M["gt"], 1)
                step(nc.vector.tensor_tensor(ties[:], other, own, ALU.is_equal), "eq")
                flat = before[:].rearrange("p e j -> p (e j)")[:, None, :].broadcast_to([128, GROUP, E * E])
                tf = ties[:].rearrange("p b e j -> p b (e j)")
                step(nc.vector.tensor_tensor(tf, tf, flat, ALU.mult), "eq2")
                need(dve, M["gt"], t + 1)
                step(nc.vector.tensor_tensor(beats[:], beats[:], ties[:], ALU.add), "sum")
                step(nc.vector.tensor_reduce(rank[:], beats[:].rearrange("p b e j -> p (b e) j"), AX.X, ALU.add), "rank")
            if expert:
                hidden(1)
            if route:
                need(dve, M["hp"], t)
                wide = inner(rank[:], R)
                h0 = hot[:, 0, :, :].rearrange("p b (e r) -> p (b e) r", r=R)
                h1 = hot[:, 1, :, :].rearrange("p b (e r) -> p (b e) r", r=R)
                step(nc.vector.tensor_scalar(h0, wide, 0.0, None, ALU.is_equal), "hot1")
                nc.vector.scalar_tensor_tensor(h1, wide, 1.0, h0, ALU.is_equal, ALU.subtract).then_inc(M["hot"], 1)
                step(nc.vector.tensor_scalar(top[:], rank[:], 2.0, None, ALU.is_lt), "top")
                step(nc.vector.tensor_tensor(top[:], top[:], merge(ex[:]), ALU.mult), "et")
                nc.vector.tensor_reduce(num[:], top[:].rearrange("p (b e) -> p b e", e=E), AX.X, ALU.add).then_inc(M["num"], 1)
                step(nc.vector.tensor_reduce(den[:], ex[:], AX.X, ALU.add), "den")
                step(nc.vector.reciprocal(rden[:], den[:]), "rden")
                need(dve, M["num"], t + 1)
                need(dve, M["out"], t - 1)
                nc.vector.tensor_tensor(vs[:, q, :], num[:], rden[:], ALU.mult).then_inc(M["vs"], 1)
            if expert:
                hidden(2)
                hidden(3)
            if norm:
                need(dve, M["rstd"], t + 2)
                need(dve, M["Tp"], t + 1)
                for b in range(GROUP):
                    last = nc.vector.tensor_scalar(xn3[:, b, :], src[:, b, :], meanvar[:, b, 0:1], rstd[:, b:b + 1],
                                                   ALU.subtract, ALU.mult)
                last.then_inc(M["xn"], 1)
            if route:
                need(dve, M["hp"], t + 1)
                need(dve, M["uT"], t + 1)
                need(dve, M["i2"], FC * (t - 1))
                for w in range(2):
                    last = nc.vector.tensor_tensor(um[:, q, w, :], bank(3 + w), uT[:], ALU.mult)
                last.then_inc(M["um"], 1)
            if expert:
                o = 1 - q
                old = x3(-1)
                need(dve, M["y"], p + 1)
                need(dve, M["vs"], p + 1)
                need(dve, s_out[o], 16 * (m + q))
                for b in range(GROUP):
                    last = nc.vector.scalar_tensor_tensor(y3[:, o, b, :], bank(7)[:, 128 * b:128 * b + 128], vs[:, o, b:b + 1],
                                                          old[:, b, :], ALU.mult, ALU.add)
                last.then_inc(M["out"], 1)

        def f_pool(pool, m, q, norm, route, expert):
            t = 2 * m + q
            if norm:
                need(pool, M["aggr"], GROUP * (t + 2))
                need(pool, M["rstd"], t + 1)
                nc.gpsimd.tensor_tensor(vareps[:], meanvar[:, :, 1], eps_tile[:, 0:GROUP], ALU.add).then_inc(M["vareps"], 1)
                need(pool, M["vareps"], t + 2)
                need(pool, M["xn"], t + 1)
                nc.gpsimd.tensor_tensor(rstd[:], vareps[:], minus_half[:, 0:GROUP], ALU.pow).then_inc(M["rstd"], 1)

        def f_flags(t):
            return (0 <= t + 1 < GROUPS, 0 <= t < GROUPS, 0 <= t - 1 < GROUPS)

        def f_ticks(engine, tick):
            for t in range(-1, 2):
                tick(t // 2, t % 2, *f_flags(t))
            with engine.Fori(1, GROUPS // 2 - 1, 1) as m:
                tick(m, 0, True, True, True)
                tick(m, 1, True, True, True)
            for t in range(GROUPS - 2, GROUPS + 1):
                tick(t // 2, t % 2, *f_flags(t))

        def f_stores(sp):
            for q in range(2):
                sp.sem_inc(s_out[q], 16)
            with sp.Fori(0, GROUPS // 2, 1) as m:
                for q in range(2):
                    g = 2 * m + q
                    sp.wait_ge(M["out"], g + 1)
                    sp.dma_start(out_d[:, bass.ds(GROUP * g, GROUP), :], y3[:, q, :, :]).then_inc(s_out[q], 16)
            for q in range(2):
                sp.wait_ge(s_out[q], 16 * (GROUPS // 2 + 1))

        blk = stack.enter_context(nc.Block())

        @blk.sync
        def _(sp):
            setup_sync(sp)
            if phases > 1:
                x_loads(sp)
            if phases < 3:
                if phases == 1:
                    sp.wait_ge(G["x1"], PAIRS)
                if phases == 2:
                    sp.wait_ge(C["x2"], B)
                sp.dma_start(out_d, X[:]).then_inc(s_out[0], 16)
                sp.wait_ge(s_out[0], 16)
            else:
                f_stores(sp)

        @blk.gpsimd
        def _(pool):
            setup_pool(pool)
            gsa_rstd(pool, 0)
            gsa_ticks(pool, lambda *a: gsa_pool(pool, *a))
            if phases > 1:
                pool.wait_ge(s_xw, XW)
                pool.wait_ge(s_km, 16)
                pool.wait_ge(s_wcopy, 6)
                pool.wait_ge(s_dconst, 2)
                x_steps(pool, lambda *a: x_pool(pool, *a))
            if phases > 2:
                f_ticks(pool, lambda *a: f_pool(pool, *a))

        @blk.scalar
        def _(act):
            setup_scalar(act)
            gsa_ticks(act, lambda t, par, gate, intra, mix, ahead: gsa_scalar(act, t, par, gate, intra, mix))
            if phases > 1:
                act.wait_ge(s_dconst, 2)
                x_steps(act, lambda *a: x_scalar(act, *a))
            if phases > 2:
                act.wait_ge(s_fw, FW)
                f_ticks(act, lambda *a: f_scalar(act, *a))

        @blk.vector
        def _(dve):
            setup_vector(dve)
            for s in s_x:
                dve.wait_ge(s, 16)
            gsa_stats(dve, 0, 0)
            gsa_normalise(dve, 0, 0)
            gsa_ticks(dve, lambda *a: gsa_vector(dve, *a))
            if phases > 1:
                dve.wait_ge(G["x1"], PAIRS)
                dve.wait_ge(s_const, CONST)
                dve.wait_ge(s_km, 16)
                x_steps(dve, lambda *a: x_vector(dve, *a))
            if phases > 2:
                dve.wait_ge(C["x2"], B)
                f_ticks(dve, lambda *a: f_vector(dve, *a))

        @blk.tensor
        def _(pe):
            setup_tensor(pe)
            pe.wait_ge(s_wcopy, 7)
            pe.wait_ge(s_dconst, 1)
            gsa_ticks(pe, lambda t, par, gate, intra, mix, ahead: gsa_tensor(pe, t, par, gate, intra, mix))
            if phases > 1:
                pe.wait_ge(G["x1"], PAIRS)
                x_steps(pe, lambda *a: x_tensor(pe, *a))
            if phases > 2:
                pe.wait_ge(C["x2"], B)
                f_ticks(pe, lambda *a: f_tensor(pe, *a))


_INS = ['x', 'ctx_1024', 'fside_Bx16xSxS2_0', 'fside_SxS2_0', 'mask_BxS2_bf0', 'L0_attn_Wq', 'L0_attn_Wk', 'L0_attn_Wv',
        'L0_attn_Wf', 'L0_attn_g_norm_w', 'L0_attn_Wo', 'L0_xattn_Wq', 'L0_xattn_bq', 'L0_xattn_Wk', 'L0_xattn_bk',
        'L0_xattn_Wv', 'L0_xattn_bv', 'L0_xattn_Wo', 'L0_xattn_bo', 'L0_ffn_wi', 'L0_ffn_bi', 'L0_ffn_wo', 'L0_ffn_bo',
        'L0_ffn_lora_A', 'L0_ffn_lora_B', 'L0_ffn_gate_w', 'L0_ffn_gate_b']


def kernel(**inputs):
    import numpy as _np
    import concourse.bacc as _bacc
    from concourse import mybir as _mybir
    from concourse.bass_utils import run_bass_kernel_spmd as _run

    nc = _bacc.Bacc("TRN2", target_bir_lowering=False, num_devices=1)
    arrays, args = {}, []
    for name in _INS:
        a = _np.ascontiguousarray(inputs[name])
        arrays[f"in_{name}_dram"] = a
        args.append(nc.dram_tensor(f"in_{name}_dram", a.shape, _mybir.dt.from_np(a.dtype), kind="ExternalInput").ap())
    out = nc.dram_tensor("out_dram", (B, T, D), _mybir.dt.float32, kind="ExternalOutput").ap()
    decoder(nc, *args, out)
    r = _run(nc, [arrays], core_ids=[0])
    return r.results[0]["out_dram"]
```

```python
import concourse.bass as bass
from concourse import mybir
from contextlib import ExitStack

B, T, D = 32, 128, 128
GH, GK, GM = 4, 32, 64
XH, XD = 16, 8
XG = 4
NI = XH // XG
F, E, R = 512, 8, 16
FC = F // 128
PAIRS = B // 2
GROUP = 4
GROUPS = B // GROUP
EPS = 1e-5
EXP_FLOOR = -87.33654
GATE_DIV = 8.0


def need(engine, semaphore, count):
    if isinstance(count, int) and count <= 0:
        return
    engine.wait_ge(semaphore, count)


def hold(engine, semaphore, count, passed):
    if isinstance(count, int) and count <= 0:
        return
    engine.wait_ge(semaphore, count)
    engine.sem_inc(passed, 1)


def upto(count, most):
    return min(count, most) if isinstance(count, int) else count


def decoder(nc, x, ctx_in, fside, amask, kmask, g_wq, g_wk, g_wv, g_wf, g_norm, g_wo,
            x_wq, x_bq, x_wk, x_bk, x_wv, x_bv, x_wo, x_bo,
            wi, bi, wo, bo, lora_a, lora_b, gate_w, gate_b, out):
    fp32, u8 = mybir.dt.float32, mybir.dt.uint8
    ALU, ACT, AX = mybir.AluOpType, mybir.ActivationFunctionType, mybir.AxisListType

    stack = ExitStack()
    with stack:
        def sb(name, shape, dt=fp32):
            return stack.enter_context(nc.sbuf_tensor(name, shape, dt))

        def sem(name):
            return stack.enter_context(nc.semaphore(name))

        X = sb("X", [128, B, D])
        ident = sb("ident", [128, 128])
        ones = sb("ones", [128, 128])
        minus_half = sb("minus_half", [128, 16])
        eps_tile = sb("eps_tile", [128, 16])
        stats = sb("stats", [128, GROUP, 6])
        meanvar = sb("meanvar", [128, GROUP, 2])
        vareps = sb("vareps", [128, GROUP])
        rstd = sb("rstd", [128, GROUP])

        g_wqkf = sb("g_wqkf", [128, 512])
        g_wv_sb = sb("g_wv_sb", [128, 128])
        g_wo_raw = sb("g_wo_raw", [128, 128])
        g_wo_sb = sb("g_wo_sb", [128, 128])
        g_norm_col = sb("g_norm_col", [128, 1])
        mask_a = sb("mask_a", [128, 128])
        mask_b = sb("mask_b", [128, 128])
        tri_centred = sb("tri_centred", [128, 128])
        head_mask = sb("head_mask", [128, GH])
        x_w_raw = sb("x_w_raw", [128, 4, 128])
        x_wT = sb("x_wT", [128, 4, 128])
        bq_raw = sb("bq_raw", [128, 1])
        bq_col = sb("bq_col", [128, 1])
        bk_col = sb("bk_col", [128, 1])
        bv_col = sb("bv_col", [128, 1])
        bv_wide = sb("bv_wide", [128, 128])
        bo_row = sb("bo_row", [1, 128])
        x_bias = sb("x_bias", [128, 128])
        in_head = sb("in_head", [128, XH])
        k_mask = sb("k_mask", [128, XG])
        half_mask = sb("half_mask", [128, 128])
        amask_sb = sb("amask_sb", [128, 128])
        kmask_sb = sb("kmask_sb", [128, B * 128], u8)
        wi_raw = sb("wi_raw", [128, FC, 128])
        wo_raw = sb("wo_raw", [128, F])
        lb_raw = sb("lb_raw", [128, FC, E * R])
        la_raw = sb("la_raw", [128, 128])
        gw_raw = sb("gw_raw", [E, 128])
        wiT = sb("wiT", [128, F])
        woT = sb("woT", [128, FC, 128])
        lbT = sb("lbT", [128, F])
        laT = sb("laT", [128, 128])
        gwT = sb("gwT", [128, E])
        bi_col = sb("bi_col", [128, FC])
        neg_bi = sb("neg_bi", [128, FC])
        bi_wide = sb("bi_wide", [128, FC, 128])
        fbo_row = sb("fbo_row", [1, 128])
        twos = sb("twos", [1, 128])
        f_bias = sb("f_bias", [128, 128])
        gb_sb = sb("gb_sb", [128, E])
        before = sb("before", [128, E, E])

        SHARED = 20736
        shared = sb("shared", [128, SHARED])
        at = [0]

        def carve(shape):
            n = 1
            for k in shape[1:]:
                n *= k
            part = shared[:, at[0]:at[0] + n]
            at[0] += n
            assert at[0] <= SHARED
            names = "abcde"[:len(shape) - 1]
            if len(names) == 1:
                return part
            return part.rearrange(f"p ({' '.join(names)}) -> p {' '.join(names)}", **dict(zip(names, shape[1:])))

        banks = stack.enter_context(nc.psum_tensor("banks", [128, 8, 512], fp32))

        s_x = [sem(f"x_loaded{i}") for i in range(4)]
        s_gw = sem("slot_weights_loaded")
        s_xw = sem("cross_weights_loaded")
        s_fw = sem("expert_weights_loaded")
        s_km = sem("key_mask_loaded")
        s_const = sem("constants_made")
        s_passed = sem("waits_passed")
        s_cstep = sem("constant_step")
        s_wT = sem("weights_transposed")
        s_wcopy = sem("transposed_weights_copied")
        s_wide = sem("wide_biases_made")
        s_dconst = sem("vector_constants_made")

        x_d = x.rearrange("b t d -> t b d")
        out_d = out.rearrange("b t d -> t b d")
        XC = B // 4

        def bank(i):
            return banks[:, i, :]

        def setup_sync(sp):
            sp.dma_start(X[:, 0:XC, :], x_d[:, 0:XC, :]).then_inc(s_x[0], 16)
            for src, lo in ((g_wq, 0), (g_wk, 128), (g_wf, 256)):
                sp.dma_start(g_wqkf[:, lo:lo + src.shape[1]], src).then_inc(s_gw, 16)
            sp.dma_start(g_wv_sb[:], g_wv).then_inc(s_gw, 16)
            sp.dma_start(g_wo_raw[:], g_wo).then_inc(s_gw, 16)
            for h in range(GH):
                sp.dma_start(g_norm_col[GK * h:GK * h + GK, :], g_norm[:, None]).then_inc(s_gw, 16)
            for c in range(1, 4):
                sp.dma_start(X[:, c * XC:(c + 1) * XC, :], x_d[:, c * XC:(c + 1) * XC, :]).then_inc(s_x[c], 16)
            for i, w in enumerate((x_wq, x_wk, x_wv, x_wo)):
                sp.dma_start(x_w_raw[:, i, :], w).then_inc(s_xw, 16)
            for dst, src in ((bq_raw, x_bq), (bk_col, x_bk), (bv_col, x_bv)):
                sp.dma_start(dst[:], src[:, None]).then_inc(s_xw, 16)
            sp.dma_start(bo_row[:], x_bo[None, :]).then_inc(s_xw, 16)
            sp.dma_start(amask_sb[:], amask).then_inc(s_xw, 16)
            sp.dma_start(kmask_sb[:], kmask.rearrange("b s -> (b s)")[None, :].broadcast_to([128, B * 128])).then_inc(s_km, 16)
            sp.dma_start(wi_raw[:], wi.rearrange("(c p) d -> p c d", p=128)).then_inc(s_fw, 16)
            sp.dma_start(wo_raw[:], wo).then_inc(s_fw, 16)
            for c in range(FC):
                sp.dma_start(lb_raw[:, c, :].rearrange("p (e r) -> p e r", r=R),
                             lora_b[:, c * 128:(c + 1) * 128, :].rearrange("e p r -> p e r")).then_inc(s_fw, 16)
            sp.dma_start(la_raw[:], lora_a.rearrange("e r d -> (e r) d")).then_inc(s_fw, 16)
            sp.dma_start(gw_raw[:], gate_w).then_inc(s_fw, 16)
            for c in range(FC):
                sp.dma_start(bi_col[:, c:c + 1], bi[c * 128:(c + 1) * 128, None]).then_inc(s_fw, 16)
            sp.dma_start(fbo_row[:], bo[None, :]).then_inc(s_fw, 16)
            sp.dma_start(gb_sb[:], gate_b[None, :].broadcast_to([128, E])).then_inc(s_fw, 16)
        GW, XW, FW = 16 * 9, 16 * 9, 16 * (2 + FC + 2 + FC + 2)

        def setup_pool(pool):
            steps = [0]

            def step(ins):
                steps[0] += 1
                ins.then_inc(s_cstep, 1)
                pool.wait_ge(s_cstep, steps[0])

            for tile, value in ((ones, 1.0), (twos, 2.0), (minus_half, -0.5), (eps_tile, EPS), (head_mask, 1.0), (before, 1.0),
                                (in_head, 1.0), (mask_a, -float(GK) ** -0.5), (mask_b, -1.0),
                                (tri_centred, 1.0 / GATE_DIV), (ident, 0.0), (vp, 0.0)):
                step(nc.gpsimd.memset(tile[:], value))
            step(nc.gpsimd.affine_select(out=ident[:], in_=ident[:], compare_op=ALU.not_equal, fill=1.0, base=0,
                                         pattern=[[-1, 128]], channel_multiplier=1))
            for m in (mask_a, mask_b, tri_centred):
                step(nc.gpsimd.affine_select(out=m[:], in_=m[:], compare_op=ALU.is_ge, fill=0.0, base=0,
                                             pattern=[[1, 128]], channel_multiplier=-1))
            step(nc.gpsimd.tensor_scalar(tri_centred[0:T // 2, :], tri_centred[0:T // 2, :], -1.0 / GATE_DIV, None, ALU.add))
            step(nc.gpsimd.affine_select(out=before[:], in_=before[:], compare_op=ALU.is_gt, fill=0.0, base=0,
                                         pattern=[[1, E], [-1, E]], channel_multiplier=0))
            for m, heads, width in ((in_head, XH, XD), (head_mask, GH, GK)):
                step(nc.gpsimd.affine_select(out=m[:], in_=m[:], compare_op=ALU.is_ge, fill=0.0, base=0,
                                             pattern=[[-width, heads]], channel_multiplier=1))
                step(nc.gpsimd.affine_select(out=m[:], in_=m[:], compare_op=ALU.is_ge, fill=0.0, base=width - 1,
                                             pattern=[[width, heads]], channel_multiplier=-1))
            nc.gpsimd.memset(ppbd[:], 0.0).then_inc(s_const, 1)

        CONST = 1

        def setup_tensor(pe):
            pe.wait_ge(s_const, CONST)
            pe.wait_ge(s_xw, XW)
            for i in range(4):
                last = nc.tensor.transpose(bank(0)[:, 128 * i:128 * i + 128], x_w_raw[:, i, :], ident[:])
            last.then_inc(s_wT, 1)
            pe.wait_ge(s_fw, FW)
            for c in range(FC):
                last = nc.tensor.transpose(bank(1)[:, 128 * c:128 * c + 128], wi_raw[:, c, :], ident[:])
            last.then_inc(s_wT, 1)
            for c in range(FC):
                last = nc.tensor.transpose(bank(2)[:, 128 * c:128 * c + 128], wo_raw[:, 128 * c:128 * c + 128], ident[:])
            last.then_inc(s_wT, 1)
            for c in range(FC):
                last = nc.tensor.transpose(bank(3)[:, 128 * c:128 * c + 128], lb_raw[:, c, :], ident[:])
            last.then_inc(s_wT, 1)
            nc.tensor.transpose(bank(4)[:, 0:128], la_raw[:], ident[:])
            nc.tensor.transpose(bank(4)[:, 128:128 + E], gw_raw[:], ident[0:E, 0:E]).then_inc(s_wT, 1)
            pe.wait_ge(s_wcopy, 5)
            pe.wait_ge(s_dconst, 3)
            nc.tensor.matmul(bank(5)[:, 0:128], bv_wide[:], x_wT[:, 3, :], start=True, stop=False)
            nc.tensor.matmul(bank(5)[:, 0:128], ones[0:1, :], bo_row[:], start=False, stop=True).then_inc(s_wT, 1)
            for c in range(FC):
                nc.tensor.matmul(bank(6)[:, 0:128], bi_wide[:, c, :], woT[:, c, :], start=(c == 0), stop=False)
            nc.tensor.matmul(bank(6)[:, 0:128], twos[:], fbo_row[:], start=False, stop=True).then_inc(s_wT, 1)

        def setup_scalar(act):
            nc.scalar.preload_act_table_set("natural_log_exp_and_others")
            for n, (dst, src) in enumerate(((x_wT[:].rearrange("p i d -> p (i d)"), bank(0)), (wiT[:], bank(1)),
                                            (woT[:].rearrange("p i d -> p (i d)"), bank(2)), (lbT[:], bank(3)))):
                act.wait_ge(s_wT, n + 1)
                nc.scalar.copy(dst, src).then_inc(s_wcopy, 1)
            act.wait_ge(s_wT, 5)
            nc.scalar.copy(laT[:], bank(4)[:, 0:128])
            nc.scalar.copy(gwT[:], bank(4)[:, 128:128 + E]).then_inc(s_wcopy, 1)
            act.wait_ge(s_wT, 6)
            nc.scalar.copy(x_bias[:], bank(5)[:, 0:128]).then_inc(s_wcopy, 1)
            act.wait_ge(s_wT, 7)
            nc.scalar.copy(f_bias[:], bank(6)[:, 0:128]).then_inc(s_wcopy, 1)

        def setup_vector(dve):
            dve.wait_ge(s_const, CONST)
            dve.wait_ge(s_gw, GW)
            nc.vector.tensor_scalar(g_wo_sb[:], g_wo_raw[:], g_norm_col[:], float(GK) ** 0.5, ALU.mult,
                                    ALU.mult).then_inc(s_dconst, 1)
            dve.wait_ge(s_xw, XW)
            nc.vector.tensor_reduce(k_mask[:], in_head[:].rearrange("p (i j) -> p j i", j=XG), AX.X, ALU.add)
            nc.vector.tensor_scalar(half_mask[:], amask_sb[:], 0.5, None, ALU.mult)
            nc.vector.tensor_scalar(bq_col[:], bq_raw[:], 0.5 * float(XD) ** -0.5, None, ALU.mult)
            nc.vector.tensor_scalar(bv_wide[:], ones[:], bv_col[:], None, ALU.mult).then_inc(s_dconst, 1)
            dve.wait_ge(s_fw, FW)
            nc.vector.tensor_scalar(neg_bi[:], bi_col[:], -1.0, None, ALU.mult)
            for c in range(FC):
                last = nc.vector.tensor_scalar(bi_wide[:, c, :], ones[:], bi_col[:, c:c + 1], None, ALU.mult)
            last.then_inc(s_dconst, 1)

        xn = carve([128, 2, 128])
        xT = carve([128, 2, 2, 128])
        wk = carve([128, 2, 512])
        LS = carve([128, 2, 512])
        sg = carve([128, 2, 256])
        dec = carve([128, 2, 256])
        qk = carve([128, 2, 256])
        qkT = carve([128, 2, 2, 2, 128])
        qbd = carve([128, 2, 2, GH, 128])
        Ep = carve([128, 2, 2, 256])
        Em = carve([128, 2, 256])
        sp_ = carve([128, 2, 2, 256])
        spT = carve([128, 2, 2, 2, 128])
        vS = carve([128, 2, 2, 128])
        Am = carve([128, 2 * GH, 128])
        lg = carve([128, 2 * GH, GM])
        mx = carve([128, 2 * GH])
        rs = carve([128, 2, 2 * GH])
        pp = carve([128, 2, 256])
        ppbd = carve([128, 2, 2, 2, 2, 128])
        Bm = carve([128, 2 * GH, 128])
        sq = carve([128, 2 * GH, GK])
        ss = carve([128, 2 * GH])
        rt = carve([128, 2 * GH])
        rr = carve([128, 2 * GH])
        on = carve([128, 2 * GH, GK])
        onT = carve([128, 2, 128])

        G = {n: sem("g_" + n) for n in (
            "stats", "aggr", "vareps", "rstd", "xn", "xTp", "xT", "z", "abs", "exp1", "ln", "ls", "sig", "dec",
            "silu", "qkTp", "qkT", "qbd", "csum", "eplus", "eminus", "s", "sTp", "sT", "a", "am", "l", "vp", "v",
            "lgts", "mx", "shift", "p", "sum", "pp", "ppTp", "ppT", "b", "bm", "o", "sq", "ss", "rt", "rt2", "r",
            "on", "onTp", "onT", "y", "x1")}

        def bc(ap, n):
            return ap[:, None, :].broadcast_to([128, n, ap.shape[1]])

        def inner(ap, n):
            return ap[:, :, None].broadcast_to([128, ap.shape[1], n])

        def gsa_tensor(pe, t, par, gate, turn, intra, mix, ahead):
            def x_turned():
                need(pe, G["xn"], t + 1)
                need(pe, G["sT"], t - 1)
                for b in range(2):
                    last = nc.tensor.transpose(bank(2)[:, 128 * b:128 * b + 128], xn[:, b, :], ident[:])
                last.then_inc(G["xTp"], 1)

            def queries_keys_gates():
                need(pe, G["xT"], t + 1)
                need(pe, G["silu"], t)
                for b in range(2):
                    last = nc.tensor.matmul(bank(b), xT[:, par, b, :], g_wqkf[:], start=True, stop=True)
                last.then_inc(G["z"], 1)

            def decay_sums():
                p = t - 1
                need(pe, G["ls"], p + 1)
                need(pe, G["v"], p)
                nc.tensor.matmul(bank(3), tri_centred[:], LS[:, :, 256:512], start=True, stop=True).then_inc(G["csum"], 1)

            def values():
                p, q = t - 1, 1 - par
                need(pe, G["eminus"], p + 1)
                for b in range(2):
                    last = nc.tensor.matmul(bank(3)[:, 128 * b:128 * b + 128], xT[:, q, b, :], g_wv_sb[:], start=True, stop=True)
                last.then_inc(G["vp"], 1)

            def qk_turned():
                p = t - 1
                need(pe, G["silu"], p + 1)
                need(pe, G["xT"], upto(t + 1, PAIRS))
                need(pe, G["sT"], p)
                for w in range(2):
                    for b in range(2):
                        i = 2 * w + b
                        last = nc.tensor.transpose(bank(2)[:, 128 * i:128 * i + 128], qk[:, b, 128 * w:128 * w + 128], ident[:])
                last.then_inc(G["qkTp"], 1)

            def s_turned():
                p, q = t - 1, 1 - par
                need(pe, G["s"], p + 1)
                need(pe, G["qkT"], p + 1)
                for b in range(2):
                    for c in range(2):
                        i = 2 * b + c
                        last = nc.tensor.transpose(bank(2)[:, 128 * i:128 * i + 128], sp_[:, q, b, 128 * c:128 * c + 128], ident[:])
                last.then_inc(G["sTp"], 1)

            def attention():
                p, q = t - 2, par
                need(pe, G["qbd"], p + 1)
                need(pe, G["ppT"], 2 * p)
                need(pe, G["lgts"], p)
                for b in range(2):
                    last = nc.tensor.matmul(bank(4 + b), qkT[:, q, 1, b, :], qbd[:, q, b, :, :].rearrange("p h t -> p (h t)"),
                                            start=True, stop=True)
                last.then_inc(G["a"], 1)

            def slot_logits():
                p, q = t - 2, par
                need(pe, G["am"], p + 1)
                for b in range(2):
                    for h in range(GH):
                        last = nc.tensor.matmul(bank(4)[:, 256 * b + GM * h:256 * b + GM * h + GM], Am[:, GH * b + h, :],
                                                sp_[:, q, b, GM * h:GM * h + GM], start=True, stop=True)
                last.then_inc(G["l"], 1)

            def weights_turned():
                p = t - 2
                need(pe, G["pp"], p + 1)
                for b in range(2):
                    for c in range(2):
                        i = 2 * b + c
                        last = nc.tensor.transpose(bank(5)[:, 128 * i:128 * i + 128], pp[:, b, 128 * c:128 * c + 128], ident[:])
                last.then_inc(G["ppTp"], 1)

            def slot_mix():
                p, q = t - 3, 1 - par
                need(pe, G["ppT"], 2 * (p + 1))
                need(pe, G["sT"], p + 1)
                need(pe, G["onT"], p)
                need(pe, G["x1"], p)
                for b in range(2):
                    for c in range(2):
                        last = nc.tensor.matmul(bank(6 + b)[:, 256 * c:256 * c + 256], spT[:, q, b, c, :],
                                                ppbd[:, q, b, c, :, :].rearrange("p h t -> p (h t)"), start=True, stop=True)
                last.then_inc(G["b"], 1)

            def outputs():
                p, q = t - 3, 1 - par
                need(pe, G["bm"], p + 1)
                need(pe, G["v"], p + 1)
                for b in range(2):
                    for h in range(GH):
                        last = nc.tensor.matmul(bank(6)[:, 128 * b + GK * h:128 * b + GK * h + GK], Bm[:, GH * b + h, :],
                                                vS[:, q, b, GK * h:GK * h + GK], start=True, stop=True)
                last.then_inc(G["o"], 1)

            def outputs_turned():
                need(pe, G["on"], t - 2)
                for b in range(2):
                    last = nc.tensor.transpose(bank(7)[:, 128 * b:128 * b + 128],
                                               on[:, GH * b:GH * b + GH, :].rearrange("p h v -> p (h v)"), ident[:])
                last.then_inc(G["onTp"], 1)

            def project_out():
                need(pe, G["onT"], t - 2)
                for b in range(2):
                    last = nc.tensor.matmul(bank(6)[:, 128 * b:128 * b + 128], onT[:, b, :], g_wo_sb[:], start=True, stop=True)
                last.then_inc(G["y"], 1)

            if gate:
                x_turned()
            if intra:
                attention()
            if turn:
                decay_sums()
                qk_turned()
            if mix:
                slot_mix()
            if intra:
                slot_logits()
            if mix:
                outputs()
            if gate:
                queries_keys_gates()
            if turn:
                s_turned()
                values()
            if intra:
                weights_turned()
            if mix:
                outputs_turned()
                project_out()

        def gsa_scalar(act, t, par, gate, turn, intra, mix, ahead):
            def x_turned():
                need(act, G["xTp"], t + 1)
                need(act, G["vp"], t - 1)
                nc.scalar.copy(xT[:, par, :, :], bank(2)[:, 0:256].rearrange("p (b t) -> p b t", b=2)).then_inc(G["xT"], 1)

            def log_sigmoid():
                p = t
                need(act, G["z"], p + 1)
                need(act, G["ls"], p)
                nc.scalar.activation(wk[:], banks[:, 0:2, :], ACT.Abs).then_inc(G["abs"], 1)
                need(act, G["abs"], p + 1)
                nc.scalar.activation(wk[:], wk[:], ACT.Exp, scale=-1.0).then_inc(G["exp1"], 1)
                need(act, G["exp1"], p + 1)
                nc.scalar.activation(wk[:], wk[:], ACT.Ln, bias=1.0).then_inc(G["ln"], 1)

            def sigmoids():
                p = t - 1
                need(act, G["ls"], p + 1)
                need(act, G["silu"], p)
                nc.scalar.activation(sg[:], LS[:, :, 0:256], ACT.Exp).then_inc(G["sig"], 1)
                need(act, G["s"], p)
                nc.scalar.activation(dec[:], LS[:, :, 256:512], ACT.Exp, scale=1.0 / GATE_DIV).then_inc(G["dec"], 1)

            def decay_exps():
                p, q = t - 1, 1 - par
                need(act, G["csum"], p + 1)
                need(act, G["s"], p)
                need(act, G["pp"], p - 1)
                csum = bank(3).rearrange("p (b m) -> p b m", b=2)
                nc.scalar.activation(Em[:], csum, ACT.Exp, scale=-1.0)
                nc.scalar.activation(Ep[:, q, :, :], csum, ACT.Exp).then_inc(G["eminus"], 1)

            def values():
                p, q = t - 1, 1 - par
                need(act, G["vp"], p + 1)
                need(act, G["o"], p - 1)
                nc.scalar.copy(vS[:, q, :, :], bank(3)[:, 0:256].rearrange("p (b v) -> p b v", b=2)).then_inc(G["v"], 1)

            def qk_turned():
                p, q = t - 1, 1 - par
                need(act, G["qkTp"], p + 1)
                need(act, G["a"], p - 1)
                nc.scalar.copy(qkT[:, q, :, :, :].rearrange("p w b t -> p (w b t)"), bank(2)).then_inc(G["qkT"], 1)

            def s_turned():
                p, q = t - 1, 1 - par
                need(act, G["sTp"], p + 1)
                need(act, G["b"], p - 1)
                nc.scalar.copy(spT[:, q, :, :, :].rearrange("p b c t -> p (b c t)"), bank(2)).then_inc(G["sT"], 1)

            def slot_exps():
                need(act, G["shift"], t - 1)
                nc.scalar.activation(lg[:], lg[:], ACT.Exp).then_inc(G["p"], 1)

            def weights_turned():
                p, q = t - 2, par
                need(act, s_const, CONST)
                need(act, G["ppTp"], p + 1)
                need(act, G["b"], p - 1)
                src = bank(5).rearrange("p (b c t) -> p b c t", b=2, c=2)
                for half in range(2):
                    rows = slice(64 * half, 64 * half + 64)
                    nc.scalar.copy(ppbd[rows, q, :, :, half, :], src[rows, :, :, :]).then_inc(G["ppT"], 1)

            def squares():
                p = t - 3
                need(act, G["o"], p + 1)
                need(act, G["ss"], p)
                nc.scalar.activation(sq[:].rearrange("p h v -> p (h v)"), bank(6)[:, 0:256], ACT.Square).then_inc(G["sq"], 1)

            def outputs_turned():
                p = t - 3
                need(act, G["onTp"], p + 1)
                need(act, G["y"], p)
                nc.scalar.copy(onT[:].rearrange("p b t -> p (b t)"), bank(7)[:, 0:256]).then_inc(G["onT"], 1)

            if gate:
                x_turned()
            if turn:
                sigmoids()
                qk_turned()
                decay_exps()
            if mix:
                squares()
            if intra:
                slot_exps()
            if gate:
                log_sigmoid()
            if mix:
                outputs_turned()
            if turn:
                s_turned()
            if intra:
                weights_turned()
            if turn:
                values()

        def gsa_stats(dve, p):
            need(dve, G["xn"], p)
            need(dve, G["aggr"], 2 * p)
            for b in range(2):
                nc.vector.bn_stats(stats[:, b, :], X[:, 2 * p + b, :]).then_inc(G["stats"], 1)
            need(dve, G["vareps"], p)
            hold(dve, G["stats"], 2 * p + 2, s_passed)
            for b in range(2):
                nc.vector.bn_aggr(meanvar[:, b, :], stats[:, b, :]).then_inc(G["aggr"], 1)

        def gsa_normalise(dve, p):
            need(dve, G["rstd"], p + 1)
            need(dve, G["xTp"], p)
            for b in range(2):
                last = nc.vector.tensor_scalar(xn[:, b, :], X[:, 2 * p + b, :], meanvar[:, b, 0:1], rstd[:, b:b + 1],
                                               ALU.subtract, ALU.mult)
            last.then_inc(G["xn"], 1)

        def gsa_vector(dve, t, par, gate, turn, intra, mix, ahead):
            def log_sigmoid():
                p = t
                need(dve, G["ln"], p + 1)
                need(dve, G["csum"], p)
                need(dve, G["dec"], p)
                nc.vector.scalar_tensor_tensor(LS[:].rearrange("p b n -> p (b n)"),
                                               banks[:, 0:2, :].rearrange("p b n -> p (b n)"), 0.0,
                                               wk[:].rearrange("p b n -> p (b n)"), ALU.min, ALU.subtract).then_inc(G["ls"], 1)

            def silu():
                p = t - 1
                need(dve, G["sig"], p + 1)
                need(dve, G["qkTp"], p)
                nc.vector.tensor_tensor(qk[:], banks[:, 0:2, 0:256], sg[:], ALU.mult).then_inc(G["silu"], 1)

            def slots():
                p, q = t - 1, 1 - par
                need(dve, G["eminus"], p + 1)
                need(dve, G["dec"], p + 1)
                need(dve, G["l"], p - 1)
                nc.vector.scalar_tensor_tensor(sp_[:, q, :, :].rearrange("p b m -> p (b m)"),
                                               dec[:].rearrange("p b m -> p (b m)"), 1.0, Em[:].rearrange("p b m -> p (b m)"),
                                               ALU.subtract, ALU.mult).then_inc(G["s"], 1)

            def heads_apart():
                p, q = t - 1, 1 - par
                need(dve, G["qkT"], p + 1)
                for b in range(2):
                    last = nc.vector.tensor_tensor(qbd[:, q, b, :, :], bc(qkT[:, q, 0, b, :], GH), inner(head_mask[:], 128), ALU.mult)
                last.then_inc(G["qbd"], 1)

            def causal_attention():
                p = t - 2
                need(dve, G["a"], p + 1)
                need(dve, G["l"], p)
                nc.vector.tensor_tensor(Am[:], banks[:, 4:6, :].rearrange("p a (h t) -> p (a h) t", t=128),
                                        bc(mask_a[:], 2 * GH), ALU.mult).then_inc(G["am"], 1)

            def slot_logits():
                p, q = t - 2, par
                need(dve, G["l"], p + 1)
                need(dve, G["pp"], p)
                nc.vector.tensor_tensor(lg[:], bank(4).rearrange("p (h m) -> p h m", m=GM),
                                        Ep[:, q, :, :].rearrange("p b (h m) -> p (b h) m", m=GM), ALU.mult).then_inc(G["lgts"], 1)
                need(dve, G["lgts"], p + 1)
                nc.vector.tensor_reduce(mx[:], lg[:], AX.X, ALU.max).then_inc(G["mx"], 1)
                need(dve, G["mx"], p + 1)
                nc.vector.tensor_tensor(lg[:], lg[:], inner(mx[:], GM), ALU.subtract).then_inc(G["shift"], 1)

            def slot_sums():
                p, q = t - 2, par
                need(dve, G["p"], p + 1)
                nc.vector.tensor_reduce(rs[:, q, :], lg[:], AX.X, ALU.add).then_inc(G["sum"], 1)

            def causal_mix():
                p = t - 3
                need(dve, G["b"], p + 1)
                need(dve, G["o"], p)
                nc.vector.tensor_tensor(Bm[:], banks[:, 6:8, :].rearrange("p a (h t) -> p (a h) t", t=128),
                                        bc(mask_b[:], 2 * GH), ALU.mult).then_inc(G["bm"], 1)

            def mean_squares():
                p, q = t - 3, 1 - par
                need(dve, G["r"], p)
                need(dve, G["sum"], p + 1)
                nc.vector.scalar_tensor_tensor(rt[:], rs[:, q, :], GK * EPS, rs[:, q, :], ALU.mult, ALU.mult).then_inc(G["rt"], 1)
                need(dve, G["sq"], p + 1)
                nc.vector.tensor_reduce(ss[:], sq[:], AX.X, ALU.add).then_inc(G["ss"], 1)
                need(dve, G["ss"], p + 1)
                need(dve, G["rt"], p + 1)
                nc.vector.tensor_tensor(rt[:], rt[:], ss[:], ALU.add).then_inc(G["rt2"], 1)

            def outputs_normalised():
                p = t - 3
                need(dve, G["r"], p + 1)
                need(dve, G["onTp"], p)
                nc.vector.tensor_tensor(on[:], bank(6)[:, 0:256].rearrange("p (h v) -> p h v", v=GK), inner(rr[:], GK),
                                        ALU.mult).then_inc(G["on"], 1)

            def add_to_stream():
                p = t - 3
                need(dve, G["y"], p + 1)
                x1 = X[:, bass.ds(2 * p, 2), :]
                nc.vector.tensor_tensor(x1, bank(6)[:, 0:256].rearrange("p (b d) -> p b d", b=2), x1, ALU.add).then_inc(G["x1"], 1)

            def statistics():
                gsa_stats(dve, t + 1)

            def normalise():
                gsa_normalise(dve, t + 1)

            if ahead:
                statistics()
            if turn:
                silu()
            if intra:
                causal_attention()
            if ahead:
                normalise()
            if mix:
                causal_mix()
            if intra:
                slot_logits()
            if turn:
                heads_apart()
            if mix:
                mean_squares()
            if turn:
                slots()
            if intra:
                slot_sums()
            if mix:
                outputs_normalised()
            if gate:
                log_sigmoid()
            if mix:
                add_to_stream()

        def gsa_rstd(pool, p):
            need(pool, G["aggr"], 2 * (p + 1))
            need(pool, G["rstd"], p)
            nc.gpsimd.tensor_tensor(vareps[:, 0:2], meanvar[:, 0:2, 1], eps_tile[:, 0:2], ALU.add).then_inc(G["vareps"], 1)
            need(pool, G["vareps"], p + 1)
            need(pool, G["xn"], p)
            nc.gpsimd.tensor_tensor(rstd[:, 0:2], vareps[:, 0:2], minus_half[:, 0:2], ALU.pow).then_inc(G["rstd"], 1)

        def gsa_pool(pool, t, par, gate, turn, intra, mix, ahead):
            def root():
                p = t - 3
                need(pool, G["rt2"], p + 1)
                need(pool, G["on"], p)
                nc.gpsimd.tensor_tensor(rr[:], rt[:], minus_half[:, 0:2 * GH], ALU.pow).then_inc(G["r"], 1)

            def slot_weights():
                p, q = t - 2, par
                need(pool, G["p"], p + 1)
                need(pool, G["ppTp"], p)
                nc.gpsimd.tensor_tensor(pp[:].rearrange("p b m -> p (b m)"), lg[:].rearrange("p h m -> p (h m)"),
                                        Ep[:, q, :, :].rearrange("p b m -> p (b m)"), ALU.mult).then_inc(G["pp"], 1)

            def roots_ahead():
                gsa_rstd(pool, t + 1)

            if ahead:
                roots_ahead()
            if intra:
                slot_weights()
            if mix:
                root()

        def gsa_peeled(tick, t):
            tick(t, t % 2, t < PAIRS, 0 <= t - 1 < PAIRS, 0 <= t - 2 < PAIRS, t >= 3, t + 1 < PAIRS)

        def gsa_loop(engine, tick):
            with engine.Fori(4, PAIRS - 2, 2) as t:
                tick(t, 0, True, True, True, True, True)
                tick(t + 1, 1, True, True, True, True, True)

        ctxb = sb("c_ctx", [128, 2, 128])
        fs = sb("c_fside", [128, 2, XH, 128])
        fm = sb("c_bias", [128, 2, XH, 128])
        cm = sb("c_cm", [128, 128])
        xn2 = sb("c_xn", [128, 128])
        xT2 = sb("c_xT", [128, 128])
        cT = sb("c_cT", [128, 2, 128])
        qx = sb("c_q", [128, 2, 128])
        kx = sb("c_k", [128, 128])
        kbd = sb("c_kbd", [128, 2, XG, 128])
        VPAD = XG * (32 + XD)
        vp = sb("c_vpad", [128, 2, NI * VPAD])
        P = sb("c_P", [128, 2, XH, 128])
        mn = sb("c_min", [128, 2, XH])
        rsx = sb("c_sum", [128, 2, XH])
        rc = sb("c_recip", [128, XH])
        rx = sb("c_recipx", [128, XH, XD])
        RT = sb("c_recipT", [128, 128])
        PTs = sb("c_PT", [128, NI, 512])
        oTs = sb("c_oT", [128, 128])

        C = {n: sem("c_" + n) for n in (
            "stats", "aggr", "vareps", "rstd", "xn", "xbias", "Tp", "T", "qkp", "q", "k", "kbd", "cm", "fm", "vpz",
            "sc", "tt", "ex", "rc", "rx", "Rp", "RT", "pt", "ptD", "ptA", "pv", "oT", "yv", "v", "x2")}
        s_ctx = [sem(f"c_ctx_loaded{i}") for i in range(2)]
        s_fs = [sem(f"c_fside_loaded{i}") for i in range(2)]

        def x_tensor(pe, m, q, norm, project, scores, attend, finish):
            n = 2 * m + q
            o = 1 - q

            def score(i):
                need(pe, C["q"], n + 2)
                need(pe, C["kbd"], n + 2)
                need(pe, C["tt"], 4 * n + i + 1)
                rows = slice(32 * i, 32 * i + 32)
                nc.tensor.matmul(bank(1 + i), qx[rows, o, :], kbd[rows, o, :, :].rearrange("p j s -> p (j s)"),
                                 start=True, stop=True).then_inc(C["sc"], 1)

            def inputs_turned():
                need(pe, C["xn"], n + 3)
                need(pe, s_ctx[q], 16 * (m + 2))
                need(pe, C["RT"], n)
                need(pe, C["k"], n + 2)
                nc.tensor.transpose(bank(0)[:, 0:128], xn2[:], ident[:])
                nc.tensor.transpose(bank(0)[:, 128:256], ctxb[:, q, :], ident[:]).then_inc(C["Tp"], 1)

            def queries_keys():
                need(pe, C["T"], n + 3)
                nc.tensor.matmul(bank(0)[:, 0:128], x_wT[:, 0, :], xT2[:], start=True, stop=True)
                nc.tensor.matmul(bank(0)[:, 128:256], x_wT[:, 1, :], cT[:, q, :], start=True, stop=True).then_inc(C["qkp"], 1)

            def outputs_values():
                if project:
                    need(pe, C["k"], n + 3)
                else:
                    need(pe, C["RT"], n)
                if finish:
                    need(pe, C["oT"], n)
                    last = nc.tensor.matmul(bank(0)[:, 0:128], oTs[:], x_wT[:, 3, :], start=True, stop=True)
                if scores:
                    last = nc.tensor.matmul(bank(0)[:, 128:256], cT[:, o, :], x_wT[:, 2, :], start=True, stop=True)
                last.then_inc(C["yv"], 1)

            def reciprocals_turned():
                need(pe, C["rx"], n + 1)
                need(pe, C["x2"], n)
                if scores:
                    need(pe, C["v"], n + 2)
                nc.tensor.transpose(bank(0)[:, 0:128], rx[:].rearrange("p h d -> p (h d)"), ident[:]).then_inc(C["Rp"], 1)

            def weights_turned(i):
                need(pe, C["ex"], 4 * n + i + 1)
                if i == 1:
                    need(pe, C["ptA"], n)
                else:
                    need(pe, C["ptD"], 3 * n + max(0, i - 1))
                for j in range(XG):
                    last = nc.tensor.transpose(bank(5 + i % 2)[:, 128 * j:128 * j + 128], P[:, q, XG * i + j, :], ident[:])
                last.then_inc(C["pt"], 1)

            def mix(i, par):
                for j in range(XG):
                    last = nc.tensor.matmul(bank(7)[32 * i:32 * i + 32, 0:128],
                                            vp[:, par, VPAD * i + 32 * j:VPAD * i + 32 * j + 32],
                                            PTs[:, i, 128 * j:128 * j + 128], start=(j == 0), stop=(j == XG - 1))
                last.then_inc(C["pv"], 1)

            def mix_last():
                need(pe, C["ptA"], n)
                mix(NI - 1, o)

            def mix_values(i):
                need(pe, C["ptD"], 3 * n + i + 1)
                if i == 0:
                    need(pe, C["oT"], n)
                    need(pe, C["v"], n + 1)
                mix(i, q)

            if scores:
                score(0)
            if project:
                inputs_turned()
            if attend:
                weights_turned(0)
            if finish:
                mix_last()
            if scores:
                score(1)
            if attend:
                weights_turned(1)
            if project:
                queries_keys()
            if attend:
                mix_values(0)
            if scores:
                score(2)
            if scores or finish:
                outputs_values()
            if attend:
                weights_turned(2)
            if scores:
                score(3)
            if attend:
                mix_values(1)
                reciprocals_turned()
                weights_turned(3)
                mix_values(2)

        def x_scalar(act, m, q, norm, project, scores, attend, finish):
            n = 2 * m + q
            o = 1 - q

            def exps(batch, par, i):
                need(act, C["tt"], 4 * batch + i + 1)
                for h in range(XG * i, XG * i + XG):
                    last = nc.scalar.activation(P[:, par, h, :], P[:, par, h, :], ACT.Exp, bias=mn[:, par, h:h + 1], scale=-1.0,
                                                accum_out=rsx[:, par, h:h + 1])
                last.then_inc(C["ex"], 1)

            def inputs_turned():
                need(act, C["Tp"], n + 3)
                need(act, C["yv"], n + 1)
                nc.scalar.copy(xT2[:], bank(0)[:, 0:128])
                nc.scalar.copy(cT[:, q, :], bank(0)[:, 128:256]).then_inc(C["T"], 1)

            def queries_keys():
                need(act, C["qkp"], n + 3)
                need(act, C["sc"], 4 * n + 4)
                nc.scalar.activation(qx[:, q, :], bank(0)[:, 0:128], ACT.Identity, bias=bq_col[:],
                                     scale=0.5 * float(XD) ** -0.5).then_inc(C["q"], 1)
                need(act, C["kbd"], n + 2)
                nc.scalar.activation(kx[:], bank(0)[:, 128:256], ACT.Identity, bias=bk_col[:]).then_inc(C["k"], 1)

            def reciprocals_turned():
                need(act, C["Rp"], n + 1)
                need(act, C["oT"], n)
                nc.scalar.copy(RT[:], bank(0)[:, 0:128]).then_inc(C["RT"], 1)

            def weights_turned():
                need(act, C["pt"], 4 * n + 4)
                need(act, C["pv"], 4 * n)
                nc.scalar.copy(PTs[:, 3, :], bank(6)).then_inc(C["ptA"], 1)

            if attend:
                exps(n, q, 3)
            if project:
                inputs_turned()
            if scores:
                exps(n + 1, o, 0)
            if project:
                queries_keys()
            if scores:
                exps(n + 1, o, 1)
                exps(n + 1, o, 2)
            if attend:
                reciprocals_turned()
                weights_turned()

        def x_row(m, q, k):
            n = 2 * m + q + k
            return X[:, n, :] if isinstance(n, int) else X[:, bass.ds(n, 1), :].rearrange("p a d -> p (a d)")

        def x_vector(dve, m, q, norm, project, scores, attend, finish):
            n = 2 * m + q
            o = 1 - q

            def score(i):
                need(dve, C["fm"], n + 2)
                need(dve, C["pt"], 4 * n - 3 + i)
                hold(dve, C["sc"], 4 * n + i + 5, s_passed)
                for j in range(XG):
                    h = XG * i + j
                    last = nc.vector.tensor_tensor_reduce(out=P[:, o, h, :], in0=bank(1 + i)[:, 128 * j:128 * j + 128],
                                                          in1=fm[:, o, h, :], scale=-2.0, scalar=3.0e38, op0=ALU.add,
                                                          op1=ALU.min, accum_out=mn[:, o, h:h + 1])
                last.then_inc(C["tt"], 1)

            def statistics():
                need(dve, C["xn"], n + 3)
                need(dve, C["aggr"], n + 3)
                nc.vector.bn_stats(stats[:, 0, :], x_row(m, q, 3)).then_inc(C["stats"], 1)

            def aggregates():
                need(dve, C["vareps"], n + 3)
                hold(dve, C["stats"], n + 4, s_passed)
                nc.vector.bn_aggr(meanvar[:, 0, :], stats[:, 0, :]).then_inc(C["aggr"], 1)

            def normalise():
                need(dve, C["rstd"], n + 4)
                need(dve, C["Tp"], n + 3)
                nc.vector.tensor_scalar(xn2[:], x_row(m, q, 3), meanvar[:, 0, 0:1], rstd[:, 0:1],
                                        ALU.subtract, ALU.mult).then_inc(C["xn"], 1)

            def masks():
                need(dve, C["fm"], n + 2)
                km = kmask_sb[:, bass.ds((n + 2) * T, T)]
                nc.vector.scalar_tensor_tensor(cm[:], km, -3.0e38, half_mask[:], ALU.mult, ALU.add).then_inc(C["cm"], 1)

            def outputs():
                need(dve, C["pv"], 4 * n)
                need(dve, C["RT"], n)
                need(dve, C["yv"], n + 1)
                nc.vector.tensor_tensor(oTs[:], bank(7)[:, 0:128], RT[:], ALU.mult).then_inc(C["oT"], 1)

            def weights_turned(i):
                need(dve, C["pt"], 4 * n + i + 1)
                need(dve, C["pv"], 4 * n - 3 + i)
                nc.vector.tensor_copy(PTs[:, i, :], bank(5 + i % 2)).then_inc(C["ptD"], 1)

            def reciprocals():
                need(dve, C["ex"], 4 * n + 4)
                nc.vector.reciprocal(rc[:], rsx[:, q, :]).then_inc(C["rc"], 1)

            def reciprocals_spread():
                need(dve, C["rc"], n + 1)
                need(dve, C["Rp"], n)
                nc.vector.tensor_copy(rx[:], inner(rc[:], XD)).then_inc(C["rx"], 1)

            def add_to_stream():
                need(dve, C["yv"], n + 2)
                need(dve, C["xbias"], n)
                nc.vector.tensor_tensor(x_row(m, q, -1), bank(0)[:, 0:128], x_row(m, q, -1), ALU.add).then_inc(C["x2"], 1)

            def values():
                need(dve, C["yv"], n + 2)
                need(dve, C["pv"], 4 * n)
                dst = vp[:, o, :].rearrange("p (i j w) -> p i j w", i=NI, j=XG)[:, :, :, 0:XD]
                nc.vector.tensor_copy(dst, bank(0)[:, 128:256].rearrange("p (i j d) -> p i j d", i=NI, j=XG)).then_inc(C["v"], 1)

            if norm:
                statistics()
            if project:
                masks()
            if scores:
                score(0)
            if attend:
                weights_turned(0)
            if finish:
                outputs()
            if scores:
                score(1)
            if attend:
                weights_turned(1)
                reciprocals()
                reciprocals_spread()
            if norm:
                aggregates()
            if scores:
                score(2)
            if finish:
                add_to_stream()
            if scores:
                values()
            if attend:
                weights_turned(2)
            if scores:
                score(3)
            if norm:
                normalise()

        def x_pool(pool, m, q, norm, project, scores, attend, finish):
            n = 2 * m + q

            def output_bias():
                need(pool, C["xn"], n + 3)
                nc.gpsimd.tensor_tensor(x_row(m, q, 2), x_row(m, q, 2), x_bias[:], ALU.add).then_inc(C["xbias"], 1)

            def roots():
                need(pool, C["aggr"], n + 4)
                need(pool, C["rstd"], n + 3)
                nc.gpsimd.tensor_tensor(vareps[:, 0:1], meanvar[:, 0, 1:2], eps_tile[:, 0:1], ALU.add).then_inc(C["vareps"], 1)
                need(pool, C["vareps"], n + 4)
                need(pool, C["xn"], n + 3)
                nc.gpsimd.tensor_tensor(rstd[:, 0:1], vareps[:, 0:1], minus_half[:, 0:1], ALU.pow).then_inc(C["rstd"], 1)

            def biases():
                need(pool, C["cm"], n + 3)
                need(pool, s_fs[q], 32 * (m + 2))
                need(pool, C["tt"], 4 * n + 4)
                nc.gpsimd.tensor_tensor(fm[:, q, :, :], fs[:, q, :, :], bc(cm[:], XH), ALU.add).then_inc(C["fm"], 1)

            def keys_apart():
                need(pool, C["k"], n + 3)
                need(pool, C["sc"], 4 * n + 4)
                nc.gpsimd.tensor_tensor(kbd[:, q, :, :], bc(kx[:], XG), inner(k_mask[:], 128), ALU.mult).then_inc(C["kbd"], 1)

            if project:
                biases()
            if norm:
                roots()
            if project:
                keys_apart()
                output_bias()

        def x_peeled(step, n):
            step(n // 2, n % 2, *(0 <= n + k < B for k in (3, 2, 1, 0, -1)))

        def x_loop(engine, step):
            with engine.Fori(1, B // 2 - 2, 1) as m:
                step(m, 0, True, True, True, True, True)
                step(m, 1, True, True, True, True, True)

        def x_loads(sp):
            def load(m, q):
                n = 2 * m + q
                need(sp, C["Tp"], n - 1)
                sp.dma_start(ctxb[:, q, :], ctx_in[bass.ds(n, 1)].rearrange("o s d -> (o s) d")).then_inc(s_ctx[q], 16)
                need(sp, C["fm"], n - 1)
                bias = fside[bass.ds(n, 1)].rearrange("o h t s -> (o t) h s")
                for half in range(2):
                    rows = slice(64 * half, 64 * half + 64)
                    sp.dma_start(fs[rows, q, :, :], bias[rows, :, :]).then_inc(s_fs[q], 16)
            load(0, 0)
            load(0, 1)
            with sp.Fori(1, B // 2, 1) as m:
                load(m, 0)
                load(m, 1)

        NT = GROUP * 128
        at[0] = 0
        xn3 = carve([128, GROUP, 128])
        xT3 = carve([128, 2, NT])
        uT = carve([128, NT])
        um = carve([128, 2, 2, NT])
        lgt = carve([128, GROUP, E])
        rmx = carve([128, GROUP])
        ex = carve([128, GROUP, E])
        beats = carve([128, GROUP, E, E])
        ties = carve([128, GROUP, E, E])
        rank = carve([128, GROUP * E])
        top = carve([128, GROUP * E])
        den = carve([128, GROUP])
        rden = carve([128, GROUP])
        num = carve([128, GROUP])
        vs = carve([128, 2, GROUP])
        hot = carve([128, 2, GROUP, E * R])
        r1 = carve([128, FC, NT])
        hT = carve([128, FC, NT])
        y3 = carve([128, 2, GROUP, 128])

        M = {n: sem("f_" + n) for n in (
            "stats", "aggr", "vareps", "rstd", "xn", "Tp", "xT", "lg", "up", "uT", "l0", "mx", "sh", "ex", "fl", "gt", "eq",
            "eq2", "sum", "rank", "top", "et", "num", "den", "rden", "vs", "hot1", "hot", "hp", "um", "i1", "r1", "i2", "h",
            "y", "out")}
        s_out = [sem(f"stored{i}") for i in range(2)]

        def f_tensor(pe, m, q, norm, route, expert):
            t = 2 * m + q
            def x_turned():
                need(pe, M["xn"], t + 1)
                need(pe, M["uT"], t)
                for b in range(GROUP):
                    last = nc.tensor.transpose(bank(1)[:, 128 * b:128 * b + 128], xn3[:, b, :], ident[:])
                last.then_inc(M["Tp"], 1)

            def logits():
                need(pe, M["xT"], t + 1)
                need(pe, M["l0"], t)
                for b in range(GROUP):
                    last = nc.tensor.matmul(bank(2)[:, E * b:E * b + E], xT3[:, q, 128 * b:128 * b + 128], gwT[:],
                                            start=True, stop=True)
                last.then_inc(M["lg"], 1)

            def lora_inner():
                need(pe, M["xT"], t + 1)
                nc.tensor.matmul(bank(1), laT[:], xT3[:, q, :], start=True, stop=True).then_inc(M["up"], 1)

            def choices_turned():
                need(pe, M["hot"], t + 1)
                need(pe, M["um"], t)
                for w in range(2):
                    for b in range(GROUP):
                        last = nc.tensor.transpose(bank(3 + w)[:, 128 * b:128 * b + 128], hot[:, w, b, :], ident[:])
                last.then_inc(M["hp"], 1)

            p, o = t - 1, 1 - q

            def first(c):
                need(pe, M["um"], p + 1)
                need(pe, M["h"], FC * p + c - 1)
                nc.tensor.matmul(bank(5 + c % 2), wiT[:, 128 * c:128 * c + 128], xT3[:, o, :], start=True, stop=False)
                nc.tensor.matmul(bank(5 + c % 2), lbT[:, 128 * c:128 * c + 128], um[:, o, 0, :], start=False,
                                 stop=True).then_inc(M["i1"], 1)

            def second(c):
                need(pe, M["r1"], FC * p + c + 1)
                nc.tensor.matmul(bank(5 + c % 2), lbT[:, 128 * c:128 * c + 128], um[:, o, 1, :], start=False, stop=True,
                                 skip_group_check=True).then_inc(M["i2"], 1)

            def down():
                need(pe, M["h"], FC * p + FC)
                need(pe, M["out"], p)
                for b in range(GROUP):
                    for c in range(FC):
                        nc.tensor.matmul(bank(7)[:, 128 * b:128 * b + 128], hT[:, c, 128 * b:128 * b + 128], woT[:, c, :],
                                         start=(c == 0), stop=False)
                    last = nc.tensor.matmul(bank(7)[:, 128 * b:128 * b + 128], ones[0:1, :], f_bias[0:1, :],
                                            start=False, stop=True)
                last.then_inc(M["y"], 1)

            if route:
                x_turned()
            if expert:
                first(0)
            if route:
                logits()
            if expert:
                second(0)
                first(1)
            if route:
                lora_inner()
            if expert:
                second(1)
                first(2)
                first(3)
                second(2)
                second(3)
            if route:
                choices_turned()
            if expert:
                down()

        def f_scalar(act, m, q, norm, route, expert):
            t = 2 * m + q
            p = t - 1

            def relu(c):
                need(act, M["i1"], FC * p + c + 1)
                need(act, M["h"], FC * (p - 1) + c + 1)
                nc.scalar.activation(r1[:, c, :], bank(5 + c % 2), ACT.Relu, bias=bi_col[:, c:c + 1]).then_inc(M["r1"], 1)

            def x_turned():
                need(act, M["Tp"], t + 1)
                need(act, M["i2"], FC * (t - 1))
                nc.scalar.copy(xT3[:, q, :], bank(1)).then_inc(M["xT"], 1)

            def lora_inner():
                need(act, M["up"], t + 1)
                need(act, M["um"], t)
                nc.scalar.copy(uT[:], bank(1)).then_inc(M["uT"], 1)

            def gate_exps():
                need(act, M["sh"], t + 1)
                need(act, M["den"], t)
                nc.scalar.activation(ex[:], lgt[:], ACT.Exp).then_inc(M["ex"], 1)

            if route:
                x_turned()
            if expert:
                relu(0)
            if route:
                gate_exps()
            if expert:
                relu(1)
            if route:
                lora_inner()
            if expert:
                relu(2)
                relu(3)

        def f_vector(dve, m, q, norm, route, expert):
            t = 2 * m + q
            p, o = t - 1, 1 - q

            def x3(k):
                g = t + k
                return X[:, GROUP * g:GROUP * g + GROUP, :] if isinstance(g, int) else X[:, bass.ds(GROUP * g, GROUP), :]

            def step(ins, name):
                ins.then_inc(M[name], 1)
                need(dve, M[name], t + 1)

            def statistics():
                need(dve, M["aggr"], GROUP * (t + 1))
                src = x3(1)
                for b in range(GROUP):
                    nc.vector.bn_stats(stats[:, b, :], src[:, b, :]).then_inc(M["stats"], 1)
                need(dve, M["vareps"], t + 1)
                hold(dve, M["stats"], GROUP * (t + 2), s_passed)
                for b in range(GROUP):
                    nc.vector.bn_aggr(meanvar[:, b, :], stats[:, b, :]).then_inc(M["aggr"], 1)

            def normalise():
                need(dve, M["rstd"], t + 2)
                need(dve, M["Tp"], t + 1)
                src = x3(1)
                for b in range(GROUP):
                    last = nc.vector.tensor_scalar(xn3[:, b, :], src[:, b, :], meanvar[:, b, 0:1], rstd[:, b:b + 1],
                                                   ALU.subtract, ALU.mult)
                last.then_inc(M["xn"], 1)

            def logits():
                need(dve, M["lg"], t + 1)
                step(nc.vector.tensor_tensor(lgt[:], bank(2)[:, 0:GROUP * E].rearrange("p (b e) -> p b e", e=E),
                                             bc(gb_sb[:], GROUP), ALU.add), "l0")
                step(nc.vector.tensor_reduce(rmx[:], lgt[:], AX.X, ALU.max), "mx")
                step(nc.vector.tensor_tensor(lgt[:], lgt[:], inner(rmx[:], E), ALU.subtract), "sh")

            def ranks():
                need(dve, M["ex"], t + 1)
                step(nc.vector.tensor_scalar(lgt[:], lgt[:], EXP_FLOOR, None, ALU.max), "fl")
                other = lgt[:, :, None, :].broadcast_to([128, GROUP, E, E])
                own = lgt[:, :, :, None].broadcast_to([128, GROUP, E, E])
                nc.vector.tensor_tensor(beats[:], other, own, ALU.is_gt).then_inc(M["gt"], 1)
                step(nc.vector.tensor_tensor(ties[:], other, own, ALU.is_equal), "eq")
                flat = before[:].rearrange("p e j -> p (e j)")[:, None, :].broadcast_to([128, GROUP, E * E])
                tf = ties[:].rearrange("p b e j -> p b (e j)")
                step(nc.vector.tensor_tensor(tf, tf, flat, ALU.mult), "eq2")
                need(dve, M["gt"], t + 1)
                step(nc.vector.tensor_tensor(beats[:], beats[:], ties[:], ALU.add), "sum")
                step(nc.vector.tensor_reduce(rank[:], beats[:].rearrange("p b e j -> p (b e) j"), AX.X, ALU.add), "rank")

            def choices():
                need(dve, M["rank"], t + 1)
                need(dve, M["hp"], t)
                wide = inner(rank[:], R)
                h0 = hot[:, 0, :, :].rearrange("p b (e r) -> p (b e) r", r=R)
                h1 = hot[:, 1, :, :].rearrange("p b (e r) -> p (b e) r", r=R)
                step(nc.vector.tensor_scalar(h0, wide, 0.0, None, ALU.is_equal), "hot1")
                nc.vector.scalar_tensor_tensor(h1, wide, 1.0, h0, ALU.is_equal, ALU.subtract).then_inc(M["hot"], 1)

            def gates():
                step(nc.vector.tensor_scalar(top[:], rank[:], 2.0, None, ALU.is_lt), "top")
                step(nc.vector.tensor_tensor(top[:], top[:], ex[:].rearrange("p b e -> p (b e)"), ALU.mult), "et")
                nc.vector.tensor_reduce(num[:], top[:].rearrange("p (b e) -> p b e", e=E), AX.X, ALU.add).then_inc(M["num"], 1)
                step(nc.vector.tensor_reduce(den[:], ex[:], AX.X, ALU.add), "den")
                step(nc.vector.reciprocal(rden[:], den[:]), "rden")
                need(dve, M["num"], t + 1)
                need(dve, M["out"], t - 1)
                nc.vector.tensor_tensor(vs[:, q, :], num[:], rden[:], ALU.mult).then_inc(M["vs"], 1)

            def chosen_inner():
                need(dve, M["hp"], t + 1)
                need(dve, M["uT"], t + 1)
                need(dve, M["i2"], FC * (t - 1))
                for w in range(2):
                    last = nc.vector.tensor_tensor(um[:, q, w, :], bank(3 + w), uT[:], ALU.mult)
                last.then_inc(M["um"], 1)

            def hidden(c):
                need(dve, M["i2"], FC * p + c + 1)
                need(dve, M["y"], p)
                nc.vector.scalar_tensor_tensor(hT[:, c, :], bank(5 + c % 2), neg_bi[:, c:c + 1], r1[:, c, :],
                                               ALU.max, ALU.add).then_inc(M["h"], 1)

            def add_to_stream():
                old = x3(-1)
                need(dve, M["y"], p + 1)
                need(dve, M["vs"], p + 1)
                need(dve, s_out[o], 16 * (m + q))
                for b in range(GROUP):
                    last = nc.vector.scalar_tensor_tensor(y3[:, o, b, :], bank(7)[:, 128 * b:128 * b + 128], vs[:, o, b:b + 1],
                                                          old[:, b, :], ALU.mult, ALU.add)
                last.then_inc(M["out"], 1)

            if route:
                logits()
            if norm:
                statistics()
            if expert:
                hidden(0)
            if route:
                ranks()
            if expert:
                hidden(1)
            if norm:
                normalise()
            if route:
                choices()
                gates()
            if expert:
                hidden(2)
                hidden(3)
            if route:
                chosen_inner()
            if expert:
                add_to_stream()

        def f_pool(pool, m, q, norm, route, expert):
            t = 2 * m + q
            if norm:
                need(pool, M["aggr"], GROUP * (t + 2))
                need(pool, M["rstd"], t + 1)
                nc.gpsimd.tensor_tensor(vareps[:], meanvar[:, :, 1], eps_tile[:, 0:GROUP], ALU.add).then_inc(M["vareps"], 1)
                need(pool, M["vareps"], t + 2)
                need(pool, M["xn"], t + 1)
                nc.gpsimd.tensor_tensor(rstd[:], vareps[:], minus_half[:, 0:GROUP], ALU.pow).then_inc(M["rstd"], 1)

        def f_peeled(tick, t):
            tick(t // 2, t % 2, 0 <= t + 1 < GROUPS, 0 <= t < GROUPS, 0 <= t - 1 < GROUPS)

        def f_loop(engine, tick):
            with engine.Fori(1, GROUPS // 2 - 1, 1) as m:
                tick(m, 0, True, True, True)
                tick(m, 1, True, True, True)

        def f_stores(sp):
            for q in range(2):
                sp.sem_inc(s_out[q], 16)
            with sp.Fori(0, GROUPS // 2, 1) as m:
                for q in range(2):
                    g = 2 * m + q
                    sp.wait_ge(M["out"], g + 1)
                    sp.dma_start(out_d[:, bass.ds(GROUP * g, GROUP), :], y3[:, q, :, :]).then_inc(s_out[q], 16)
            for q in range(2):
                sp.wait_ge(s_out[q], 16 * (GROUPS // 2 + 1))

        blk = stack.enter_context(nc.Block())

        @blk.sync
        def _(sp):
            setup_sync(sp)
            x_loads(sp)
            f_stores(sp)

        @blk.gpsimd
        def _(pool):
            gsa = lambda *a: gsa_pool(pool, *a)
            cross = lambda *a: x_pool(pool, *a)
            experts = lambda *a: f_pool(pool, *a)
            setup_pool(pool)
            gsa_rstd(pool, 0)
            for t in range(4):
                gsa_peeled(gsa, t)
            gsa_loop(pool, gsa)
            for t in range(PAIRS - 2, PAIRS + 1):
                gsa_peeled(gsa, t)
            pool.wait_ge(G["xn"], PAIRS)
            x_peeled(cross, -3)
            gsa_peeled(gsa, PAIRS + 1)
            pool.wait_ge(s_xw, XW)
            pool.wait_ge(s_wcopy, 6)
            pool.wait_ge(s_dconst, 2)
            x_peeled(cross, -2)
            gsa_peeled(gsa, PAIRS + 2)
            for n in range(-1, 2):
                x_peeled(cross, n)
            x_loop(pool, cross)
            for n in range(B - 4, B - 2):
                x_peeled(cross, n)
            pool.wait_ge(C["xn"], B)
            f_peeled(experts, -1)
            for n in range(B - 2, B):
                x_peeled(cross, n)
            f_peeled(experts, 0)
            x_peeled(cross, B)
            f_peeled(experts, 1)
            f_loop(pool, experts)
            for t in range(GROUPS - 2, GROUPS + 1):
                f_peeled(experts, t)

        @blk.scalar
        def _(act):
            gsa = lambda *a: gsa_scalar(act, *a)
            cross = lambda *a: x_scalar(act, *a)
            experts = lambda *a: f_scalar(act, *a)
            setup_scalar(act)
            for t in range(4):
                gsa_peeled(gsa, t)
            gsa_loop(act, gsa)
            for t in range(PAIRS - 2, PAIRS + 1):
                gsa_peeled(gsa, t)
            act.wait_ge(s_dconst, 2)
            act.wait_ge(s_xw, XW)
            x_peeled(cross, -3)
            gsa_peeled(gsa, PAIRS + 1)
            x_peeled(cross, -2)
            gsa_peeled(gsa, PAIRS + 2)
            for n in range(-1, 2):
                x_peeled(cross, n)
            x_loop(act, cross)
            for n in range(B - 4, B - 2):
                x_peeled(cross, n)
            act.wait_ge(s_fw, FW)
            f_peeled(experts, -1)
            for n in range(B - 2, B):
                x_peeled(cross, n)
            f_peeled(experts, 0)
            x_peeled(cross, B)
            f_peeled(experts, 1)
            f_loop(act, experts)
            for t in range(GROUPS - 2, GROUPS + 1):
                f_peeled(experts, t)

        @blk.vector
        def _(dve):
            gsa = lambda *a: gsa_vector(dve, *a)
            cross = lambda *a: x_vector(dve, *a)
            experts = lambda *a: f_vector(dve, *a)
            setup_vector(dve)
            dve.wait_ge(s_x[0], 16)
            gsa_stats(dve, 0)
            gsa_normalise(dve, 0)
            for t in range(3):
                gsa_peeled(gsa, t)
            dve.wait_ge(s_x[1], 16)
            gsa_peeled(gsa, 3)
            dve.wait_ge(s_x[2], 16)
            dve.wait_ge(s_x[3], 16)
            gsa_loop(dve, gsa)
            for t in range(PAIRS - 2, PAIRS + 1):
                gsa_peeled(gsa, t)
            dve.wait_ge(G["xn"], PAIRS)
            dve.wait_ge(G["x1"], 2)
            x_peeled(cross, -3)
            gsa_peeled(gsa, PAIRS + 1)
            dve.wait_ge(s_km, 16)
            dve.wait_ge(s_const, CONST)
            x_peeled(cross, -2)
            gsa_peeled(gsa, PAIRS + 2)
            x_peeled(cross, -1)
            dve.wait_ge(G["x1"], PAIRS)
            for n in range(0, 2):
                x_peeled(cross, n)
            x_loop(dve, cross)
            for n in range(B - 4, B - 2):
                x_peeled(cross, n)
            dve.wait_ge(C["xn"], B)
            dve.wait_ge(C["x2"], 2 * GROUP)
            f_peeled(experts, -1)
            for n in range(B - 2, B):
                x_peeled(cross, n)
            f_peeled(experts, 0)
            x_peeled(cross, B)
            dve.wait_ge(C["x2"], B)
            f_peeled(experts, 1)
            f_loop(dve, experts)
            for t in range(GROUPS - 2, GROUPS + 1):
                f_peeled(experts, t)

        @blk.tensor
        def _(pe):
            gsa = lambda *a: gsa_tensor(pe, *a)
            cross = lambda *a: x_tensor(pe, *a)
            experts = lambda *a: f_tensor(pe, *a)
            setup_tensor(pe)
            pe.wait_ge(s_wcopy, 7)
            pe.wait_ge(s_dconst, 1)
            for t in range(4):
                gsa_peeled(gsa, t)
            gsa_loop(pe, gsa)
            for t in range(PAIRS - 2, PAIRS + 1):
                gsa_peeled(gsa, t)
            x_peeled(cross, -3)
            gsa_peeled(gsa, PAIRS + 1)
            pe.wait_ge(G["silu"], PAIRS)
            x_peeled(cross, -2)
            gsa_peeled(gsa, PAIRS + 2)
            pe.wait_ge(G["sT"], PAIRS)
            pe.wait_ge(G["v"], PAIRS)
            pe.wait_ge(G["lgts"], PAIRS)
            x_peeled(cross, -1)
            pe.wait_ge(G["x1"], PAIRS)
            for n in range(0, 2):
                x_peeled(cross, n)
            x_loop(pe, cross)
            for n in range(B - 4, B - 2):
                x_peeled(cross, n)
            f_peeled(experts, -1)
            for n in range(B - 2, B):
                x_peeled(cross, n)
            pe.wait_ge(C["tt"], 4 * B)
            f_peeled(experts, 0)
            x_peeled(cross, B)
            pe.wait_ge(C["x2"], B)
            f_peeled(experts, 1)
            f_loop(pe, experts)
            for t in range(GROUPS - 2, GROUPS + 1):
                f_peeled(experts, t)


_INS = ['x', 'ctx_1024', 'fside_Bx16xSxS2_0', 'fside_SxS2_0', 'mask_BxS2_bf0', 'L0_attn_Wq', 'L0_attn_Wk', 'L0_attn_Wv',
        'L0_attn_Wf', 'L0_attn_g_norm_w', 'L0_attn_Wo', 'L0_xattn_Wq', 'L0_xattn_bq', 'L0_xattn_Wk', 'L0_xattn_bk',
        'L0_xattn_Wv', 'L0_xattn_bv', 'L0_xattn_Wo', 'L0_xattn_bo', 'L0_ffn_wi', 'L0_ffn_bi', 'L0_ffn_wo', 'L0_ffn_bo',
        'L0_ffn_lora_A', 'L0_ffn_lora_B', 'L0_ffn_gate_w', 'L0_ffn_gate_b']


def kernel(**inputs):
    import numpy as _np
    import concourse.bacc as _bacc
    from concourse import mybir as _mybir
    from concourse.bass_utils import run_bass_kernel_spmd as _run

    nc = _bacc.Bacc("TRN2", target_bir_lowering=False, num_devices=1)
    arrays, args = {}, []
    for name in _INS:
        a = _np.ascontiguousarray(inputs[name])
        arrays[f"in_{name}_dram"] = a
        args.append(nc.dram_tensor(f"in_{name}_dram", a.shape, _mybir.dt.from_np(a.dtype), kind="ExternalInput").ap())
    out = nc.dram_tensor("out_dram", (B, T, D), _mybir.dt.float32, kind="ExternalOutput").ap()
    decoder(nc, *args, out)
    r = _run(nc, [arrays], core_ids=[0])
    return r.results[0]["out_dram"]
```

```python
import concourse.bass as bass
from concourse import mybir
from contextlib import ExitStack

B, T, D = 32, 128, 128
GH, GK, GM = 4, 32, 64
XH, XD = 16, 8
XG = 4
NI = XH // XG
F, E, R = 512, 8, 16
FC = F // 128
PAIRS = B // 2
GROUP = 4
GROUPS = B // GROUP
EPS = 1e-5
EXP_FLOOR = -87.33654
GATE_DIV = 8.0


def need(engine, semaphore, count):
    if isinstance(count, int) and count <= 0:
        return
    engine.wait_ge(semaphore, count)


def hold(engine, semaphore, count, passed):
    if isinstance(count, int) and count <= 0:
        return
    engine.wait_ge(semaphore, count)
    engine.sem_inc(passed, 1)


def upto(count, most):
    return min(count, most) if isinstance(count, int) else count


def decoder(nc, x, ctx_in, fside, amask, kmask, g_wq, g_wk, g_wv, g_wf, g_norm, g_wo,
            x_wq, x_bq, x_wk, x_bk, x_wv, x_bv, x_wo, x_bo,
            wi, bi, wo, bo, lora_a, lora_b, gate_w, gate_b, out):
    fp32, fp32r, u8 = mybir.dt.float32, mybir.dt.float32r, mybir.dt.uint8
    ALU, ACT, AX = mybir.AluOpType, mybir.ActivationFunctionType, mybir.AxisListType

    stack = ExitStack()
    with stack:
        def sb(name, shape, dt=fp32):
            return stack.enter_context(nc.sbuf_tensor(name, shape, dt))

        def sem(name):
            return stack.enter_context(nc.semaphore(name))

        X = sb("X", [128, B, D])
        ident = sb("ident", [128, 128])
        ones = sb("ones", [128, 128])
        minus_half = sb("minus_half", [128, 16])
        eps_tile = sb("eps_tile", [128, 16])
        stats = sb("stats", [128, GROUP, 6])
        meanvar = sb("meanvar", [128, GROUP, 2])
        vareps = sb("vareps", [128, GROUP])
        rstd = sb("rstd", [128, GROUP])

        g_wqkf = sb("g_wqkf", [128, 512])
        g_wv_sb = sb("g_wv_sb", [128, 128])
        g_wo_raw = sb("g_wo_raw", [128, 128])
        g_wo_sb = sb("g_wo_sb", [128, 128])
        g_norm_col = sb("g_norm_col", [128, 1])
        mask_a = sb("mask_a", [128, 128])
        mask_b = sb("mask_b", [128, 128])
        tri_centred = sb("tri_centred", [128, 128])
        head_mask = sb("head_mask", [128, GH])
        x_wT = sb("x_wT", [128, 4, 128])
        bq_raw = sb("bq_raw", [128, 1])
        bq_col = sb("bq_col", [128, 1])
        bk_col = sb("bk_col", [128, 1])
        bv_col = sb("bv_col", [128, 1])
        bv_wide = sb("bv_wide", [128, 128])
        bo_row = sb("bo_row", [1, 128])
        x_bias = sb("x_bias", [128, 128])
        in_head = sb("in_head", [128, XH])
        k_mask = sb("k_mask", [128, XG])
        half_mask = sb("half_mask", [128, 128])
        amask_sb = sb("amask_sb", [128, 128])
        kmask_sb = sb("kmask_sb", [128, B * 128], u8)
        la_raw = sb("la_raw", [128, 128])
        gw_raw = sb("gw_raw", [E, 128])
        woT = sb("woT", [128, FC, 128])
        laT = sb("laT", [128, 128])
        gwT = sb("gwT", [128, E])
        bi_col = sb("bi_col", [128, FC])
        neg_bi = sb("neg_bi", [128, FC])
        fbo_row = sb("fbo_row", [1, 128])
        twos = sb("twos", [1, 128])
        f_bias = sb("f_bias", [128, 128])
        gb_sb = sb("gb_sb", [128, E])
        before = sb("before", [128, E, E])

        P = sb("c_P", [128, 2, XH, 128])
        spare = P[:].rearrange("p q (n c) t -> p (q n) c t", c=FC)
        x_w_raw, wi_raw, lb_raw, wo_raw, bi_wide = (spare[:, k, :, :] for k in range(5))

        HIGH, LOW = 0, 1
        PASSES = ((HIGH, HIGH), (HIGH, LOW), (LOW, HIGH))
        NT = GROUP * 128
        xs = sb("xs", [128, 2, 2, NT], fp32r)
        um = sb("um", [128, 2, 2, 2, NT], fp32r)
        wi_s = sb("wi_s", [128, 2, F], fp32r)
        lb_s = sb("lb_s", [128, 2, F], fp32r)

        SHARED = 20736
        shared = sb("shared", [128, SHARED])
        at = [0]

        def carve(shape):
            n = 1
            for k in shape[1:]:
                n *= k
            part = shared[:, at[0]:at[0] + n]
            at[0] += n
            assert at[0] <= SHARED
            names = "abcde"[:len(shape) - 1]
            if len(names) == 1:
                return part
            return part.rearrange(f"p ({' '.join(names)}) -> p {' '.join(names)}", **dict(zip(names, shape[1:])))

        banks = stack.enter_context(nc.psum_tensor("banks", [128, 8, 512], fp32))

        s_x = [sem(f"x_loaded{i}") for i in range(4)]
        s_gw = sem("slot_weights_loaded")
        s_xw = sem("cross_weights_loaded")
        s_fw = sem("expert_weights_loaded")
        s_km = sem("key_mask_loaded")
        s_ident = sem("identity_made")
        s_masks = sem("slot_masks_made")
        s_const = sem("constants_made")
        s_passed = sem("waits_passed")
        s_cstep = sem("constant_step")
        s_wT = sem("weights_transposed")
        s_wcopy = sem("transposed_weights_copied")
        s_dconst = sem("vector_constants_made")

        x_d = x.rearrange("b t d -> t b d")
        out_d = out.rearrange("b t d -> t b d")
        XC = B // 4

        def bank(i):
            return banks[:, i, :]

        def setup_sync(sp):
            sp.dma_start(X[:, 0:XC, :], x_d[:, 0:XC, :]).then_inc(s_x[0], 16)
            for src, lo in ((g_wq, 0), (g_wk, 128), (g_wf, 256)):
                sp.dma_start(g_wqkf[:, lo:lo + src.shape[1]], src).then_inc(s_gw, 16)
            sp.dma_start(g_wv_sb[:], g_wv).then_inc(s_gw, 16)
            sp.dma_start(g_wo_raw[:], g_wo).then_inc(s_gw, 16)
            for h in range(GH):
                sp.dma_start(g_norm_col[GK * h:GK * h + GK, :], g_norm[:, None]).then_inc(s_gw, 16)
            for i, w in enumerate((x_wq, x_wk, x_wv, x_wo)):
                sp.dma_start(x_w_raw[:, i, :], w).then_inc(s_xw, 16)
            for dst, src in ((bq_raw, x_bq), (bk_col, x_bk), (bv_col, x_bv)):
                sp.dma_start(dst[:], src[:, None]).then_inc(s_xw, 16)
            sp.dma_start(bo_row[:], x_bo[None, :]).then_inc(s_xw, 16)
            sp.dma_start(amask_sb[:], amask).then_inc(s_xw, 16)
            sp.dma_start(wi_raw, wi.rearrange("(c p) d -> p c d", p=128)).then_inc(s_fw, 16)
            sp.dma_start(wo_raw, wo.rearrange("d (c f) -> d c f", c=FC)).then_inc(s_fw, 16)
            for c in range(FC):
                sp.dma_start(lb_raw[:, c, :].rearrange("p (e r) -> p e r", r=R),
                             lora_b[:, c * 128:(c + 1) * 128, :].rearrange("e p r -> p e r")).then_inc(s_fw, 16)
            sp.dma_start(la_raw[:], lora_a.rearrange("e r d -> (e r) d")).then_inc(s_fw, 16)
            sp.dma_start(gw_raw[:], gate_w).then_inc(s_fw, 16)
            for c in range(FC):
                sp.dma_start(bi_col[:, c:c + 1], bi[c * 128:(c + 1) * 128, None]).then_inc(s_fw, 16)
            sp.dma_start(fbo_row[:], bo[None, :]).then_inc(s_fw, 16)
            sp.dma_start(gb_sb[:], gate_b[None, :].broadcast_to([128, E])).then_inc(s_fw, 16)
            for c in range(1, 4):
                sp.dma_start(X[:, c * XC:(c + 1) * XC, :], x_d[:, c * XC:(c + 1) * XC, :]).then_inc(s_x[c], 16)
            sp.dma_start(kmask_sb[:], kmask.rearrange("b s -> (b s)")[None, :].broadcast_to([128, B * 128])).then_inc(s_km, 16)
        GW, XW, FW = 16 * 9, 16 * 9, 16 * (2 + FC + 2 + FC + 2)

        pool_steps = [0]

        def pool_step(pool, ins):
            pool_steps[0] += 1
            ins.then_inc(s_cstep, 1)
            pool.wait_ge(s_cstep, pool_steps[0])

        def fill(pool, *tiles):
            for tile, value in tiles:
                pool_step(pool, nc.gpsimd.memset(tile[:], value))

        def keep(pool, m, op, base, pattern, per_partition, other=0.0):
            pool_step(pool, nc.gpsimd.affine_select(out=m[:], in_=m[:], compare_op=op, fill=other, base=base,
                                                    pattern=pattern, channel_multiplier=per_partition))

        def in_block(pool, m, heads, width):
            keep(pool, m, ALU.is_ge, 0, [[-width, heads]], 1)
            keep(pool, m, ALU.is_ge, width - 1, [[width, heads]], -1)

        def setup_identity(pool):
            fill(pool, (minus_half, -0.5), (eps_tile, EPS), (ident, 0.0))
            keep(pool, ident, ALU.not_equal, 0, [[-1, 128]], 1, other=1.0)
            pool.sem_inc(s_ident, 1)

        def setup_slot_masks(pool):
            fill(pool, (tri_centred, 1.0 / GATE_DIV), (head_mask, 1.0), (mask_a, -float(GK) ** -0.5), (mask_b, -1.0))
            for m in (tri_centred, mask_a, mask_b):
                keep(pool, m, ALU.is_ge, 0, [[1, 128]], -1)
            pool_step(pool, nc.gpsimd.tensor_scalar(tri_centred[0:T // 2, :], tri_centred[0:T // 2, :], -1.0 / GATE_DIV, None,
                                                    ALU.add))
            in_block(pool, head_mask, GH, GK)
            pool.sem_inc(s_masks, 1)

        def setup_constants(pool):
            fill(pool, (ppbd, 0.0), (ones, 1.0), (twos, 2.0), (vp, 0.0), (in_head, 1.0), (before, 1.0))
            keep(pool, before, ALU.is_gt, 0, [[1, E], [-1, E]], 0)
            in_block(pool, in_head, XH, XD)
            pool.sem_inc(s_const, 1)

        def turn_weights(pieces):
            for place, weight, unit in pieces:
                last = nc.tensor.transpose(place, weight, unit)
            last.then_inc(s_wT, 1)

        def setup_tensor_0(pe):
            pe.wait_ge(s_xw, XW)
            turn_weights((bank(6)[:, 128 * i:128 * i + 128], x_w_raw[:, i, :], ident[:]) for i in range(4))

        def setup_tensor_1(pe):
            pe.wait_ge(s_fw, FW)
            turn_weights((bank(7)[:, 128 * c:128 * c + 128], wi_raw[:, c, :], ident[:]) for c in range(FC))
            pe.wait_ge(s_wcopy, 1)
            turn_weights((bank(6)[:, 128 * c:128 * c + 128], wo_raw[:, c, :], ident[:]) for c in range(FC))
            turn_weights((bank(4)[:, 128 * c:128 * c + 128], lb_raw[:, c, :], ident[:]) for c in range(FC))
            turn_weights(((bank(5)[:, 0:128], la_raw[:], ident[:]), (bank(5)[:, 128:128 + E], gw_raw[:], ident[0:E, 0:E])))

        def setup_tensor_2(pe):
            pe.wait_ge(s_const, 1)
            pe.wait_ge(s_wcopy, 3)
            pe.wait_ge(s_dconst, 3)
            nc.tensor.matmul(bank(6)[:, 0:128], bv_wide[:], x_wT[:, 3, :], start=True, stop=False)
            nc.tensor.matmul(bank(6)[:, 0:128], ones[0:1, :], bo_row[:], start=False, stop=True)
            for c in range(FC):
                nc.tensor.matmul(bank(6)[:, 128:256], bi_wide[:, c, :], woT[:, c, :], start=(c == 0), stop=False)
            nc.tensor.matmul(bank(6)[:, 128:256], twos[:], fbo_row[:], start=False, stop=True).then_inc(s_wT, 1)

        def setup_scalar_0(act):
            act.wait_ge(s_wT, 1)
            nc.scalar.copy(x_wT[:].rearrange("p i d -> p (i d)"), bank(6)).then_inc(s_wcopy, 1)

        def setup_scalar_1(act):
            act.wait_ge(s_wT, 2)
            nc.scalar.copy(wi_s[:, HIGH, :], bank(7)).then_inc(s_wcopy, 1)
            act.wait_ge(s_wT, 3)
            nc.scalar.copy(woT[:].rearrange("p i d -> p (i d)"), bank(6)).then_inc(s_wcopy, 1)
            act.wait_ge(s_wT, 4)
            nc.scalar.copy(lb_s[:, HIGH, :], bank(4)).then_inc(s_wcopy, 1)
            act.wait_ge(s_wT, 5)
            nc.scalar.copy(laT[:], bank(5)[:, 0:128])
            nc.scalar.copy(gwT[:], bank(5)[:, 128:128 + E]).then_inc(s_wcopy, 1)

        def setup_scalar_2(act):
            act.wait_ge(s_wT, 6)
            nc.scalar.copy(x_bias[:], bank(6)[:, 0:128])
            nc.scalar.copy(f_bias[:], bank(6)[:, 128:256]).then_inc(s_wcopy, 1)

        def setup_vector(dve):
            dve.wait_ge(s_const, 1)
            dve.wait_ge(s_gw, GW)
            nc.vector.tensor_scalar(g_wo_sb[:], g_wo_raw[:], g_norm_col[:], float(GK) ** 0.5, ALU.mult,
                                    ALU.mult).then_inc(s_dconst, 1)
            dve.wait_ge(s_xw, XW)
            nc.vector.tensor_reduce(k_mask[:], in_head[:].rearrange("p (i j) -> p j i", j=XG), AX.X, ALU.add)
            nc.vector.tensor_scalar(half_mask[:], amask_sb[:], 0.5, None, ALU.mult)
            nc.vector.tensor_scalar(bq_col[:], bq_raw[:], 0.5 * float(XD) ** -0.5, None, ALU.mult)
            nc.vector.tensor_scalar(bv_wide[:], ones[:], bv_col[:], None, ALU.mult).then_inc(s_dconst, 1)
            dve.wait_ge(s_fw, FW)
            nc.vector.tensor_scalar(neg_bi[:], bi_col[:], -1.0, None, ALU.mult)
            for c in range(FC):
                last = nc.vector.tensor_scalar(bi_wide[:, c, :], ones[:], bi_col[:, c:c + 1], None, ALU.mult)
            last.then_inc(s_dconst, 1)
            dve.wait_ge(s_wcopy, 2)
            nc.vector.tensor_tensor(wi_s[:, LOW, :], bank(7), wi_s[:, HIGH, :], ALU.subtract).then_inc(s_dconst, 1)
            dve.wait_ge(s_wcopy, 4)
            nc.vector.tensor_tensor(lb_s[:, LOW, :], bank(4), lb_s[:, HIGH, :], ALU.subtract).then_inc(s_dconst, 1)

        xn = carve([128, 2, 128])
        xT = carve([128, 2, 2, 128])
        qkT = carve([128, 2, 2, 2, 128])
        qbd = carve([128, 2, 2, GH, 128])
        Ep = carve([128, 2, 2, 256])
        Em = carve([128, 2, 256])
        sp_ = carve([128, 2, 2, 256])
        spT = carve([128, 2, 2, 2, 128])
        vS = carve([128, 2, 2, 128])
        Am = carve([128, 2 * GH, 128])
        lg = carve([128, 2 * GH, GM])
        mx = carve([128, 2 * GH])
        rs = carve([128, 2, 2 * GH])
        pp = carve([128, 2, 256])
        ppbd = carve([128, 2, 2, 2, 2, 128])
        Bm = carve([128, 2 * GH, 128])
        un = carve([128, 2, 256])
        sq = carve([128, 256])
        ss = carve([128, 2 * GH])
        rt = carve([128, 2 * GH])
        rr = carve([128, 2 * GH])
        on = carve([128, 2 * GH, GK])
        onT = carve([128, 2, 128])
        late = at[0]
        wk = carve([128, 2, 512])
        LS = carve([128, 2, 512])
        sg = carve([128, 2, 256])
        dec = carve([128, 2, 256])
        qk = carve([128, 2, 256])

        G = {n: sem("g_" + n) for n in (
            "stats", "aggr", "vareps", "rstd", "xn", "xTp", "xT", "z", "abs", "exp1", "ln", "ls", "sig", "dec",
            "silu", "qkTp", "qkT", "qbd", "csum", "eminus", "s", "sTp", "sT", "a", "am", "l", "vp", "v",
            "lgts", "mx", "shift", "p", "sum", "pp", "ppTp", "ppT", "b", "bm", "o", "un", "sq", "ss", "rt", "rt2", "r",
            "on", "onTp", "onT", "y", "x1")}

        def bc(ap, n):
            return ap[:, None, :].broadcast_to([128, n, ap.shape[1]])

        def inner(ap, n):
            return ap[:, :, None].broadcast_to([128, ap.shape[1], n])

        def gsa_tensor(pe, t, par, gate, turn, intra, mix, finish, ahead):
            def x_turned():
                need(pe, G["xn"], t + 1)
                need(pe, G["sT"], t - 1)
                need(pe, G["onT"], t - 3)
                for b in range(2):
                    last = nc.tensor.transpose(bank(2)[:, 128 * b:128 * b + 128], xn[:, b, :], ident[:])
                last.then_inc(G["xTp"], 1)

            def queries_keys_gates():
                need(pe, G["xT"], t + 1)
                need(pe, G["silu"], t)
                for b in range(2):
                    last = nc.tensor.matmul(bank(b), xT[:, par, b, :], g_wqkf[:], start=True, stop=True)
                last.then_inc(G["z"], 1)

            def decay_sums():
                p = t - 1
                need(pe, G["ls"], p + 1)
                need(pe, G["x1"], t - 4)
                need(pe, G["v"], p)
                nc.tensor.matmul(bank(3), tri_centred[:], LS[:, :, 256:512], start=True, stop=True).then_inc(G["csum"], 1)

            def values():
                p, q = t - 1, 1 - par
                need(pe, G["eminus"], p + 1)
                for b in range(2):
                    last = nc.tensor.matmul(bank(3)[:, 128 * b:128 * b + 128], xT[:, q, b, :], g_wv_sb[:], start=True, stop=True)
                last.then_inc(G["vp"], 1)

            def qk_turned():
                p = t - 1
                need(pe, G["silu"], p + 1)
                need(pe, G["xT"], upto(t + 1, PAIRS))
                need(pe, G["onT"], t - 3)
                for w in range(2):
                    for b in range(2):
                        i = 2 * w + b
                        last = nc.tensor.transpose(bank(2)[:, 128 * i:128 * i + 128], qk[:, b, 128 * w:128 * w + 128], ident[:])
                last.then_inc(G["qkTp"], 1)

            def s_turned():
                p, q = t - 1, 1 - par
                need(pe, G["s"], p + 1)
                need(pe, G["qkT"], p + 1)
                for b in range(2):
                    for c in range(2):
                        i = 2 * b + c
                        last = nc.tensor.transpose(bank(2)[:, 128 * i:128 * i + 128], sp_[:, q, b, 128 * c:128 * c + 128], ident[:])
                last.then_inc(G["sTp"], 1)

            def attention():
                p, q = t - 2, par
                need(pe, G["qbd"], p + 1)
                need(pe, G["lgts"], p)
                for b in range(2):
                    last = nc.tensor.matmul(bank(4 + b), qkT[:, q, 1, b, :], qbd[:, q, b, :, :].rearrange("p h t -> p (h t)"),
                                            start=True, stop=True)
                last.then_inc(G["a"], 1)

            def slot_logits():
                p, q = t - 2, par
                need(pe, G["am"], p + 1)
                for b in range(2):
                    for h in range(GH):
                        last = nc.tensor.matmul(bank(4)[:, 256 * b + GM * h:256 * b + GM * h + GM], Am[:, GH * b + h, :],
                                                sp_[:, q, b, GM * h:GM * h + GM], start=True, stop=True)
                last.then_inc(G["l"], 1)

            def weights_turned():
                p = t - 2
                need(pe, G["pp"], p + 1)
                need(pe, G["bm"], p)
                for b in range(2):
                    for c in range(2):
                        i = 2 * b + c
                        last = nc.tensor.transpose(bank(7)[:, 128 * i:128 * i + 128], pp[:, b, 128 * c:128 * c + 128], ident[:])
                last.then_inc(G["ppTp"], 1)

            def slot_mix():
                p, q = t - 3, 1 - par
                need(pe, G["ppT"], 2 * (p + 1))
                need(pe, G["sT"], p + 1)
                need(pe, G["un"], p)
                for b in range(2):
                    for c in range(2):
                        last = nc.tensor.matmul(bank(6 + b)[:, 256 * c:256 * c + 256], spT[:, q, b, c, :],
                                                ppbd[:, q, b, c, :, :].rearrange("p h t -> p (h t)"), start=True, stop=True)
                last.then_inc(G["b"], 1)

            def outputs():
                p, q = t - 3, 1 - par
                need(pe, G["bm"], p + 1)
                need(pe, G["v"], p + 1)
                for b in range(2):
                    for h in range(GH):
                        last = nc.tensor.matmul(bank(6)[:, 128 * b + GK * h:128 * b + GK * h + GK], Bm[:, GH * b + h, :],
                                                vS[:, q, b, GK * h:GK * h + GK], start=True, stop=True)
                last.then_inc(G["o"], 1)

            def outputs_turned():
                need(pe, G["on"], t - 3)
                need(pe, G["sT"], upto(t - 1, PAIRS))
                for b in range(2):
                    last = nc.tensor.transpose(bank(2)[:, 128 * b:128 * b + 128],
                                               on[:, GH * b:GH * b + GH, :].rearrange("p h v -> p (h v)"), ident[:])
                last.then_inc(G["onTp"], 1)

            def project_out():
                need(pe, G["onT"], t - 3)
                need(pe, G["v"], upto(t, PAIRS))
                for b in range(2):
                    last = nc.tensor.matmul(bank(3)[:, 128 * b:128 * b + 128], onT[:, b, :], g_wo_sb[:], start=True, stop=True)
                last.then_inc(G["y"], 1)

            if intra:
                attention()
            if mix:
                slot_mix()
            if finish:
                outputs_turned()
            if turn:
                decay_sums()
            if gate:
                x_turned()
            if intra:
                slot_logits()
            if turn:
                qk_turned()
            if gate:
                queries_keys_gates()
            if mix:
                outputs()
            if turn:
                values()
                s_turned()
            if finish:
                project_out()
            if intra:
                weights_turned()

        def gsa_scalar(act, t, par, gate, turn, intra, mix, finish, ahead):
            def x_turned():
                need(act, G["xTp"], t + 1)
                need(act, G["vp"], t - 1)
                nc.scalar.copy(xT[:, par, :, :], bank(2)[:, 0:256].rearrange("p (b t) -> p b t", b=2)).then_inc(G["xT"], 1)

            def absolutes():
                need(act, G["z"], t + 1)
                need(act, G["ls"], t)
                nc.scalar.activation(wk[:], banks[:, 0:2, :], ACT.Abs).then_inc(G["abs"], 1)

            def exps():
                need(act, G["abs"], t + 1)
                nc.scalar.activation(wk[:], wk[:], ACT.Exp, scale=-1.0).then_inc(G["exp1"], 1)

            def logs():
                need(act, G["exp1"], t + 1)
                nc.scalar.activation(wk[:], wk[:], ACT.Ln, bias=1.0).then_inc(G["ln"], 1)

            def sigmoids():
                p = t - 1
                need(act, G["ls"], p + 1)
                need(act, G["silu"], p)
                nc.scalar.activation(sg[:], LS[:, :, 0:256], ACT.Exp).then_inc(G["sig"], 1)

            def decays():
                p = t - 1
                need(act, G["ls"], p + 1)
                need(act, G["s"], p)
                nc.scalar.activation(dec[:], LS[:, :, 256:512], ACT.Exp, scale=1.0 / GATE_DIV).then_inc(G["dec"], 1)

            def decay_exps():
                p, q = t - 1, 1 - par
                need(act, G["csum"], p + 1)
                need(act, G["s"], p)
                need(act, G["pp"], p - 1)
                csum = bank(3).rearrange("p (b m) -> p b m", b=2)
                nc.scalar.activation(Em[:], csum, ACT.Exp, scale=-1.0)
                nc.scalar.activation(Ep[:, q, :, :], csum, ACT.Exp).then_inc(G["eminus"], 1)

            def values():
                p, q = t - 1, 1 - par
                need(act, G["vp"], p + 1)
                need(act, G["o"], p - 1)
                nc.scalar.copy(vS[:, q, :, :], bank(3)[:, 0:256].rearrange("p (b v) -> p b v", b=2)).then_inc(G["v"], 1)

            def qk_turned():
                p, q = t - 1, 1 - par
                need(act, G["qkTp"], p + 1)
                need(act, G["a"], p - 1)
                nc.scalar.copy(qkT[:, q, :, :, :].rearrange("p w b t -> p (w b t)"), bank(2)).then_inc(G["qkT"], 1)

            def s_turned():
                p, q = t - 1, 1 - par
                need(act, G["sTp"], p + 1)
                need(act, G["b"], p - 1)
                nc.scalar.copy(spT[:, q, :, :, :].rearrange("p b c t -> p (b c t)"), bank(2)).then_inc(G["sT"], 1)

            def slot_exps():
                need(act, G["shift"], t - 1)
                nc.scalar.activation(lg[:], lg[:], ACT.Exp).then_inc(G["p"], 1)

            def weights_turned():
                p, q = t - 2, par
                need(act, G["ppTp"], p + 1)
                need(act, G["b"], p - 1)
                src = bank(7).rearrange("p (b c t) -> p b c t", b=2, c=2)
                for half in range(2):
                    rows = slice(64 * half, 64 * half + 64)
                    nc.scalar.copy(ppbd[rows, q, :, :, half, :], src[rows, :, :, :]).then_inc(G["ppT"], 1)

            def outputs():
                p, q = t - 3, 1 - par
                need(act, G["o"], p + 1)
                need(act, G["on"], p - 1)
                nc.scalar.copy(un[:, q, :], bank(6)[:, 0:256]).then_inc(G["un"], 1)

            def outputs_turned():
                p = t - 4
                need(act, G["onTp"], p + 1)
                need(act, G["y"], p)
                nc.scalar.copy(onT[:].rearrange("p b t -> p (b t)"), bank(2)[:, 0:256]).then_inc(G["onT"], 1)

            if turn:
                sigmoids()
            if finish:
                outputs_turned()
            if gate:
                x_turned()
            if turn:
                decays()
                decay_exps()
                qk_turned()
            if gate:
                absolutes()
            if intra:
                slot_exps()
            if gate:
                exps()
            if turn:
                values()
            if mix:
                outputs()
            if gate:
                logs()
            if intra:
                weights_turned()
            if turn:
                s_turned()

        def gsa_stats(dve, p):
            need(dve, G["xn"], p)
            need(dve, G["aggr"], 2 * p)
            for b in range(2):
                nc.vector.bn_stats(stats[:, b, :], X[:, 2 * p + b, :]).then_inc(G["stats"], 1)
            need(dve, G["vareps"], p)
            hold(dve, G["stats"], 2 * p + 2, s_passed)
            for b in range(2):
                nc.vector.bn_aggr(meanvar[:, b, :], stats[:, b, :]).then_inc(G["aggr"], 1)

        def gsa_normalise(dve, p):
            need(dve, G["rstd"], p + 1)
            need(dve, G["xTp"], p)
            for b in range(2):
                last = nc.vector.tensor_scalar(xn[:, b, :], X[:, 2 * p + b, :], meanvar[:, b, 0:1], rstd[:, b:b + 1],
                                               ALU.subtract, ALU.mult)
            last.then_inc(G["xn"], 1)

        def gsa_vector(dve, t, par, gate, turn, intra, mix, finish, ahead):
            def log_sigmoid():
                p = t
                need(dve, G["ln"], p + 1)
                need(dve, G["csum"], p)
                need(dve, G["dec"], p)
                nc.vector.scalar_tensor_tensor(LS[:].rearrange("p b n -> p (b n)"),
                                               banks[:, 0:2, :].rearrange("p b n -> p (b n)"), 0.0,
                                               wk[:].rearrange("p b n -> p (b n)"), ALU.min, ALU.subtract).then_inc(G["ls"], 1)

            def silu():
                p = t - 1
                need(dve, G["sig"], p + 1)
                need(dve, G["qkTp"], p)
                nc.vector.tensor_tensor(qk[:], banks[:, 0:2, 0:256], sg[:], ALU.mult).then_inc(G["silu"], 1)

            def slots():
                p, q = t - 1, 1 - par
                need(dve, G["eminus"], p + 1)
                need(dve, G["dec"], p + 1)
                need(dve, G["l"], p - 1)
                nc.vector.scalar_tensor_tensor(sp_[:, q, :, :].rearrange("p b m -> p (b m)"),
                                               dec[:].rearrange("p b m -> p (b m)"), 1.0, Em[:].rearrange("p b m -> p (b m)"),
                                               ALU.subtract, ALU.mult).then_inc(G["s"], 1)

            def causal_attention():
                p = t - 2
                need(dve, G["a"], p + 1)
                need(dve, G["l"], p)
                nc.vector.tensor_tensor(Am[:], banks[:, 4:6, :].rearrange("p a (h t) -> p (a h) t", t=128),
                                        bc(mask_a[:], 2 * GH), ALU.mult).then_inc(G["am"], 1)

            def slot_logits():
                p, q = t - 2, par
                need(dve, G["l"], p + 1)
                need(dve, G["pp"], p)
                nc.vector.tensor_tensor(lg[:], bank(4).rearrange("p (h m) -> p h m", m=GM),
                                        Ep[:, q, :, :].rearrange("p b (h m) -> p (b h) m", m=GM), ALU.mult).then_inc(G["lgts"], 1)

            def slot_maxima():
                p = t - 2
                need(dve, G["lgts"], p + 1)
                nc.vector.tensor_reduce(mx[:], lg[:], AX.X, ALU.max).then_inc(G["mx"], 1)
                need(dve, G["mx"], p + 1)
                nc.vector.tensor_tensor(lg[:], lg[:], inner(mx[:], GM), ALU.subtract).then_inc(G["shift"], 1)

            def slot_sums():
                p, q = t - 2, par
                need(dve, G["p"], p + 1)
                nc.vector.tensor_reduce(rs[:, q, :], lg[:], AX.X, ALU.add).then_inc(G["sum"], 1)

            def causal_mix():
                p = t - 3
                need(dve, G["b"], p + 1)
                need(dve, G["o"], p)
                nc.vector.tensor_tensor(Bm[:], banks[:, 6:8, :].rearrange("p a (h t) -> p (a h) t", t=128),
                                        bc(mask_b[:], 2 * GH), ALU.mult).then_inc(G["bm"], 1)

            def mean_squares():
                p, q = t - 3, 1 - par
                need(dve, G["r"], p)
                need(dve, G["sum"], p + 1)
                nc.vector.scalar_tensor_tensor(rt[:], rs[:, q, :], GK * EPS, rs[:, q, :], ALU.mult, ALU.mult).then_inc(G["rt"], 1)
                need(dve, G["sq"], p + 1)
                nc.vector.tensor_reduce(ss[:], sq[:].rearrange("p (h v) -> p h v", v=GK), AX.X, ALU.add).then_inc(G["ss"], 1)
                need(dve, G["ss"], p + 1)
                need(dve, G["rt"], p + 1)
                nc.vector.tensor_tensor(rt[:], rt[:], ss[:], ALU.add).then_inc(G["rt2"], 1)

            def outputs_normalised():
                p, q = t - 4, par
                need(dve, G["r"], p + 1)
                need(dve, G["onTp"], p)
                nc.vector.tensor_tensor(on[:], un[:, q, :].rearrange("p (h v) -> p h v", v=GK), inner(rr[:], GK),
                                        ALU.mult).then_inc(G["on"], 1)

            def add_to_stream():
                p = t - 4
                need(dve, G["y"], p + 1)
                x1 = X[:, bass.ds(2 * p, 2), :]
                nc.vector.tensor_tensor(x1, bank(3)[:, 0:256].rearrange("p (b d) -> p b d", b=2), x1, ALU.add).then_inc(G["x1"], 1)

            def statistics():
                gsa_stats(dve, t + 1)

            def normalise():
                gsa_normalise(dve, t + 1)

            if finish:
                outputs_normalised()
            if intra:
                causal_attention()
            if turn:
                silu()
            if mix:
                causal_mix()
            if ahead:
                statistics()
            if intra:
                slot_logits()
                slot_maxima()
            if turn:
                slots()
            if intra:
                slot_sums()
            if ahead:
                normalise()
            if mix:
                mean_squares()
            if finish:
                add_to_stream()
            if gate:
                log_sigmoid()

        def gsa_rstd(pool, p):
            need(pool, G["aggr"], 2 * (p + 1))
            need(pool, G["rstd"], p)
            nc.gpsimd.tensor_tensor(vareps[:, 0:2], meanvar[:, 0:2, 1], eps_tile[:, 0:2], ALU.add).then_inc(G["vareps"], 1)
            need(pool, G["vareps"], p + 1)
            need(pool, G["xn"], p)
            nc.gpsimd.tensor_tensor(rstd[:, 0:2], vareps[:, 0:2], minus_half[:, 0:2], ALU.pow).then_inc(G["rstd"], 1)

        def gsa_pool(pool, t, par, gate, turn, intra, mix, finish, ahead):
            def heads_apart():
                p, q = t - 1, 1 - par
                need(pool, G["qkT"], p + 1)
                need(pool, G["a"], p - 1)
                for b in range(2):
                    last = nc.gpsimd.tensor_tensor(qbd[:, q, b, :, :], bc(qkT[:, q, 0, b, :], GH), inner(head_mask[:], 128), ALU.mult)
                last.then_inc(G["qbd"], 1)

            def squares():
                p, q = t - 3, 1 - par
                need(pool, G["un"], p + 1)
                need(pool, G["ss"], p)
                nc.gpsimd.tensor_tensor(sq[:], un[:, q, :], un[:, q, :], ALU.mult).then_inc(G["sq"], 1)

            def root():
                p = t - 3
                need(pool, G["rt2"], p + 1)
                need(pool, G["on"], p)
                nc.gpsimd.tensor_tensor(rr[:], rt[:], minus_half[:, 0:2 * GH], ALU.pow).then_inc(G["r"], 1)

            def slot_weights():
                p, q = t - 2, par
                need(pool, G["p"], p + 1)
                need(pool, G["ppTp"], p)
                nc.gpsimd.tensor_tensor(pp[:].rearrange("p b m -> p (b m)"), lg[:].rearrange("p h m -> p (h m)"),
                                        Ep[:, q, :, :].rearrange("p b m -> p (b m)"), ALU.mult).then_inc(G["pp"], 1)

            def roots_ahead():
                gsa_rstd(pool, t + 1)

            if ahead:
                roots_ahead()
            if turn:
                heads_apart()
            if intra:
                slot_weights()
            if mix:
                squares()
                root()

        def gsa_peeled(tick, t):
            tick(t, t % 2, *(0 <= t - k < PAIRS for k in (0, 1, 2, 3, 4, -1)))

        def gsa_loop(engine, tick):
            with engine.Fori(6, PAIRS - 2, 2) as t:
                tick(t, 0, True, True, True, True, True, True)
                tick(t + 1, 1, True, True, True, True, True, True)

        ctxb = sb("c_ctx", [128, 2, 128])
        fs = sb("c_fside", [128, 2, XH, 128])
        fm = sb("c_bias", [128, 2, XH, 128])
        cm = sb("c_cm", [128, 128])
        xn2 = sb("c_xn", [128, 128])
        cT = sb("c_cT", [128, 2, 128])
        qx = sb("c_q", [128, 2, 128])
        kx = sb("c_k", [128, 128])
        VPAD = XG * (32 + XD)
        vp = sb("c_vpad", [128, 2, NI * VPAD])
        mn = sb("c_min", [128, 2, XH])
        rsx = sb("c_sum", [128, 2, XH])
        rc = sb("c_recip", [128, XH])

        at[0] = late
        kbd = carve([128, 2, XG, 128])
        PTs = carve([128, NI, 512])
        xT2 = carve([128, 128])
        rx = carve([128, XH, XD])
        RT = carve([128, 128])
        oTs = carve([128, 128])

        C = {n: sem("c_" + n) for n in (
            "stats", "aggr", "vareps", "rstd", "xn", "xbias", "Tp", "T", "qkp", "q", "k", "kbd", "cm", "fm", 
            "sc", "tt", "ex", "rc", "rx", "Rp", "RT", "pt", "ptD", "ptA", "pv", "oT", "yv", "v", "x2")}
        s_ctx = [sem(f"c_ctx_loaded{i}") for i in range(2)]
        s_fs = [sem(f"c_fside_loaded{i}") for i in range(2)]

        SCORE_BANKS = (1, 4, 5, 6)

        def x_tensor(pe, m, q, norm, project, scores, attend, finish):
            n = 2 * m + q
            o = 1 - q

            def score(i):
                need(pe, C["q"], n + 2)
                need(pe, C["kbd"], n + 2)
                need(pe, C["tt"], 4 * n + i + 1)
                rows = slice(32 * i, 32 * i + 32)
                nc.tensor.matmul(bank(SCORE_BANKS[i]), qx[rows, o, :], kbd[rows, o, :, :].rearrange("p j s -> p (j s)"),
                                 start=True, stop=True).then_inc(C["sc"], 1)

            def inputs_turned():
                need(pe, C["xn"], n + 3)
                need(pe, s_ctx[q], 16 * (m + 2))
                need(pe, C["RT"], n)
                need(pe, C["k"], n + 2)
                nc.tensor.transpose(bank(0)[:, 0:128], xn2[:], ident[:])
                nc.tensor.transpose(bank(0)[:, 128:256], ctxb[:, q, :], ident[:]).then_inc(C["Tp"], 1)

            def queries_keys():
                need(pe, C["T"], n + 3)
                nc.tensor.matmul(bank(0)[:, 0:128], x_wT[:, 0, :], xT2[:], start=True, stop=True)
                nc.tensor.matmul(bank(0)[:, 128:256], x_wT[:, 1, :], cT[:, q, :], start=True, stop=True).then_inc(C["qkp"], 1)

            def outputs_values():
                if project:
                    need(pe, C["k"], n + 3)
                else:
                    need(pe, C["RT"], n)
                if finish:
                    need(pe, C["oT"], n)
                    last = nc.tensor.matmul(bank(0)[:, 0:128], oTs[:], x_wT[:, 3, :], start=True, stop=True)
                if scores:
                    last = nc.tensor.matmul(bank(0)[:, 128:256], cT[:, o, :], x_wT[:, 2, :], start=True, stop=True)
                last.then_inc(C["yv"], 1)

            def reciprocals_turned():
                need(pe, C["rx"], n + 1)
                need(pe, C["x2"], n)
                if scores:
                    need(pe, C["v"], n + 2)
                nc.tensor.transpose(bank(0)[:, 0:128], rx[:].rearrange("p h d -> p (h d)"), ident[:]).then_inc(C["Rp"], 1)

            def weights_turned(i):
                need(pe, C["ex"], 4 * n + i + 1)
                if i == 1:
                    need(pe, C["ptA"], n)
                else:
                    need(pe, C["ptD"], 3 * n + max(0, i - 1))
                for j in range(XG):
                    last = nc.tensor.transpose(bank(2 + i % 2)[:, 128 * j:128 * j + 128], P[:, q, XG * i + j, :], ident[:])
                last.then_inc(C["pt"], 1)

            def mix(i, par):
                for j in range(XG):
                    last = nc.tensor.matmul(bank(7)[32 * i:32 * i + 32, 0:128],
                                            vp[:, par, VPAD * i + 32 * j:VPAD * i + 32 * j + 32],
                                            PTs[:, i, 128 * j:128 * j + 128], start=(j == 0), stop=(j == XG - 1))
                last.then_inc(C["pv"], 1)

            def mix_last():
                need(pe, C["ptA"], n)
                mix(NI - 1, o)

            def mix_values(i):
                need(pe, C["ptD"], 3 * n + i + 1)
                if i == 0:
                    need(pe, C["oT"], n)
                    need(pe, C["v"], n + 1)
                mix(i, q)

            if attend:
                weights_turned(0)
            if scores:
                score(0)
            if finish:
                mix_last()
            if project:
                inputs_turned()
            if scores:
                score(1)
            if attend:
                weights_turned(1)
            if project:
                queries_keys()
            if attend:
                mix_values(0)
            if scores:
                score(2)
            if scores or finish:
                outputs_values()
            if attend:
                weights_turned(2)
            if scores:
                score(3)
            if attend:
                mix_values(1)
                reciprocals_turned()
                weights_turned(3)
                mix_values(2)

        def x_scalar(act, m, q, norm, project, scores, attend, finish):
            n = 2 * m + q
            o = 1 - q

            def exps(batch, par, i):
                need(act, C["tt"], 4 * batch + i + 1)
                for h in range(XG * i, XG * i + XG):
                    last = nc.scalar.activation(P[:, par, h, :], P[:, par, h, :], ACT.Exp, bias=mn[:, par, h:h + 1], scale=-1.0,
                                                accum_out=rsx[:, par, h:h + 1])
                last.then_inc(C["ex"], 1)

            def inputs_turned():
                need(act, C["Tp"], n + 3)
                need(act, C["yv"], n + 1)
                nc.scalar.copy(xT2[:], bank(0)[:, 0:128])
                nc.scalar.copy(cT[:, q, :], bank(0)[:, 128:256]).then_inc(C["T"], 1)

            def queries_keys():
                need(act, C["qkp"], n + 3)
                need(act, C["sc"], 4 * n + 4)
                nc.scalar.activation(qx[:, q, :], bank(0)[:, 0:128], ACT.Identity, bias=bq_col[:],
                                     scale=0.5 * float(XD) ** -0.5).then_inc(C["q"], 1)
                need(act, C["kbd"], n + 2)
                nc.scalar.activation(kx[:], bank(0)[:, 128:256], ACT.Identity, bias=bk_col[:]).then_inc(C["k"], 1)

            def reciprocals_turned():
                need(act, C["Rp"], n + 1)
                need(act, C["oT"], n)
                nc.scalar.copy(RT[:], bank(0)[:, 0:128]).then_inc(C["RT"], 1)

            def weights_turned():
                need(act, C["pt"], 4 * n + 4)
                need(act, C["pv"], 4 * n)
                nc.scalar.copy(PTs[:, 3, :], bank(3)).then_inc(C["ptA"], 1)

            if attend:
                exps(n, q, 3)
            if project:
                inputs_turned()
            if scores:
                exps(n + 1, o, 0)
            if project:
                queries_keys()
            if scores:
                exps(n + 1, o, 1)
                exps(n + 1, o, 2)
            if attend:
                weights_turned()
                reciprocals_turned()

        def x_row(m, q, k):
            n = 2 * m + q + k
            return X[:, n, :] if isinstance(n, int) else X[:, bass.ds(n, 1), :].rearrange("p a d -> p (a d)")

        def x_vector(dve, m, q, norm, project, scores, attend, finish):
            n = 2 * m + q
            o = 1 - q

            def score(i):
                need(dve, C["fm"], n + 2)
                need(dve, C["pt"], 4 * n - 3 + i)
                hold(dve, C["sc"], 4 * n + i + 5, s_passed)
                for j in range(XG):
                    h = XG * i + j
                    last = nc.vector.tensor_tensor_reduce(out=P[:, o, h, :], in0=bank(SCORE_BANKS[i])[:, 128 * j:128 * j + 128],
                                                          in1=fm[:, o, h, :], scale=-2.0, scalar=3.0e38, op0=ALU.add,
                                                          op1=ALU.min, accum_out=mn[:, o, h:h + 1])
                last.then_inc(C["tt"], 1)

            def statistics():
                need(dve, C["xn"], n + 3)
                need(dve, C["aggr"], n + 3)
                nc.vector.bn_stats(stats[:, 0, :], x_row(m, q, 3)).then_inc(C["stats"], 1)

            def aggregates():
                need(dve, C["vareps"], n + 3)
                hold(dve, C["stats"], n + 4, s_passed)
                nc.vector.bn_aggr(meanvar[:, 0, :], stats[:, 0, :]).then_inc(C["aggr"], 1)

            def normalise():
                need(dve, C["rstd"], n + 4)
                need(dve, C["Tp"], n + 3)
                nc.vector.tensor_scalar(xn2[:], x_row(m, q, 3), meanvar[:, 0, 0:1], rstd[:, 0:1],
                                        ALU.subtract, ALU.mult).then_inc(C["xn"], 1)

            def masks():
                need(dve, C["fm"], n + 2)
                km = kmask_sb[:, bass.ds((n + 2) * T, T)]
                nc.vector.scalar_tensor_tensor(cm[:], km, -3.0e38, half_mask[:], ALU.mult, ALU.add).then_inc(C["cm"], 1)

            def outputs():
                need(dve, C["pv"], 4 * n)
                need(dve, C["RT"], n)
                need(dve, C["yv"], n + 1)
                nc.vector.tensor_tensor(oTs[:], bank(7)[:, 0:128], RT[:], ALU.mult).then_inc(C["oT"], 1)

            def weights_turned(i):
                need(dve, C["pt"], 4 * n + i + 1)
                need(dve, C["pv"], 4 * n - 3 + i)
                nc.vector.tensor_copy(PTs[:, i, :], bank(2 + i % 2)).then_inc(C["ptD"], 1)

            def reciprocals():
                need(dve, C["ex"], 4 * n + 4)
                nc.vector.reciprocal(rc[:], rsx[:, q, :]).then_inc(C["rc"], 1)

            def reciprocals_spread():
                need(dve, C["rc"], n + 1)
                need(dve, C["Rp"], n)
                nc.vector.tensor_copy(rx[:], inner(rc[:], XD)).then_inc(C["rx"], 1)

            def add_to_stream():
                need(dve, C["yv"], n + 2)
                need(dve, C["xbias"], n)
                nc.vector.tensor_tensor(x_row(m, q, -1), bank(0)[:, 0:128], x_row(m, q, -1), ALU.add).then_inc(C["x2"], 1)

            def values():
                need(dve, C["yv"], n + 2)
                need(dve, C["pv"], 4 * n)
                dst = vp[:, o, :].rearrange("p (i j w) -> p i j w", i=NI, j=XG)[:, :, :, 0:XD]
                nc.vector.tensor_copy(dst, bank(0)[:, 128:256].rearrange("p (i j d) -> p i j d", i=NI, j=XG)).then_inc(C["v"], 1)

            if project:
                masks()
            if attend:
                weights_turned(0)
            if scores:
                score(0)
            if finish:
                outputs()
            if norm:
                statistics()
            if scores:
                score(1)
            if attend:
                weights_turned(1)
                reciprocals()
                reciprocals_spread()
            if norm:
                aggregates()
            if scores:
                score(2)
                values()
            if finish:
                add_to_stream()
            if attend:
                weights_turned(2)
            if norm:
                normalise()
            if scores:
                score(3)

        def x_pool(pool, m, q, norm, project, scores, attend, finish):
            n = 2 * m + q

            def output_bias():
                need(pool, C["xn"], n + 3)
                nc.gpsimd.tensor_tensor(x_row(m, q, 2), x_row(m, q, 2), x_bias[:], ALU.add).then_inc(C["xbias"], 1)

            def roots():
                need(pool, C["aggr"], n + 4)
                need(pool, C["rstd"], n + 3)
                nc.gpsimd.tensor_tensor(vareps[:, 0:1], meanvar[:, 0, 1:2], eps_tile[:, 0:1], ALU.add).then_inc(C["vareps"], 1)
                need(pool, C["vareps"], n + 4)
                need(pool, C["xn"], n + 3)
                nc.gpsimd.tensor_tensor(rstd[:, 0:1], vareps[:, 0:1], minus_half[:, 0:1], ALU.pow).then_inc(C["rstd"], 1)

            def biases():
                need(pool, C["cm"], n + 3)
                need(pool, s_fs[q], 32 * (m + 2))
                need(pool, C["tt"], 4 * n + 4)
                nc.gpsimd.tensor_tensor(fm[:, q, :, :], fs[:, q, :, :], bc(cm[:], XH), ALU.add).then_inc(C["fm"], 1)

            def keys_apart():
                need(pool, C["k"], n + 3)
                need(pool, C["sc"], 4 * n + 4)
                nc.gpsimd.tensor_tensor(kbd[:, q, :, :], bc(kx[:], XG), inner(k_mask[:], 128), ALU.mult).then_inc(C["kbd"], 1)

            if project:
                output_bias()
                biases()
            if norm:
                roots()
            if project:
                keys_apart()

        def x_peeled(step, n):
            step(n // 2, n % 2, *(0 <= n + k < B for k in (3, 2, 1, 0, -1)))

        def x_loop(engine, step):
            with engine.Fori(1, B // 2 - 2, 1) as m:
                step(m, 0, True, True, True, True, True)
                step(m, 1, True, True, True, True, True)

        def x_loads(sp):
            def load(m, q):
                n = 2 * m + q
                need(sp, C["Tp"], n - 1)
                sp.dma_start(ctxb[:, q, :], ctx_in[bass.ds(n, 1)].rearrange("o s d -> (o s) d")).then_inc(s_ctx[q], 16)
                need(sp, C["fm"], n - 1)
                bias = fside[bass.ds(n, 1)].rearrange("o h t s -> (o t) h s")
                for half in range(2):
                    rows = slice(64 * half, 64 * half + 64)
                    sp.dma_start(fs[rows, q, :, :], bias[rows, :, :]).then_inc(s_fs[q], 16)
            load(0, 0)
            load(0, 1)
            with sp.Fori(1, B // 2, 1) as m:
                load(m, 0)
                load(m, 1)

        at[0] = 0
        xn3 = carve([128, GROUP, 128])
        xT3 = carve([128, 2, NT])
        uT = carve([128, NT])
        lgt = carve([128, GROUP, E])
        rmx = carve([128, GROUP])
        ex = carve([128, GROUP, E])
        beats = carve([128, GROUP, E, E])
        ties = carve([128, GROUP, E, E])
        rank = carve([128, GROUP * E])
        top = carve([128, GROUP * E])
        den = carve([128, GROUP])
        rden = carve([128, GROUP])
        num = carve([128, GROUP])
        vs = carve([128, 2, GROUP])
        hot = carve([128, 2, GROUP, E * R])
        r1 = carve([128, FC, NT])
        hT = carve([128, FC, NT])

        us = carve([128, 2, NT]).bitcast(fp32r)
        y3 = carve([128, 2, GROUP, 128])
        gated_bias = carve([128, GROUP, 128])
        assert at[0] <= late

        M = {n: sem("f_" + n) for n in (
            "stats", "aggr", "vareps", "rstd", "xn", "Tp", "xT", "lg", "up", "uT", "l0", "mx", "sh", "ex", "fl", "gt", "eq",
            "eq2", "sum", "rank", "top", "et", "num", "den", "rden", "vs", "hot1", "hot", "hp", "um", "i1", "r1", "i2", "h",
            "y", "out", "bias", "added",
            "x_high", "x_low", "u_high", "u_low")}
        s_out = [sem(f"stored{i}") for i in range(2)]

        def f_tensor(pe, m, q, norm, route, expert):
            t = 2 * m + q
            def x_turned():
                need(pe, M["xn"], t + 1)
                need(pe, M["uT"], t)
                for b in range(GROUP):
                    last = nc.tensor.transpose(bank(1)[:, 128 * b:128 * b + 128], xn3[:, b, :], ident[:])
                last.then_inc(M["Tp"], 1)

            def logits():
                need(pe, M["xT"], t + 1)
                need(pe, M["l0"], t)
                for b in range(GROUP):
                    last = nc.tensor.matmul(bank(4)[:, E * b:E * b + E], xT3[:, q, 128 * b:128 * b + 128], gwT[:],
                                            start=True, stop=True)
                last.then_inc(M["lg"], 1)

            def lora_inner():
                need(pe, M["xT"], t + 1)
                nc.tensor.matmul(bank(1), laT[:], xT3[:, q, :], start=True, stop=True).then_inc(M["up"], 1)

            def choices_turned():
                need(pe, M["hot"], t + 1)
                need(pe, M["um"], t)
                for w in range(2):
                    for b in range(GROUP):
                        last = nc.tensor.transpose(bank(5 + w)[:, 128 * b:128 * b + 128], hot[:, w, b, :], ident[:])
                last.then_inc(M["hp"], 1)

            def product(out, weight, moving, start, stop, **also):
                for k, (a, b) in enumerate(PASSES):
                    last = nc.tensor.matmul(out, weight[:, a, :], moving[:, b, :], start=start and k == 0,
                                            stop=stop and k == len(PASSES) - 1, **also)
                return last

            p, o = t - 1, 1 - q

            def first(c):
                need(pe, M["um"], p + 1)
                need(pe, M["x_low"], p + 1)
                need(pe, M["h"], FC * p + c - 1)
                product(bank(2 + c % 2), wi_s[:, :, 128 * c:128 * c + 128], xs[:, o, :, :], True, False)
                product(bank(2 + c % 2), lb_s[:, :, 128 * c:128 * c + 128], um[:, o, 0, :, :], False, True).then_inc(M["i1"], 1)

            def second(c):
                need(pe, M["r1"], FC * p + c + 1)
                product(bank(2 + c % 2), lb_s[:, :, 128 * c:128 * c + 128], um[:, o, 1, :, :], False, True,
                        skip_group_check=True).then_inc(M["i2"], 1)

            def down():
                need(pe, M["h"], FC * p + FC)
                need(pe, M["out"], p)
                for b in range(GROUP):
                    for c in range(FC):
                        last = nc.tensor.matmul(bank(7)[:, 128 * b:128 * b + 128], hT[:, c, 128 * b:128 * b + 128],
                                                woT[:, c, :], start=(c == 0), stop=(c == FC - 1))
                last.then_inc(M["y"], 1)

            if route:
                x_turned()
            if expert:
                first(0)
            if route:
                logits()
            if expert:
                second(0)
                first(1)
            if route:
                lora_inner()
            if expert:
                second(1)
                first(2)
                first(3)
                second(2)
                second(3)
            if route:
                choices_turned()
            if expert:
                down()

        def f_scalar(act, m, q, norm, route, expert):
            t = 2 * m + q
            p = t - 1

            def relu(c):
                need(act, M["i1"], FC * p + c + 1)
                need(act, M["h"], FC * (p - 1) + c + 1)
                nc.scalar.activation(r1[:, c, :], bank(2 + c % 2), ACT.Relu, bias=bi_col[:, c:c + 1]).then_inc(M["r1"], 1)

            def x_turned():
                need(act, M["Tp"], t + 1)
                need(act, M["x_low"], t - 1)
                nc.scalar.copy(xT3[:, q, :], bank(1)).then_inc(M["xT"], 1)

            def x_high():
                need(act, M["xT"], t + 1)
                need(act, M["i1"], FC * (t - 1))
                nc.scalar.copy(xs[:, q, HIGH, :], xT3[:, q, :]).then_inc(M["x_high"], 1)

            def lora_inner():
                need(act, M["up"], t + 1)
                need(act, M["u_low"], t)
                nc.scalar.copy(uT[:], bank(1)).then_inc(M["uT"], 1)
                need(act, M["uT"], t + 1)
                need(act, M["um"], t)
                nc.scalar.copy(us[:, HIGH, :], uT[:]).then_inc(M["u_high"], 1)

            def gate_exps():
                need(act, M["sh"], t + 1)
                need(act, M["den"], t)
                nc.scalar.activation(ex[:], lgt[:], ACT.Exp).then_inc(M["ex"], 1)

            if route:
                x_turned()
            if expert:
                relu(0)
            if route:
                gate_exps()
            if expert:
                relu(1)
            if route:
                lora_inner()
                x_high()
            if expert:
                relu(2)
                relu(3)

        def f_vector(dve, m, q, norm, route, expert):
            t = 2 * m + q
            p, o = t - 1, 1 - q

            def x3(k):
                g = t + k
                return X[:, GROUP * g:GROUP * g + GROUP, :] if isinstance(g, int) else X[:, bass.ds(GROUP * g, GROUP), :]

            def step(ins, name):
                ins.then_inc(M[name], 1)
                need(dve, M[name], t + 1)

            def statistics():
                need(dve, M["aggr"], GROUP * (t + 1))
                src = x3(1)
                for b in range(GROUP):
                    nc.vector.bn_stats(stats[:, b, :], src[:, b, :]).then_inc(M["stats"], 1)
                need(dve, M["vareps"], t + 1)
                hold(dve, M["stats"], GROUP * (t + 2), s_passed)
                for b in range(GROUP):
                    nc.vector.bn_aggr(meanvar[:, b, :], stats[:, b, :]).then_inc(M["aggr"], 1)

            def normalise():
                need(dve, M["rstd"], t + 2)
                need(dve, M["Tp"], t + 1)
                src = x3(1)
                for b in range(GROUP):
                    last = nc.vector.tensor_scalar(xn3[:, b, :], src[:, b, :], meanvar[:, b, 0:1], rstd[:, b:b + 1],
                                                   ALU.subtract, ALU.mult)
                last.then_inc(M["xn"], 1)

            def logits():
                need(dve, M["lg"], t + 1)
                step(nc.vector.tensor_tensor(lgt[:], bank(4)[:, 0:GROUP * E].rearrange("p (b e) -> p b e", e=E),
                                             bc(gb_sb[:], GROUP), ALU.add), "l0")
                step(nc.vector.tensor_reduce(rmx[:], lgt[:], AX.X, ALU.max), "mx")
                step(nc.vector.tensor_tensor(lgt[:], lgt[:], inner(rmx[:], E), ALU.subtract), "sh")

            def ranks():
                need(dve, M["ex"], t + 1)
                step(nc.vector.tensor_scalar(lgt[:], lgt[:], EXP_FLOOR, None, ALU.max), "fl")
                other = lgt[:, :, None, :].broadcast_to([128, GROUP, E, E])
                own = lgt[:, :, :, None].broadcast_to([128, GROUP, E, E])
                nc.vector.tensor_tensor(beats[:], other, own, ALU.is_gt).then_inc(M["gt"], 1)
                step(nc.vector.tensor_tensor(ties[:], other, own, ALU.is_equal), "eq")
                flat = before[:].rearrange("p e j -> p (e j)")[:, None, :].broadcast_to([128, GROUP, E * E])
                tf = ties[:].rearrange("p b e j -> p b (e j)")
                step(nc.vector.tensor_tensor(tf, tf, flat, ALU.mult), "eq2")
                need(dve, M["gt"], t + 1)
                step(nc.vector.tensor_tensor(beats[:], beats[:], ties[:], ALU.add), "sum")
                step(nc.vector.tensor_reduce(rank[:], beats[:].rearrange("p b e j -> p (b e) j"), AX.X, ALU.add), "rank")

            def choices():
                need(dve, M["rank"], t + 1)
                need(dve, M["hp"], t)
                wide = inner(rank[:], R)
                h0 = hot[:, 0, :, :].rearrange("p b (e r) -> p (b e) r", r=R)
                h1 = hot[:, 1, :, :].rearrange("p b (e r) -> p (b e) r", r=R)
                step(nc.vector.tensor_scalar(h0, wide, 0.0, None, ALU.is_equal), "hot1")
                nc.vector.scalar_tensor_tensor(h1, wide, 1.0, h0, ALU.is_equal, ALU.subtract).then_inc(M["hot"], 1)

            def gates():
                step(nc.vector.tensor_scalar(top[:], rank[:], 2.0, None, ALU.is_lt), "top")
                step(nc.vector.tensor_tensor(top[:], top[:], ex[:].rearrange("p b e -> p (b e)"), ALU.mult), "et")
                nc.vector.tensor_reduce(num[:], top[:].rearrange("p (b e) -> p b e", e=E), AX.X, ALU.add).then_inc(M["num"], 1)
                step(nc.vector.tensor_reduce(den[:], ex[:], AX.X, ALU.add), "den")
                step(nc.vector.reciprocal(rden[:], den[:]), "rden")
                need(dve, M["num"], t + 1)
                need(dve, M["out"], t - 1)
                need(dve, M["bias"], t - 1)
                nc.vector.tensor_tensor(vs[:, q, :], num[:], rden[:], ALU.mult).then_inc(M["vs"], 1)

            def chosen_inner():
                need(dve, M["hp"], t + 1)
                need(dve, M["u_low"], t + 1)
                need(dve, M["i2"], FC * (t - 1))
                for w in range(2):
                    for part in (HIGH, LOW):
                        last = nc.vector.tensor_tensor(um[:, q, w, part, :], bank(5 + w), us[:, part, :], ALU.mult)
                last.then_inc(M["um"], 1)

            def hidden(c):
                need(dve, M["i2"], FC * p + c + 1)
                need(dve, M["y"], p)
                nc.vector.scalar_tensor_tensor(hT[:, c, :], bank(2 + c % 2), neg_bi[:, c:c + 1], r1[:, c, :],
                                               ALU.max, ALU.add).then_inc(M["h"], 1)

            def add_to_stream():
                old = x3(-1)
                need(dve, M["y"], p + 1)
                need(dve, M["added"], p + 1)
                need(dve, s_out[o], 16 * (m + q))
                for b in range(GROUP):
                    last = nc.vector.scalar_tensor_tensor(y3[:, o, b, :], bank(7)[:, 128 * b:128 * b + 128], vs[:, o, b:b + 1],
                                                          old[:, b, :], ALU.mult, ALU.add)
                last.then_inc(M["out"], 1)

            if norm:
                statistics()
            if route:
                logits()
            if expert:
                hidden(0)
            if route:
                ranks()
            if expert:
                hidden(1)
            if route:
                choices()
                gates()
            if expert:
                hidden(2)
                hidden(3)
            if norm:
                normalise()
            if route:
                chosen_inner()
            if expert:
                add_to_stream()

        def f_pool(pool, m, q, norm, route, expert):
            t = 2 * m + q

            def roots():
                need(pool, M["aggr"], GROUP * (t + 2))
                need(pool, M["rstd"], t + 1)
                nc.gpsimd.tensor_tensor(vareps[:], meanvar[:, :, 1], eps_tile[:, 0:GROUP], ALU.add).then_inc(M["vareps"], 1)
                need(pool, M["vareps"], t + 2)
                need(pool, M["xn"], t + 1)
                nc.gpsimd.tensor_tensor(rstd[:], vareps[:], minus_half[:, 0:GROUP], ALU.pow).then_inc(M["rstd"], 1)

            def x_low():
                need(pool, M["x_high"], t + 1)
                nc.gpsimd.tensor_tensor(xs[:, q, LOW, :], xT3[:, q, :], xs[:, q, HIGH, :], ALU.subtract).then_inc(M["x_low"], 1)

            def u_low():
                need(pool, M["u_high"], t + 1)
                nc.gpsimd.tensor_tensor(us[:, LOW, :], uT[:], us[:, HIGH, :], ALU.subtract).then_inc(M["u_low"], 1)

            def output_bias():
                need(pool, M["vs"], t + 1)
                need(pool, M["added"], t)
                nc.gpsimd.tensor_tensor(gated_bias[:], bc(f_bias[:], GROUP), inner(vs[:, q, :], 128), ALU.mult).then_inc(M["bias"], 1)
                need(pool, M["bias"], t + 1)
                x3 = X[:, bass.ds(GROUP * t, GROUP), :]
                nc.gpsimd.tensor_tensor(x3, x3, gated_bias[:], ALU.add).then_inc(M["added"], 1)

            if route:
                x_low()
            if norm:
                roots()
            if route:
                u_low()
                output_bias()

        def f_peeled(tick, t):
            tick(t // 2, t % 2, *(0 <= t + k < GROUPS for k in (1, 0, -1)))

        def f_loop(engine, tick):
            with engine.Fori(1, GROUPS // 2 - 1, 1) as m:
                tick(m, 0, True, True, True)
                tick(m, 1, True, True, True)

        def f_stores(sp):
            for q in range(2):
                sp.sem_inc(s_out[q], 16)
            with sp.Fori(0, GROUPS // 2, 1) as m:
                for q in range(2):
                    g = 2 * m + q
                    sp.wait_ge(M["out"], g + 1)
                    sp.dma_start(out_d[:, bass.ds(GROUP * g, GROUP), :], y3[:, q, :, :]).then_inc(s_out[q], 16)
            for q in range(2):
                sp.wait_ge(s_out[q], 16 * (GROUPS // 2 + 1))

        blk = stack.enter_context(nc.Block())

        @blk.sync
        def _(sp):
            setup_sync(sp)
            x_loads(sp)
            f_stores(sp)

        @blk.gpsimd
        def _(pool):
            gsa = lambda *a: gsa_pool(pool, *a)
            cross = lambda *a: x_pool(pool, *a)
            experts = lambda *a: f_pool(pool, *a)
            setup_identity(pool)
            gsa_rstd(pool, 0)
            setup_slot_masks(pool)
            gsa_peeled(gsa, 0)
            setup_constants(pool)
            for t in range(1, 6):
                gsa_peeled(gsa, t)
            gsa_loop(pool, gsa)
            for t in range(PAIRS - 2, PAIRS + 1):
                gsa_peeled(gsa, t)
            pool.wait_ge(G["xn"], PAIRS)
            x_peeled(cross, -3)
            gsa_peeled(gsa, PAIRS + 1)
            pool.wait_ge(s_xw, XW)
            pool.wait_ge(s_wcopy, 6)
            pool.wait_ge(s_dconst, 2)
            x_peeled(cross, -2)
            gsa_peeled(gsa, PAIRS + 2)
            x_peeled(cross, -1)
            gsa_peeled(gsa, PAIRS + 3)
            for n in range(0, 2):
                x_peeled(cross, n)
            x_loop(pool, cross)
            for n in range(B - 4, B - 2):
                x_peeled(cross, n)
            pool.wait_ge(C["xn"], B)
            f_peeled(experts, -1)
            for n in range(B - 2, B):
                x_peeled(cross, n)
            f_peeled(experts, 0)
            x_peeled(cross, B)
            f_peeled(experts, 1)
            f_loop(pool, experts)
            for t in range(GROUPS - 2, GROUPS + 1):
                f_peeled(experts, t)

        @blk.scalar
        def _(act):
            gsa = lambda *a: gsa_scalar(act, *a)
            cross = lambda *a: x_scalar(act, *a)
            experts = lambda *a: f_scalar(act, *a)
            nc.scalar.preload_act_table_set("natural_log_exp_and_others")
            gsa_peeled(gsa, 0)
            setup_scalar_0(act)
            gsa_peeled(gsa, 1)
            setup_scalar_1(act)
            act.wait_ge(s_const, 1)
            gsa_peeled(gsa, 2)
            setup_scalar_2(act)
            for t in range(3, 6):
                gsa_peeled(gsa, t)
            gsa_loop(act, gsa)
            for t in range(PAIRS - 2, PAIRS + 1):
                gsa_peeled(gsa, t)
            act.wait_ge(s_dconst, 2)
            act.wait_ge(s_xw, XW)
            x_peeled(cross, -3)
            gsa_peeled(gsa, PAIRS + 1)
            x_peeled(cross, -2)
            gsa_peeled(gsa, PAIRS + 2)
            x_peeled(cross, -1)
            gsa_peeled(gsa, PAIRS + 3)
            for n in range(0, 2):
                x_peeled(cross, n)
            x_loop(act, cross)
            for n in range(B - 4, B - 2):
                x_peeled(cross, n)
            act.wait_ge(s_fw, FW)
            act.wait_ge(G["x1"], PAIRS)
            f_peeled(experts, -1)
            for n in range(B - 2, B):
                x_peeled(cross, n)
            f_peeled(experts, 0)
            x_peeled(cross, B)
            f_peeled(experts, 1)
            f_loop(act, experts)
            for t in range(GROUPS - 2, GROUPS + 1):
                f_peeled(experts, t)

        @blk.vector
        def _(dve):
            gsa = lambda *a: gsa_vector(dve, *a)
            cross = lambda *a: x_vector(dve, *a)
            experts = lambda *a: f_vector(dve, *a)
            dve.wait_ge(s_x[0], 16)
            gsa_stats(dve, 0)
            gsa_normalise(dve, 0)
            gsa_peeled(gsa, 0)
            dve.wait_ge(s_masks, 1)
            gsa_peeled(gsa, 1)
            setup_vector(dve)
            gsa_peeled(gsa, 2)
            dve.wait_ge(s_x[1], 16)
            gsa_peeled(gsa, 3)
            dve.wait_ge(s_x[2], 16)
            dve.wait_ge(s_x[3], 16)
            for t in range(4, 6):
                gsa_peeled(gsa, t)
            gsa_loop(dve, gsa)
            for t in range(PAIRS - 2, PAIRS + 1):
                gsa_peeled(gsa, t)
            dve.wait_ge(G["xn"], PAIRS)
            dve.wait_ge(G["x1"], 2)
            x_peeled(cross, -3)
            gsa_peeled(gsa, PAIRS + 1)
            dve.wait_ge(s_km, 16)
            x_peeled(cross, -2)
            gsa_peeled(gsa, PAIRS + 2)
            x_peeled(cross, -1)
            gsa_peeled(gsa, PAIRS + 3)
            dve.wait_ge(G["x1"], PAIRS)
            for n in range(0, 2):
                x_peeled(cross, n)
            x_loop(dve, cross)
            for n in range(B - 4, B - 2):
                x_peeled(cross, n)
            dve.wait_ge(C["xn"], B)
            dve.wait_ge(C["x2"], 2 * GROUP)
            f_peeled(experts, -1)
            for n in range(B - 2, B):
                x_peeled(cross, n)
            f_peeled(experts, 0)
            x_peeled(cross, B)
            dve.wait_ge(C["x2"], B)
            f_peeled(experts, 1)
            f_loop(dve, experts)
            for t in range(GROUPS - 2, GROUPS + 1):
                f_peeled(experts, t)

        @blk.tensor
        def _(pe):
            gsa = lambda *a: gsa_tensor(pe, *a)
            cross = lambda *a: x_tensor(pe, *a)
            experts = lambda *a: f_tensor(pe, *a)
            pe.wait_ge(s_ident, 1)
            pe.wait_ge(s_gw, GW)
            gsa_peeled(gsa, 0)
            setup_tensor_0(pe)
            pe.wait_ge(s_masks, 1)
            gsa_peeled(gsa, 1)
            setup_tensor_1(pe)
            pe.wait_ge(s_wcopy, 5)
            pe.wait_ge(s_dconst, 5)
            gsa_peeled(gsa, 2)
            setup_tensor_2(pe)
            pe.wait_ge(s_wcopy, 6)
            for t in range(3, 6):
                gsa_peeled(gsa, t)
            gsa_loop(pe, gsa)
            for t in range(PAIRS - 2, PAIRS + 1):
                gsa_peeled(gsa, t)
            x_peeled(cross, -3)
            gsa_peeled(gsa, PAIRS + 1)
            pe.wait_ge(G["silu"], PAIRS)
            x_peeled(cross, -2)
            gsa_peeled(gsa, PAIRS + 2)
            pe.wait_ge(G["lgts"], PAIRS)
            pe.wait_ge(G["un"], PAIRS)
            x_peeled(cross, -1)
            gsa_peeled(gsa, PAIRS + 3)
            pe.wait_ge(G["x1"], PAIRS)
            for n in range(0, 2):
                x_peeled(cross, n)
            x_loop(pe, cross)
            for n in range(B - 4, B - 2):
                x_peeled(cross, n)
            f_peeled(experts, -1)
            for n in range(B - 2, B):
                x_peeled(cross, n)
            pe.wait_ge(C["tt"], 4 * B)
            f_peeled(experts, 0)
            x_peeled(cross, B)
            pe.wait_ge(C["x2"], B)
            f_peeled(experts, 1)
            f_loop(pe, experts)
            for t in range(GROUPS - 2, GROUPS + 1):
                f_peeled(experts, t)


_INS = ['x', 'ctx_1024', 'fside_Bx16xSxS2_0', 'fside_SxS2_0', 'mask_BxS2_bf0', 'L0_attn_Wq', 'L0_attn_Wk', 'L0_attn_Wv',
        'L0_attn_Wf', 'L0_attn_g_norm_w', 'L0_attn_Wo', 'L0_xattn_Wq', 'L0_xattn_bq', 'L0_xattn_Wk', 'L0_xattn_bk',
        'L0_xattn_Wv', 'L0_xattn_bv', 'L0_xattn_Wo', 'L0_xattn_bo', 'L0_ffn_wi', 'L0_ffn_bi', 'L0_ffn_wo', 'L0_ffn_bo',
        'L0_ffn_lora_A', 'L0_ffn_lora_B', 'L0_ffn_gate_w', 'L0_ffn_gate_b']


def kernel(**inputs):
    import numpy as _np
    import concourse.bacc as _bacc
    from concourse import mybir as _mybir
    from concourse.bass_utils import run_bass_kernel_spmd as _run

    nc = _bacc.Bacc("TRN2", target_bir_lowering=False, num_devices=1)
    arrays, args = {}, []
    for name in _INS:
        a = _np.ascontiguousarray(inputs[name])
        arrays[f"in_{name}_dram"] = a
        args.append(nc.dram_tensor(f"in_{name}_dram", a.shape, _mybir.dt.from_np(a.dtype), kind="ExternalInput").ap())
    out = nc.dram_tensor("out_dram", (B, T, D), _mybir.dt.float32, kind="ExternalOutput").ap()
    decoder(nc, *args, out)
    r = _run(nc, [arrays], core_ids=[0])
    return r.results[0]["out_dram"]
```
